# Optimizing a Trainium2 kernel written in Bass

```python
import numpy as np
import jax
import jax.numpy as jnp

def _softmax(x, axis=-1):
    return jax.nn.softmax(x, axis=axis)

def _gelu(x):
    return jax.nn.gelu(x, approximate=True)

def _silu(x):
    return jax.nn.silu(x)

def _sigmoid(x):
    return jax.nn.sigmoid(x)

def _layernorm(x, axis=-1, eps=1e-05):
    m = jnp.mean(x, axis=axis, keepdims=True)
    v = jnp.var(x, axis=axis, keepdims=True)
    return (x - m) / jnp.sqrt(v + eps)

def _scatter_add(tgt, idx, src, axis=0):
    return tgt.at[idx].add(src)

def _segment_sum(src, seg, n):
    return jax.ops.segment_sum(src, seg, n)
kernel_name = 'mk_flamingo_gated_d1_seqx_r8_91030b'

def setup_inputs(seed: int=0):
    np.random.seed(seed)
    _w = jnp.asarray

    def _rec_inputs():
        import jax
        import jax.numpy as jnp
        _rk = jax.random.key(seed)
        x = -0.0002928 + 1 * jax.random.normal(jax.random.fold_in(_rk, 1), (16, 256, 128), jnp.float32)
        _lenS = 256 - jax.random.randint(jax.random.fold_in(_rk, 7), (16,), 0, max(1, 256 // 4) + 1, jnp.int32)
        _lenS2 = 1601 - jax.random.randint(jax.random.fold_in(_rk, 8), (16,), 0, max(1, 1601 // 4) + 1, jnp.int32)
        _ctx_512P = jax.random.normal(jax.random.fold_in(_rk, 11), (16, 16, 64), jnp.float32)
        _ctx_512c = jax.random.dirichlet(jax.random.fold_in(_rk, 511), 0.3 * jnp.ones((16,), jnp.float32), (16, 1601))
        _ctx_512t = jnp.einsum('bsk,bkd->bsd', _ctx_512c, _ctx_512P)
        _ctx_512t = _ctx_512t * jax.lax.rsqrt(jnp.mean(jnp.square(_ctx_512t)) + 1e-12) * 0.953939
        ctx_512 = 0.00222621 + 0.99962 * (_ctx_512t + 0.3 * jax.random.normal(jax.random.fold_in(_rk, 611), (16, 1601, 64), jnp.float32))
        _g = jax.random.normal(jax.random.fold_in(_rk, 9001), (2, 1), jnp.float32)
        _g = jnp.sign(_g) * jnp.maximum(jnp.abs(_g), 1.0) + (_g == 0) * 1.0
        g_xattn = _g[0]
        g_ffn = _g[1]
        return (x, ctx_512, g_xattn, g_ffn)
    x, ctx_512, g_xattn, g_ffn = _rec_inputs()

    def _L0_xattn_setup():
        import jax, jax.numpy as jnp
        import numpy as np
        B, T, TC, C, CC, H = (2, 256, 64, 128, 64, 16)
        D = C // H

        def _heads(t):
            b, l, _ = t.shape
            return t.reshape(b, l, H, D).transpose(0, 2, 1, 3)
        key = jax.random.key(seed)
        ks = jax.random.split(key, 18)
        w = lambda k, i, o: jax.random.normal(k, (i, o), jnp.float32) / np.sqrt(i).astype(np.float32)
        return {'x': jax.random.normal(ks[0], (B, T, C), jnp.float32), 'cross_input': jax.random.normal(ks[1], (B, TC, CC), jnp.float32), 'Wk': w(ks[2], C, C), 'bk': jnp.zeros((C,), jnp.float32), 'Wq': w(ks[3], C, C), 'bq': jnp.zeros((C,), jnp.float32), 'Wv': w(ks[4], C, C), 'bv': jnp.zeros((C,), jnp.float32), 'Wck': w(ks[5], CC, C), 'bck': jnp.zeros((C,), jnp.float32), 'Wcq': w(ks[6], C, C), 'bcq': jnp.zeros((C,), jnp.float32), 'Wcv': w(ks[7], CC, C), 'bcv': jnp.zeros((C,), jnp.float32), 'Wp': w(ks[8], C, C), 'bp': jnp.zeros((C,), jnp.float32)}
    _L0_xattn_all = _L0_xattn_setup()
    _L0_xattn_in = {k: v for k, v in _L0_xattn_all.items() if k in ('Wk', 'bk', 'Wq', 'bq', 'Wv', 'bv', 'Wck', 'bck', 'Wcq', 'bcq', 'Wcv', 'bcv', 'Wp', 'bp')}
    del _L0_xattn_all

    def _L0_ffn_setup():
        import jax, jax.numpy as jnp
        import numpy as np
        EMB, HID, E, TOPK = (128, 512, 8, 2)
        key = jax.random.key(seed)
        ks = jax.random.split(key, 10)
        s = 0.02
        return {'x': jax.random.normal(ks[0], (4, 256, EMB), jnp.float32), 'rw1': s * jax.random.normal(ks[1], (EMB, HID), jnp.float32), 'rb1': jnp.zeros((HID,), jnp.float32), 'rw2': s * jax.random.normal(ks[2], (HID, E), jnp.float32), 'rb2': jnp.zeros((E,), jnp.float32), 'w1': s * jax.random.normal(ks[3], (E, EMB, HID), jnp.float32), 'b1': jnp.zeros((E, HID), jnp.float32), 'w2': s * jax.random.normal(ks[4], (E, HID, EMB), jnp.float32), 'b2': jnp.zeros((E, EMB), jnp.float32)}
    _L0_ffn_all = _L0_ffn_setup()
    _L0_ffn_in = {k: v for k, v in _L0_ffn_all.items() if k in ('rw1', 'rb1', 'rw2', 'rb2', 'w1', 'b1', 'w2', 'b2')}
    del _L0_ffn_all
    return {'x': x, 'ctx_512': ctx_512, 'g_xattn': g_xattn, 'g_ffn': g_ffn, 'L0_xattn_Wk': _L0_xattn_in['Wk'], 'L0_xattn_bk': _L0_xattn_in['bk'], 'L0_xattn_Wq': _L0_xattn_in['Wq'], 'L0_xattn_bq': _L0_xattn_in['bq'], 'L0_xattn_Wv': _L0_xattn_in['Wv'], 'L0_xattn_bv': _L0_xattn_in['bv'], 'L0_xattn_Wck': _L0_xattn_in['Wck'], 'L0_xattn_bck': _L0_xattn_in['bck'], 'L0_xattn_Wcq': _L0_xattn_in['Wcq'], 'L0_xattn_bcq': _L0_xattn_in['bcq'], 'L0_xattn_Wcv': _L0_xattn_in['Wcv'], 'L0_xattn_bcv': _L0_xattn_in['bcv'], 'L0_xattn_Wp': _L0_xattn_in['Wp'], 'L0_xattn_bp': _L0_xattn_in['bp'], 'L0_ffn_rw1': _L0_ffn_in['rw1'], 'L0_ffn_rb1': _L0_ffn_in['rb1'], 'L0_ffn_rw2': _L0_ffn_in['rw2'], 'L0_ffn_rb2': _L0_ffn_in['rb2'], 'L0_ffn_w1': _L0_ffn_in['w1'], 'L0_ffn_b1': _L0_ffn_in['b1'], 'L0_ffn_w2': _L0_ffn_in['w2'], 'L0_ffn_b2': _L0_ffn_in['b2']}

def reference(x, ctx_512, g_xattn, g_ffn, L0_xattn_Wk, L0_xattn_bk, L0_xattn_Wq, L0_xattn_bq, L0_xattn_Wv, L0_xattn_bv, L0_xattn_Wck, L0_xattn_bck, L0_xattn_Wcq, L0_xattn_bcq, L0_xattn_Wcv, L0_xattn_bcv, L0_xattn_Wp, L0_xattn_bp, L0_ffn_rw1, L0_ffn_rb1, L0_ffn_rw2, L0_ffn_rb2, L0_ffn_w1, L0_ffn_b1, L0_ffn_w2, L0_ffn_b2):
    import jax
    import jax.numpy as jnp

    def _L0_xattn_ref(x, cross_input, Wk, bk, Wq, bq, Wv, bv, Wck, bck, Wcq, bcq, Wcv, bcv, Wp, bp):
        import jax, jax.numpy as jnp
        import numpy as np
        B, T, TC, C, CC, H = (2, 256, 64, 128, 64, 16)
        D = C // H

        def _heads(t):
            b, l, _ = t.shape
            return t.reshape(b, l, H, D).transpose(0, 2, 1, 3)
        scale = np.float32(1.0 / np.sqrt(D))
        q = _heads(x @ Wq + bq)
        k = _heads(x @ Wk + bk)
        v = _heads(x @ Wv + bv)
        att = jnp.einsum('bhqd,bhkd->bhqk', q, k) * scale
        causal = jnp.tril(jnp.ones((T, T), bool))
        att = jnp.where(causal[None, None], att, -jnp.inf)
        y = jnp.einsum('bhqk,bhkd->bhqd', jax.nn.softmax(att, axis=-1), v)
        qc = _heads(x @ Wcq + bcq)
        kc = _heads(cross_input @ Wck + bck)
        vc = _heads(cross_input @ Wcv + bcv)
        attc = jnp.einsum('bhqd,bhkd->bhqk', qc, kc) * scale
        y = y + jnp.einsum('bhqk,bhkd->bhqd', jax.nn.softmax(attc, axis=-1), vc)
        y = y.transpose(0, 2, 1, 3).reshape(x.shape[0], T, C)
        return y @ Wp + bp

    def _L0_ffn_ref(x, rw1, rb1, rw2, rb2, w1, b1, w2, b2):
        import jax, jax.numpy as jnp
        import numpy as np
        EMB, HID, E, TOPK = (128, 512, 8, 2)
        B, S, D = x.shape
        logits = jax.nn.silu(jnp.einsum('bsd,dh->bsh', x, rw1) + rb1)
        logits = jnp.einsum('bsh,he->bse', logits, rw2) + rb2
        k_logits, k_index = jax.lax.top_k(logits, TOPK)
        k_prob = jax.nn.softmax(k_logits, axis=-1)
        xf = x.reshape(B * S, D)
        k_index_f = k_index.reshape(B * S, TOPK)
        k_prob_f = k_prob.reshape(B * S, TOPK)
        out = jnp.zeros_like(xf)
        for e in range(E):
            we = jnp.sum(jnp.where(k_index_f == e, k_prob_f, 0.0), axis=-1)
            h = jax.nn.silu(xf @ w1[e] + b1[e]) @ w2[e] + b2[e]
            out = out + we[:, None] * h
        return out.reshape(B, S, D)
    x = x + jnp.tanh(g_xattn[0]) * _L0_xattn_ref(_layernorm(x, axis=-1), ctx_512, L0_xattn_Wk, L0_xattn_bk, L0_xattn_Wq, L0_xattn_bq, L0_xattn_Wv, L0_xattn_bv, L0_xattn_Wck, L0_xattn_bck, L0_xattn_Wcq, L0_xattn_bcq, L0_xattn_Wcv, L0_xattn_bcv, L0_xattn_Wp, L0_xattn_bp)
    x = x + jnp.tanh(g_ffn[0]) * _L0_ffn_ref(_layernorm(x, axis=-1), L0_ffn_rw1, L0_ffn_rb1, L0_ffn_rw2, L0_ffn_rb2, L0_ffn_w1, L0_ffn_b1, L0_ffn_w2, L0_ffn_b2)
    return x

_drawn_inputs = setup_inputs


def setup_inputs(seed=0):
    import zlib

    import numpy as np

    out = dict(_drawn_inputs(seed))
    spreads = {'L0_xattn_bk': (0.0, 0.8),
     'L0_xattn_bq': (0.0, 0.531),
     'L0_xattn_bv': (0.0, 0.1),
     'L0_xattn_bck': (0.0, 0.8),
     'L0_xattn_bcq': (0.0, 0.457),
     'L0_xattn_bcv': (0.0, 0.1),
     'L0_xattn_bp': (0.0, 0.1),
     'L0_ffn_rb1': (0.0, 0.313),
     'L0_ffn_rb2': (0.0, 0.1),
     'L0_ffn_b1': (0.0, 0.533),
     'L0_ffn_b2': (0.0, 0.1)}
    factors = {}
    for name, (base, spread) in spreads.items():
        noise = np.random.default_rng([zlib.crc32(name.encode()), seed]).standard_normal(out[name].shape)
        drawn = base * np.exp(spread * noise) if base else spread * noise
        out[name] = jnp.asarray(drawn.astype(out[name].dtype))
    for name, factor in factors.items():
        out[name] = (out[name] * factor).astype(out[name].dtype)
    return out
```

```python
from contextlib import ExitStack

import concourse.bass as bass
from concourse import mybir
from concourse.alu_op_type import AluOpType as ALU

F32 = mybir.dt.float32
F32R = mybir.dt.float32r
BF16 = mybir.dt.bfloat16
U32 = mybir.dt.uint32
ACT = mybir.ActivationFunctionType
AX_X = mybir.AxisListType.X

P = 128
T = 256
C = 128
H = 16
D = C // H
HEAD_ROWS = 4 * D
HEADS_IN_TILE = 3
SHIFT = HEADS_IN_TILE * HEAD_ROWS
ROWS = SHIFT + 2
HALF = H // 2
TILES = 3
GROUP = 4
GROUPS = H // GROUP
VW = 2 * D
EPS = 1e-5
NEG = -1.0e37
DMA = 16
LEAD = 5


def join_stats(nc, dve, stats, joined, mean, var_eps, joined_1, joined_2, eps_done, n):
    nc.vector.tensor_tensor(joined[:, :, 0:2], stats[:, :, 1:3], stats[:, :, 4:6], ALU.add)
    nc.vector.tensor_tensor(joined[:, :, 2], stats[:, :, 1], stats[:, :, 4], ALU.subtract).then_inc(joined_1, 1)
    dve.wait_ge(joined_1, n + 1)
    nc.vector.tensor_scalar(mean[:, :], joined[:, :, 0], 0.5, None, ALU.mult)
    nc.vector.tensor_scalar(joined[:, :, 3], joined[:, :, 1], 1.0 / C, EPS, ALU.mult, ALU.add)
    nc.vector.scalar_tensor_tensor(joined[:, :, 4], joined[:, :, 2], 0.25, joined[:, :, 2], ALU.mult,
                                   ALU.mult).then_inc(joined_2, 1)
    dve.wait_ge(joined_2, n + 1)
    nc.vector.tensor_tensor(var_eps[:, :], joined[:, :, 3], joined[:, :, 4], ALU.add).then_inc(eps_done, 1)


def known(eng, count):
    if not isinstance(count, int):
        eng.lower_val(count)
    return count


def attention(nc, x, ctx_t, g_x, w, x1, scratch):
    B = x.shape[0]
    TC = ctx_t.shape[2]
    CK = ctx_t.shape[1]
    NCH = -(-TC // P)
    TAIL = TC - (NCH - 1) * P
    STEPS = NCH + 2
    BSTEPS = STEPS * GROUPS
    NFULL = TC // 512
    REST = TC - NFULL * 512
    REST_W = REST + REST % 2
    SCALE = float(D) ** -0.5
    BANKS = 3
    assert BSTEPS % BANKS == 0 and GROUP * REST_W <= 512

    UNITS = [("cross", qt, i, kc) for qt in range(2) for i in range(GROUP) for kc in range(NFULL)]
    UNITS += [("cross_rest", qt, 0, 0) for qt in range(2)]
    UNITS += [("self", qt, i, 0) for qt in range(2) for i in (0, 2)]
    NU = len(UNITS)
    assert NU % BANKS == 0

    def units_at(pos):
        return range(NU * pos // STEPS, NU * (pos + 1) // STEPS)

    def target(j):
        s, pos = divmod(j + LEAD, STEPS)
        ahead, g = divmod(1 + s, GROUPS)
        return ahead, g, pos

    def in_half(g, i):
        h8 = GROUP * (g % 2) + i
        return g // 2, h8, h8 // HEADS_IN_TILE, h8 % HEADS_IN_TILE

    qs, kself_s, kx_s, ys = scratch["q"], scratch["kself"], scratch["kx"], scratch["y"]
    Wq, Wk, Wv, Wcq, Wp = w["Wq"], w["Wk"], w["Wv"], w["Wcq"], w["Wp"]

    with ExitStack() as ctx:
        def sb(name, shape, dt=F32):
            return ctx.enter_context(nc.sbuf_tensor(name, shape, dt))

        def psum(name, shape):
            return ctx.enter_context(nc.psum_tensor(name, shape, F32))

        def sem(name):
            return ctx.enter_context(nc.semaphore(name))

        wq_sb, wk_sb, wv_sb, wcq_sb, wp_sb = (sb(f"{n}_sb", [P, C]) for n in ("wq", "wk", "wv", "wcq", "wp"))
        wck_sb, wcv_sb = sb("wck_sb", [CK, C]), sb("wcv_sb", [CK - 1, C])
        bias_sb = sb("bias_sb", [P, 3])
        v_bias, bp_row = sb("v_bias", [P, 2, C]), sb("bp_row", [P, C])
        gate_in, gate = sb("gate_in", [P, 1]), sb("gate", [P, 1])
        ident = sb("ident", [P, P])
        ident_b = sb("ident_b", [P, P], BF16)
        mask_q = sb("mask_q", [P, 2, T], BF16)
        mask_k = sb("mask_k", [P, 2, T], BF16)
        minus_half = sb("minus_half", [P, 2])

        kx = [sb(f"kx{i}", [ROWS, TILES, TC], F32R) for i in range(2)]
        kself = [sb(f"kself{i}", [ROWS, TILES, T], F32R) for i in range(2)]
        qx = [sb(f"qx{i}", [ROWS, HALF, T], F32R) for i in range(2)]
        qself = [sb(f"qself{i}", [ROWS, HALF, T], F32R) for i in range(2)]
        v_all = sb("v_all", [P, STEPS, C])
        v_half = [sb(f"v_half{i}", [P, STEPS, HALF, VW]) for i in range(2)]

        x_in, xn, x_res = sb("x_in", [P, 2, C]), sb("xn", [P, 2, C]), sb("x_res", [P, 2, C])
        xn_t = sb("xn_t", [P, T])
        stats, joined, mean = sb("stats", [P, 2, 6]), sb("joined", [P, 2, 6]), sb("mean", [P, 2])
        var_eps, rstd = sb("var_eps", [P, 2]), sb("rstd", [P, 2])
        ctx_in = sb("ctx_in", [CK, TC])
        parts = sb("parts", [P, 3, 2, T], F32R)
        ck_parts = sb("ck_parts", [P, 2, TC], F32R)
        max_x = sb("max_x", [P, GROUP, 2, NFULL + 1])
        max_s = sb("max_s", [P, GROUP, 2])
        neg_max = sb("neg_max", [P, 2, GROUP * 2])
        shift = sb("shift", [P, 2, 2 * GROUP * 2], F32R)
        shift_t = sb("shift_t", [4 * GROUP * 2, P], F32R)
        probs = sb("probs", [P, 3, GROUP * T])
        y_raw = sb("y_raw", [P, 2, 2, T])
        y_in = sb("y_in", [P, 2, 2, T])
        y_rec, y_nrm = sb("y_rec", [P, 2, T]), sb("y_nrm", [P, 2, T])
        y_sum = sb("y_sum", [P, T])
        att = sb("att", [P, 2, C])
        x_new = sb("x_new", [P, 2, C])

        ps_s = psum("ps_s", [P, BANKS, 2, T])
        ps_a = psum("ps_a", [P, BANKS, 512])
        ps_m = psum("ps_m", [P, 512])
        ps_y = psum("ps_y", [P, 2, T])

        consts_in = sem("consts_in")
        zeroed = sem("zeroed")
        ones_set = sem("ones_set")
        masks_zero = sem("masks_zero")
        masks_set = sem("masks_set")
        gate_set = sem("gate_set")
        x_loaded = sem("x_loaded")
        ctx_loaded = sem("ctx_loaded")
        stats_done = sem("stats_done")
        joined_1, joined_2 = sem("joined_1"), sem("joined_2")
        eps_done = sem("eps_done")
        rstd_done = sem("rstd_done")
        xn_done = sem("xn_done")
        xnt_ps = sem("xnt_ps")
        xnt_done = sem("xnt_done")
        qk_ps = sem("qk_ps")
        qk_hi = sem("qk_hi")
        qk_lo = sem("qk_lo")
        cq_ps = sem("cq_ps")
        cq_hi = sem("cq_hi")
        cq_lo = sem("cq_lo")
        ck_ps = sem("ck_ps")
        ck_hi = sem("ck_hi")
        ck_lo = sem("ck_lo")
        cv_ps = sem("cv_ps")
        cv_done = sem("cv_done")
        v_ps = sem("v_ps")
        v_done = sem("v_done")
        qk_stored = sem("qk_stored")
        kx_stored = sem("kx_stored")
        half_in = [sem("half0_in"), sem("half1_in")]
        vhalf_done = [sem("vhalf0_done"), sem("vhalf1_done")]
        unit_ready = sem("unit_ready")
        unit_reduced = sem("unit_reduced")
        neg_done = sem("neg_done")
        shift_hi = sem("shift_hi")
        shift_lo = sem("shift_lo")
        shift_ps = sem("shift_ps")
        shift_t_done = sem("shift_t_done")
        shift_in = sem("shift_in")
        scores_ready = sem("scores_ready")
        exp_done = sem("exp_done")
        pv_done = sem("pv_done")
        y_copied = sem("y_copied")
        y_stored = [sem("y_stored_even"), sem("y_stored_odd")]
        y_loaded = sem("y_loaded")
        rec_done = sem("rec_done")
        nrm_done = sem("nrm_done")
        ysum_done = sem("ysum_done")
        xres_loaded = sem("xres_loaded")
        out_ps = sem("out_ps")
        att_done = sem("att_done")
        x1_done = sem("x1_done")
        x1_stored = sem("x1_stored")

        HALF_DMAS = 3 + 2 + 2 * HEADS_IN_TILE
        NCK = -(-TC // 512)
        NCV = -(-NCH // 4)
        N_CONST = 12

        J_LN, J_XN, J_XT, J_QK, J_CQ, J_REC, J_OUT = 2, 3, 4, 6, 8, 8, 12
        J_CK = [14, 16, 18, 20][:NCK]
        J_CV = [22, 24, 27, 29][:NCV]
        J_V = 31
        J_SHIFT = [STEPS * g + 10 for g in range(GROUPS)]

        block = ctx.enter_context(nc.Block())

        @block.sync
        def _(sp):
            def load_x(c):
                sp.wait_ge(masks_zero, 1)
                if not (isinstance(c, int) and c == 0):
                    sp.wait_ge(xn_done, c)
                sp.dma_start(x_in[:, :, :], x[c, :, :].rearrange("(t p) c -> p t c", p=P)).then_inc(x_loaded, DMA)
                sp.wait_ge(masks_zero, 1)
                if not (isinstance(c, int) and c == 0):
                    sp.wait_ge(cv_ps, c * NCV)
                sp.dma_start(ctx_in[:, :], ctx_t[c, :, :]).then_inc(ctx_loaded, DMA)

            def store_q_parts(c):
                sp.wait_ge(masks_zero, 1)
                sp.wait_ge(qk_lo, c + 1)
                for a in range(2):
                    for b in range(2):
                        sp.dma_start(qs[c, 0, :, a, b, :, :], parts[:, 0, a, :].bitcast(F32)).then_inc(qk_stored, DMA)
                        sp.dma_start(kself_s[c, :, a, b, :, :], parts[:, 1, b, :].bitcast(F32)).then_inc(qk_stored, DMA)
                sp.wait_ge(masks_zero, 1)
                sp.wait_ge(cq_lo, c + 1)
                for a in range(2):
                    for b in range(2):
                        sp.dma_start(qs[c, 1, :, a, b, :, :], parts[:, 2, a, :].bitcast(F32)).then_inc(qk_stored, DMA)

            def store_k_parts(c):
                sp.wait_ge(masks_zero, 1)
                sp.wait_ge(ck_lo, (c + 1) * NCK)
                for a in range(2):
                    for b in range(2):
                        sp.dma_start(kx_s[c, :, a, b, :, :], ck_parts[:, b, :].bitcast(F32)).then_inc(kx_stored, DMA)

            def load_half(c, half):
                q_rows, k_rows = known(sp, (c + 1) * 12 * DMA), known(sp, (c + 1) * 4 * DMA)
                read = known(sp, 2 * (c - 1) * BSTEPS + (half + 1) * BSTEPS)
                sp.wait_ge(masks_zero, 1)
                sp.wait_ge(qk_stored, q_rows)
                sp.wait_ge(kx_stored, k_rows)
                if not (isinstance(c, int) and c == 0):
                    sp.wait_ge(scores_ready, read)
                h0 = half * HALF
                kxr = kx_s[c, h0:h0 + HALF].rearrange("h a b d n -> (h a b d) n")
                ksr = kself_s[c, h0:h0 + HALF].rearrange("h a b d n -> (h a b d) n")
                for g in range(TILES):
                    r0, r1 = g * SHIFT, min((g + 1) * SHIFT, HALF * HEAD_ROWS)
                    sp.dma_start(kx[half][0:r1 - r0, g, :].bitcast(F32), kxr[r0:r1, :]).then_inc(half_in[half], DMA)
                sp.dma_start(kself[half][0:SHIFT, 0:2, :].bitcast(F32),
                             ksr[0:2 * SHIFT, :].rearrange("(g r) n -> r g n", g=2)).then_inc(half_in[half], DMA)
                sp.dma_start(kself[half][0:HALF * HEAD_ROWS - 2 * SHIFT, 2, :].bitcast(F32),
                             ksr[2 * SHIFT:, :]).then_inc(half_in[half], DMA)
                for st, dst in enumerate((qself[half], qx[half])):
                    src = qs[c, st, h0:h0 + HALF].rearrange("h a b d n -> (a b d) h n")
                    for q in range(HEADS_IN_TILE):
                        sp.dma_start(dst[q * HEAD_ROWS:(q + 1) * HEAD_ROWS, q:HALF:HEADS_IN_TILE, :].bitcast(F32),
                                     src[:, q:HALF:HEADS_IN_TILE, :]).then_inc(half_in[half], DMA)

            def store_shift(s, g):
                sp.wait_ge(shift_t_done, s + 1)
                n = GROUP * 2
                for part in range(2):
                    for st, dst in enumerate((qx[g // 2], qself[g // 2])):
                        r = (part * 2 + st) * n
                        h0 = GROUP * (g % 2)
                        sp.dma_start(dst[SHIFT + part:SHIFT + part + 1, h0:h0 + GROUP, :].bitcast(F32),
                                     shift_t[r:r + n, :].bitcast(F32)).then_inc(shift_in, DMA)

            def store_y(b, g):
                copied = known(sp, GROUPS * b + g + 1)
                sp.wait_ge(masks_zero, 1)
                sp.wait_ge(y_copied, copied)
                for i in range(GROUP):
                    sp.dma_start(ys[b, :, GROUP * g + i, :, :].rearrange("s r q -> r s q"),
                                 y_raw[32 * i:32 * i + VW, g % 2, :, :]).then_inc(y_stored[g % 2], DMA)

            def load_y(b):
                stored = known(sp, (b + 1) * (GROUPS // 2) * GROUP * DMA)
                sp.wait_ge(masks_zero, 1)
                for even_odd in y_stored:
                    sp.wait_ge(even_odd, stored)
                for st in range(2):
                    for part in range(2):
                        sp.dma_start(y_in[:, st, part, :],
                                     ys[b, st, :, part * D:(part + 1) * D, :]
                                     ).then_inc(y_loaded, DMA)
                sp.dma_start(x_res[:, :, :], x[b, :, :].rearrange("(t p) c -> p t c", p=P)).then_inc(xres_loaded, DMA)

            def store_x1(b):
                sp.wait_ge(masks_zero, 1)
                sp.wait_ge(x1_done, b + 1)
                sp.dma_start(x1[b, :, :].rearrange("(t p) c -> p t c", p=P), x_new[:, :, :]).then_inc(x1_stored, DMA)

            def element(b, first, last):
                if not last:
                    load_x(b + 1)
                if not first:
                    load_half(b, 1)
                    store_y(b - 1, GROUPS - 1)
                    load_y(b - 1)
                if not last:
                    store_q_parts(b + 1)
                store_shift(GROUPS * b + 1, 1)
                if not first:
                    store_x1(b - 1)
                store_y(b, 0)
                if not last:
                    store_k_parts(b + 1)
                store_shift(GROUPS * b + 2, 2)
                store_y(b, 1)
                if not last:
                    load_half(b + 1, 0)
                store_shift(GROUPS * b + 3, 3)
                store_y(b, 2)
                if not last:
                    store_shift(GROUPS * b + 4, 0)

            load_x(0)
            for dst, src in ((wq_sb, Wq), (wk_sb, Wk), (wcq_sb, Wcq), (wv_sb, Wv), (wp_sb, Wp),
                             (wck_sb, w["Wck"]), (wcv_sb, w["Wcv"])):
                sp.dma_start(dst[:, :], src).then_inc(consts_in, DMA)
            sp.dma_start(bias_sb[:, :], w["qk_bias"]).then_inc(consts_in, DMA)
            for st, n in enumerate(("bcv", "bv")):
                sp.dma_start(v_bias[:, st, :], w[n].rearrange("(a n) -> a n", a=1).broadcast_to([P, C])).then_inc(consts_in, DMA)
            sp.dma_start(bp_row[:, :], w["bp"].rearrange("(a n) -> a n", a=1).broadcast_to([P, C])).then_inc(consts_in, DMA)
            sp.dma_start(gate_in[:, :], g_x.rearrange("(a n) -> a n", a=1).broadcast_to([P, 1])).then_inc(consts_in, DMA)
            store_q_parts(0)
            store_k_parts(0)
            sp.wait_ge(zeroed, 1)
            sp.wait_ge(ones_set, 1)
            load_half(0, 0)
            load_half(0, 1)
            store_shift(0, 0)
            element(0, True, False)
            with sp.Fori(1, B - 1) as b:
                element(b, False, False)
            element(B - 1, False, True)
            store_y(B - 1, GROUPS - 1)
            load_y(B - 1)
            store_x1(B - 1)
            sp.wait_ge(x1_stored, B * DMA)

        @block.tensor
        def _(pe):
            def scores(b, j, pair):
                g, t = divmod(j, STEPS)
                k = 2 * (BSTEPS * b + j) + pair
                if not (isinstance(k, int) and k < BANKS):
                    pe.wait_ge(exp_done, k - BANKS + 1)
                if t == 0 and pair == 0:
                    pe.wait_ge(shift_in, (GROUPS * b + g + 1) * 4 * DMA)
                out = ps_s[:, (2 * j + pair) % BANKS, :, :]
                own = t - NCH
                if own >= 0:
                    qs_ = slice(own * P, (own + 1) * P)
                    pe.matmul(out[:, :, qs_], ident_b[:, :], mask_k[:, own:own + 1, qs_].broadcast_to([P, 2, P]),
                              start=True, stop=False, skip_group_check=True)
                for i in (2 * pair, 2 * pair + 1):
                    half, h8, tile, _ = in_half(g, i)
                    if own < 0:
                        n = P if t < NCH - 1 else TAIL
                        mm = pe.matmul(out[0:n, i % 2, :], kx[half][:, tile, t * P:t * P + n],
                                       qx[half][:, h8, :], start=True, stop=True)
                    else:
                        mm = pe.matmul(out[:, i % 2, :], kself[half][:, tile, own * P:(own + 1) * P],
                                       qself[half][:, h8, :], start=False, stop=(i % 2 == 1), skip_group_check=True)
                mm.then_inc(scores_ready, 1)

            def unit(b, g, u):
                number = NU * (GROUPS * b + g) + u
                if not (isinstance(number, int) and number < BANKS):
                    pe.wait_ge(unit_reduced, number - BANKS + 1)
                kind, qt, i0, kc = UNITS[u]
                out = ps_a[:, u % BANKS, :]
                q = slice(qt * P, (qt + 1) * P)
                if kind == "cross":
                    half, h8, tile, _ = in_half(g, i0)
                    mm = pe.matmul(out, qx[half][0:SHIFT, h8, q], kx[half][0:SHIFT, tile, kc * 512:(kc + 1) * 512],
                                   start=True, stop=True)
                elif kind == "cross_rest":
                    for i in range(GROUP):
                        half, h8, tile, _ = in_half(g, i)
                        mm = pe.matmul(out[:, i * REST_W:(i + 1) * REST_W], qx[half][0:SHIFT, h8, q],
                                       kx[half][0:SHIFT, tile, TC - REST_W:TC], start=True, stop=True)
                else:
                    out = out.rearrange("p (i n) -> p i n", n=T)
                    pe.matmul(out[:, :, q], ident_b[:, :], mask_q[:, qt:qt + 1, q].broadcast_to([P, 2, P]),
                              start=True, stop=False, skip_group_check=True)
                    for i in (i0, i0 + 1):
                        half, h8, tile, _ = in_half(g, i)
                        mm = pe.matmul(out[:, i - i0, :], qself[half][0:SHIFT, h8, q],
                                       kself[half][0:SHIFT, tile, :], start=False, stop=(i == i0 + 1),
                                       skip_group_check=True)
                mm.then_inc(unit_ready, 1)

            def operands_here(b, g):
                if g % 2 == 0:
                    pe.wait_ge(half_in[g // 2], (b + 1) * HALF_DMAS * DMA)

            def pv(b, j):
                g, t = divmod(j, STEPS)
                pe.wait_ge(exp_done, 2 * (BSTEPS * b + j) + 2)
                if t == 0:
                    if not (isinstance(b, int) and GROUPS * b + g == 0):
                        pe.wait_ge(y_copied, GROUPS * b + g)
                    if g % 2 == 0:
                        pe.wait_ge(vhalf_done[g // 2], b + 1)
                for i in range(GROUP):
                    half, h8, _, _ = in_half(g, i)
                    if t < NCH:
                        n = P if t < NCH - 1 else TAIL
                        mm = pe.matmul(ps_y[32 * i:32 * i + VW, 0, :], v_half[half][0:n, t, h8, :],
                                       probs[0:n, j % 3, i * T:(i + 1) * T], start=(t == 0), stop=(t == NCH - 1))
                    elif t == NCH:
                        mm = pe.matmul(ps_y[32 * i:32 * i + VW, 1, :], v_half[half][:, t, h8, :],
                                       probs[:, j % 3, i * T:(i + 1) * T], start=True, stop=False)
                    else:
                        mm = pe.matmul(ps_y[32 * i:32 * i + VW, 1, P:T], v_half[half][:, t, h8, :],
                                       probs[:, j % 3, i * T + P:(i + 1) * T], start=False, stop=True)
                mm.then_inc(pv_done, 1)

            def shift_job(s):
                pe.wait_ge(shift_lo, s + 1)
                pe.transpose(ps_m[0:4 * GROUP * 2, 0:P], shift[:, :, :].rearrange("p a n -> p (a n)").bitcast(F32),
                             ident[:, :]).then_inc(shift_ps, 1)

            def xn_job(c):
                pe.wait_ge(xn_done, c + 1)
                if not (isinstance(c, int) and c == 0):
                    pe.wait_ge(shift_t_done, GROUPS * c - GROUPS + 1)
                for t in range(2):
                    mm = pe.transpose(ps_m[:, t * P:(t + 1) * P], xn[:, t, :], ident[:, :])
                mm.then_inc(xnt_ps, 1)

            def qk_job(c):
                pe.wait_ge(xnt_done, c + 1)
                pe.matmul(ps_m[:, 0:T], wq_sb[:, :], xn_t[:, :], start=True, stop=True)
                pe.matmul(ps_m[:, T:2 * T], wk_sb[:, :], xn_t[:, :], start=True, stop=True).then_inc(qk_ps, 1)

            def cq_job(c):
                pe.wait_ge(qk_lo, c + 1)
                pe.matmul(ps_m[:, 0:T], wcq_sb[:, :], xn_t[:, :], start=True, stop=True).then_inc(cq_ps, 1)

            def ck_job(c, n):
                if n > 0:
                    pe.wait_ge(ck_lo, c * NCK + n)
                else:
                    pe.wait_ge(cq_lo, c + 1)
                    pe.wait_ge(ctx_loaded, (c + 1) * DMA)
                k0, k1 = n * 512, min((n + 1) * 512, TC)
                pe.matmul(ps_m[:, 0:k1 - k0], wck_sb[:, :], ctx_in[:, k0:k1], start=True, stop=True).then_inc(ck_ps, 1)

            def cv_job(c, n):
                if n > 0:
                    pe.wait_ge(cv_done, c * NCV + n)
                else:
                    pe.wait_ge(ck_lo, (c + 1) * NCK)
                for ch in range(4 * n, min(4 * n + 4, NCH)):
                    k = P if ch < NCH - 1 else TAIL
                    mm = pe.matmul(ps_m[0:k, (ch - 4 * n) * C:(ch - 4 * n + 1) * C], ctx_in[0:CK - 1, ch * P:ch * P + k],
                                   wcv_sb[:, :], start=True, stop=True)
                mm.then_inc(cv_ps, 1)

            def v_job(c):
                pe.wait_ge(cv_done, (c + 1) * NCV)
                for t in range(2):
                    mm = pe.matmul(ps_m[:, t * C:(t + 1) * C], xn_t[:, t * P:(t + 1) * P], wv_sb[:, :],
                                   start=True, stop=True)
                mm.then_inc(v_ps, 1)

            def out_job(b):
                pe.wait_ge(ysum_done, b + 1)
                for t in range(2):
                    mm = pe.matmul(ps_m[:, t * C:(t + 1) * C], y_sum[:, t * P:(t + 1) * P], wp_sb[:, :],
                                   start=True, stop=True)
                mm.then_inc(out_ps, 1)

            def element(b, first, last):
                for j in range(BSTEPS):
                    ahead, g, pos = target(j)
                    mine = [] if last and ahead else list(units_at(pos))
                    for pair in range(2):
                        if j + 1 < BSTEPS:
                            scores(b, j + 1, pair)
                        elif not last:
                            scores(b + 1, 0, pair)
                        if mine and pos == 0 and pair == 0:
                            operands_here(b + ahead, g)
                        if mine:
                            unit(b + ahead, g, mine[pair])
                    if not last:
                        if j == J_XT:
                            xn_job(b + 1)
                        if j == J_QK:
                            qk_job(b + 1)
                        if j == J_CQ:
                            cq_job(b + 1)
                        if j in J_CK:
                            if j == J_CK[0] and not first:
                                pe.wait_ge(att_done, b)
                            if j in J_CK[:1]:
                                pe.wait_ge(shift_t_done, GROUPS * b + 2)
                            ck_job(b + 1, J_CK.index(j))
                        if j in J_CV:
                            if j == J_CV[2]:
                                pe.wait_ge(shift_t_done, GROUPS * b + 3)
                            cv_job(b + 1, J_CV.index(j))
                        if j == J_V:
                            v_job(b + 1)
                    if j == J_OUT and not first:
                        pe.wait_ge(shift_t_done, GROUPS * b + 2)
                        out_job(b - 1)
                    if j in J_SHIFT and not (last and j == J_SHIFT[-1]):
                        k = J_SHIFT.index(j)
                        if k == 0 and not last:
                            pe.wait_ge(cq_lo, b + 2)
                        if k == 0 and last:
                            pe.wait_ge(shift_t_done, GROUPS * b + 1)
                        if k == 1 and not last:
                            pe.wait_ge(cv_done, (b + 1) * NCV + 2)
                        if k == 1 and last:
                            pe.wait_ge(att_done, b)
                        if k == 2 and not last:
                            pe.wait_ge(v_done, b + 2)
                        if k == 2 and last or k == 3:
                            pe.wait_ge(shift_t_done, GROUPS * b + k + 1)
                        shift_job(GROUPS * b + 1 + k)
                    pv(b, j)

            pe.wait_ge(consts_in, N_CONST * DMA)
            pe.wait_ge(masks_set, 4)
            xn_job(0)
            qk_job(0)
            cq_job(0)
            for n in range(NCK):
                ck_job(0, n)
            for n in range(NCV):
                cv_job(0, n)
            v_job(0)
            pe.wait_ge(ones_set, 1)
            operands_here(0, 0)
            for u in range(NU):
                unit(0, 0, u)
            pe.wait_ge(v_done, 1)
            shift_job(0)
            for pos in range(LEAD):
                for u in units_at(pos):
                    unit(0, 1, u)
            scores(0, 0, 0)
            scores(0, 0, 1)
            element(0, True, False)
            with pe.Fori(1, B - 1) as b:
                element(b, False, False)
            element(B - 1, False, True)
            pe.wait_ge(shift_t_done, GROUPS * B)
            out_job(B - 1)

        @block.scalar
        def _(act):
            def exp(b, j):
                g, t = divmod(j, STEPS)
                if not (isinstance(b, int) and BSTEPS * b + j < 3):
                    act.wait_ge(pv_done, BSTEPS * b + j - 2)
                n = TAIL if t == NCH - 1 else P
                q0 = P if t == NCH + 1 else 0
                dst = probs[0:n, j % 3, :].rearrange("p (i q) -> p i q", q=T)
                for pair in range(2):
                    act.wait_ge(scores_ready, 2 * (BSTEPS * b + j) + pair + 1)
                    act.activation(dst[:, 2 * pair:2 * pair + 2, q0:T], ps_s[0:n, (2 * j + pair) % BANKS, :, q0:T],
                                   ACT.Exp, scale=SCALE).then_inc(exp_done, 1)

            def copy_y(b, g):
                act.wait_ge(pv_done, BSTEPS * b + (g + 1) * STEPS)
                if not (isinstance(b, int) and GROUPS * b + g < 2):
                    act.wait_ge(y_stored[g % 2], (GROUPS // 2 * b + g // 2) * GROUP * DMA)
                act.activation(y_raw[:, g % 2, :, :], ps_y[:, :, :], ACT.Copy).then_inc(y_copied, 1)

            def xnt(c):
                act.wait_ge(xnt_ps, c + 1)
                if not (isinstance(c, int) and c == 0):
                    act.wait_ge(v_ps, c)
                act.activation(xn_t[:, :], ps_m[:, 0:T], ACT.Copy).then_inc(xnt_done, 1)

            def qk(c):
                act.wait_ge(qk_ps, c + 1)
                if not (isinstance(c, int) and c == 0):
                    act.wait_ge(qk_stored, c * 12 * DMA)
                for i in range(2):
                    a = act.activation(parts[:, i, 0, :], ps_m[:, i * T:(i + 1) * T], ACT.Identity, bias=bias_sb[:, i:i + 1])
                a.then_inc(qk_hi, 1)

            def cq(c):
                act.wait_ge(cq_ps, c + 1)
                act.activation(parts[:, 2, 0, :], ps_m[:, 0:T], ACT.Identity, bias=bias_sb[:, 2:3]).then_inc(cq_hi, 1)

            def ck(c, n):
                act.wait_ge(ck_ps, c * NCK + n + 1)
                if n == 0 and not (isinstance(c, int) and c == 0):
                    act.wait_ge(kx_stored, c * 4 * DMA)
                k0, k1 = n * 512, min((n + 1) * 512, TC)
                act.activation(ck_parts[:, 0, k0:k1], ps_m[:, 0:k1 - k0], ACT.Copy).then_inc(ck_hi, 1)

            def cv(c, n):
                act.wait_ge(cv_ps, c * NCV + n + 1)
                if n == 0 and not (isinstance(c, int) and c == 0):
                    act.wait_ge(vhalf_done[1], c)
                full = min(4 * n + 4, NCH - 1) - 4 * n
                a = None
                if full > 0:
                    a = act.activation(v_all[:, 4 * n:4 * n + full, :],
                                       ps_m[:, 0:full * C].rearrange("p (a c) -> p a c", c=C), ACT.Copy)
                if 4 * n + 4 >= NCH:
                    a = act.activation(v_all[0:TAIL, NCH - 1, :], ps_m[0:TAIL, full * C:(full + 1) * C], ACT.Copy)
                a.then_inc(cv_done, 1)

            def shift_rows(s):
                act.wait_ge(shift_ps, s + 1)
                if not (isinstance(s, int) and s == 0):
                    act.wait_ge(shift_in, s * 4 * DMA)
                act.activation(shift_t[:, :], ps_m[0:4 * GROUP * 2, 0:P], ACT.Copy).then_inc(shift_t_done, 1)

            def element(b, first, last):
                for j in range(BSTEPS):
                    if j + 1 < BSTEPS:
                        exp(b, j + 1)
                    elif not last:
                        exp(b + 1, 0)
                    if j % STEPS == STEPS - 1:
                        copy_y(b, j // STEPS)
                    if not last:
                        if j == J_XT:
                            xnt(b + 1)
                        if j == J_QK:
                            qk(b + 1)
                        if j == J_CQ:
                            cq(b + 1)
                        if j in J_CK:
                            ck(b + 1, J_CK.index(j))
                        if j in J_CV:
                            cv(b + 1, J_CV.index(j))
                    if j in J_SHIFT and not (last and j == J_SHIFT[-1]):
                        shift_rows(GROUPS * b + 1 + J_SHIFT.index(j))

            act.wait_ge(consts_in, N_CONST * DMA)
            act.activation(gate[:, :], gate_in[:, :], ACT.Tanh).then_inc(gate_set, 1)
            xnt(0)
            qk(0)
            cq(0)
            for n in range(NCK):
                ck(0, n)
            act.wait_ge(zeroed, 1)
            for n in range(NCV):
                cv(0, n)
            shift_rows(0)
            exp(0, 0)
            element(0, True, False)
            with act.Fori(1, B - 1) as b:
                element(b, False, False)
            element(B - 1, False, True)

        @block.vector
        def _(dve):
            def reduce_unit(b, g, u):
                dve.wait_ge(unit_ready, NU * (GROUPS * b + g) + u + 1)
                kind, qt, i0, kc = UNITS[u]
                src = ps_a[:, u % BANKS, :]
                if kind == "cross":
                    out = max_x[:, i0, qt, kc:kc + 1]
                elif kind == "cross_rest":
                    out, src = max_x[:, :, qt, NFULL], src[:, 0:GROUP * REST_W].rearrange("p (i n) -> p i n", n=REST_W)
                else:
                    out, src = max_s[:, i0:i0 + 2, qt], src.rearrange("p (i n) -> p i n", n=T)[:, :, 0:(qt + 1) * P]
                nc.vector.tensor_reduce(out, src, AX_X, ALU.max).then_inc(unit_reduced, 1)

            def shift_parts(b, g):
                s = GROUPS * b + g
                dve.wait_ge(unit_reduced, NU * (s + 1))
                if not (isinstance(s, int) and s == 0):
                    dve.wait_ge(shift_ps, s)
                nc.vector.tensor_reduce(neg_max[:, 0, :], max_x[:, :, :, :].rearrange("p i t n -> p (i t) n"),
                                        AX_X, ALU.max, negate=True)
                nc.vector.tensor_scalar(neg_max[:, 1, :], max_s[:, :, :].rearrange("p i t -> p (i t)"), -1.0, None,
                                        ALU.mult).then_inc(neg_done, 1)
                dve.wait_ge(neg_done, s + 1)
                flat = neg_max[:, :, :].rearrange("p a n -> p (a n)")
                nc.vector.tensor_copy(shift[:, 0, :], flat).then_inc(shift_hi, 1)
                dve.wait_ge(shift_hi, s + 1)
                nc.vector.tensor_tensor(shift[:, 1, :], flat, shift[:, 0, :].bitcast(F32), ALU.subtract).then_inc(shift_lo, 1)

            def ln_stats(c):
                dve.wait_ge(x_loaded, (c + 1) * DMA)
                for t in range(2):
                    a = nc.vector.bn_stats(stats[:, t, :], x_in[:, t, :])
                a.then_inc(stats_done, 1)
                dve.wait_ge(stats_done, c + 1)
                join_stats(nc, dve, stats, joined, mean, var_eps, joined_1, joined_2, eps_done, c)

            def ln_apply(c):
                dve.wait_ge(rstd_done, c + 1)
                for t in range(2):
                    a = nc.vector.tensor_scalar(xn[:, t, :], x_in[:, t, :], mean[:, t:t + 1], rstd[:, t:t + 1],
                                                ALU.subtract, ALU.mult)
                a.then_inc(xn_done, 1)

            def lo_part(out_lo, hi, src, bias):
                return nc.vector.scalar_tensor_tensor(out_lo, src, bias, hi.bitcast(F32), ALU.add, ALU.subtract)

            def qk(c):
                dve.wait_ge(qk_hi, c + 1)
                for i in range(2):
                    a = lo_part(parts[:, i, 1, :], parts[:, i, 0, :], ps_m[:, i * T:(i + 1) * T], bias_sb[:, i:i + 1])
                a.then_inc(qk_lo, 1)

            def cq(c):
                dve.wait_ge(cq_hi, c + 1)
                lo_part(parts[:, 2, 1, :], parts[:, 2, 0, :], ps_m[:, 0:T], bias_sb[:, 2:3]).then_inc(cq_lo, 1)

            def ck(c, n):
                dve.wait_ge(ck_hi, c * NCK + n + 1)
                k0, k1 = n * 512, min((n + 1) * 512, TC)
                nc.vector.tensor_tensor(ck_parts[:, 1, k0:k1], ps_m[:, 0:k1 - k0], ck_parts[:, 0, k0:k1].bitcast(F32),
                                        ALU.subtract).then_inc(ck_lo, 1)

            def v(c):
                dve.wait_ge(v_ps, c + 1)
                if not (isinstance(c, int) and c == 0):
                    dve.wait_ge(vhalf_done[1], c)
                nc.vector.tensor_copy(v_all[:, NCH:NCH + 2, :],
                                      ps_m[:, 0:2 * C].rearrange("p (a c) -> p a c", c=C)).then_inc(v_done, 1)

            def reciprocals(b):
                dve.wait_ge(y_loaded, (b + 1) * 4 * DMA)
                if not (isinstance(b, int) and b == 0):
                    dve.wait_ge(nrm_done, b)
                nc.vector.reciprocal(y_rec[:, :, :], y_in[:, :, 1, :]).then_inc(rec_done, 1)

            def residual(b):
                dve.wait_ge(out_ps, b + 1)
                dve.wait_ge(xres_loaded, (b + 1) * DMA)
                nc.vector.tensor_tensor(att[:, :, :], ps_m[:, 0:2 * C].rearrange("p (a c) -> p a c", c=C),
                                        bp_row[:, :].rearrange("p (a c) -> p a c", a=1).broadcast_to([P, 2, C]),
                                        ALU.add).then_inc(att_done, 1)
                dve.wait_ge(att_done, b + 1)
                if not (isinstance(b, int) and b == 0):
                    dve.wait_ge(x1_stored, b * DMA)
                nc.vector.scalar_tensor_tensor(x_new[:, :, :], att[:, :, :], gate[:, 0:1], x_res[:, :, :],
                                               ALU.mult, ALU.add).then_inc(x1_done, 1)

            def element(b, first, last):
                for j in range(BSTEPS):
                    ahead, g, pos = target(j)
                    if not (last and ahead):
                        for u in units_at(pos):
                            reduce_unit(b + ahead, g, u)
                        if pos == STEPS - 1:
                            shift_parts(b + ahead, g)
                    if not last:
                        if j == J_LN:
                            ln_stats(b + 1)
                        if j == J_XN:
                            ln_apply(b + 1)
                        if j == J_QK + 1:
                            qk(b + 1)
                        if j == J_CQ + 1:
                            cq(b + 1)
                        if j - 1 in J_CK:
                            ck(b + 1, J_CK.index(j - 1))
                        if j == J_V + 1:
                            v(b + 1)
                    if not first:
                        if j == J_REC:
                            reciprocals(b - 1)
                        if j == J_OUT + 1:
                            residual(b - 1)

            ln_stats(0)
            ln_apply(0)
            nc.vector.memset(ps_y[:, :, :], 0.0)
            nc.vector.memset(v_all[64:P, NCH - 1, :], 0.0)
            for i in range(2):
                nc.vector.memset(kx[i][64:ROWS, TILES - 1, :].bitcast(F32), 0.0)
                nc.vector.memset(kself[i][64:ROWS, TILES - 1, :].bitcast(F32), 0.0)
                nc.vector.memset(qx[i][:, :, :].bitcast(F32), 0.0)
                a = nc.vector.memset(qself[i][:, :, :].bitcast(F32), 0.0)
            a.then_inc(zeroed, 1)
            dve.wait_ge(zeroed, 1)
            for i in range(2):
                nc.vector.memset(kx[i][SHIFT:ROWS, :, :].bitcast(F32), 1.0)
                a = nc.vector.memset(kself[i][SHIFT:ROWS, :, :].bitcast(F32), 1.0)
            a.then_inc(ones_set, 1)
            dve.wait_ge(consts_in, N_CONST * DMA)
            qk(0)
            cq(0)
            for n in range(NCK):
                ck(0, n)
            v(0)
            for u in range(NU):
                reduce_unit(0, 0, u)
            shift_parts(0, 0)
            for pos in range(LEAD):
                for u in units_at(pos):
                    reduce_unit(0, 1, u)
            dve.wait_ge(gate_set, 1)
            element(0, True, False)
            with dve.Fori(1, B - 1) as b:
                element(b, False, False)
            element(B - 1, False, True)
            reciprocals(B - 1)
            residual(B - 1)

        @block.gpsimd
        def _(pool):
            def fill_v_half(b, half):
                pool.wait_ge(cv_done, (b + 1) * NCV)
                pool.wait_ge(v_done, b + 1)
                if not (isinstance(b, int) and b == 0):
                    pool.wait_ge(pv_done, (b - 1) * BSTEPS + (half + 1) * (BSTEPS // 2))
                for st, (n0, n1) in enumerate(((0, NCH), (NCH, NCH + 2))):
                    src = v_all[:, n0:n1, half * HALF * D:(half + 1) * HALF * D].rearrange("p n (h d) -> p n h d", d=D)
                    bias = v_bias[:, st:st + 1, half * HALF * D:(half + 1) * HALF * D].rearrange("p n (h d) -> p n h d", d=D)
                    a = nc.gpsimd.tensor_tensor(v_half[half][:, n0:n1, :, 0:D], src,
                                                bias.broadcast_to([P, n1 - n0, HALF, D]), ALU.add)
                a.then_inc(vhalf_done[half], 1)

            def rstd_of(c):
                pool.wait_ge(eps_done, c + 1)
                nc.gpsimd.tensor_tensor(rstd[:, :], var_eps[:, :], minus_half[:, :], ALU.pow).then_inc(rstd_done, 1)

            def normalise(b):
                pool.wait_ge(rec_done, b + 1)
                nc.gpsimd.tensor_tensor(y_nrm[:, :, :], y_in[:, :, 0, :], y_rec[:, :, :], ALU.mult).then_inc(nrm_done, 1)
                pool.wait_ge(nrm_done, b + 1)
                if not (isinstance(b, int) and b == 0):
                    pool.wait_ge(out_ps, b)
                nc.gpsimd.tensor_tensor(y_sum[:, :], y_nrm[:, 0, :], y_nrm[:, 1, :], ALU.add).then_inc(ysum_done, 1)

            def element(b, first, last):
                if not first:
                    fill_v_half(b, 1)
                if not last:
                    rstd_of(b + 1)
                if not first:
                    normalise(b - 1)
                if not last:
                    fill_v_half(b + 1, 0)

            nc.gpsimd.memset(minus_half[:, :], -0.5).then_inc(masks_zero, 1)
            pool.wait_ge(masks_zero, 1)
            rstd_of(0)
            for m in (ident, ident_b):
                nc.gpsimd.memset(m[:, :], 0.0).then_inc(masks_zero, 1)
            for m in (mask_q, mask_k):
                nc.gpsimd.memset(m[:, :, :], 0.0).then_inc(masks_zero, 1)
            pool.wait_ge(masks_zero, 5)
            for m in (ident, ident_b):
                nc.gpsimd.affine_select(out=m[:, :], in_=m[:, :], compare_op=ALU.not_equal, fill=1.0, base=0,
                                        pattern=[[-1, P]], channel_multiplier=1).then_inc(masks_set, 1)
            nc.gpsimd.affine_select(out=mask_q[:, :, :], in_=mask_q[:, :, :], compare_op=ALU.is_ge, fill=NEG, base=0,
                                    pattern=[[P, 2], [-1, T]], channel_multiplier=1).then_inc(masks_set, 1)
            nc.gpsimd.affine_select(out=mask_k[:, :, :], in_=mask_k[:, :, :], compare_op=ALU.is_ge, fill=NEG, base=0,
                                    pattern=[[-P, 2], [1, T]], channel_multiplier=-1).then_inc(masks_set, 1)
            for i in range(2):
                nc.gpsimd.memset(v_half[i][:, :, :, D:VW], 1.0)
            pool.wait_ge(zeroed, 1)
            pool.wait_ge(consts_in, N_CONST * DMA)
            fill_v_half(0, 0)
            fill_v_half(0, 1)
            element(0, True, False)
            with pool.Fori(1, B - 1) as b:
                element(b, False, False)
            element(B - 1, False, True)
            normalise(B - 1)


def experts(nc, x1, g_f, w, out):
    R = x1.shape[0]
    E, _, HID = w["w1"].shape
    TR = 512
    NT = R // TR
    SUB = TR // P
    M = HID // P
    NE = E + 1

    with ExitStack() as ctx:
        def sb(name, shape, dt=F32):
            return ctx.enter_context(nc.sbuf_tensor(name, shape, dt))

        def psum(name, shape):
            return ctx.enter_context(nc.psum_tensor(name, shape, F32))

        def sem(name):
            return ctx.enter_context(nc.semaphore(name))

        up_w = sb("up_w", [P, NE, HID])
        up_b = sb("up_b", [P, NE, M])
        down_w = sb("down_w", [P, E, M, C])
        rw2_sb = sb("rw2_sb", [P, M, E])
        rb2_row = sb("rb2_row", [P, E])
        b2_sb = sb("b2_sb", [E, C])
        gate_in, gate = sb("fgate_in", [P, 1]), sb("fgate", [P, 1])
        ident = sb("fident", [P, P])
        expert_no = sb("expert_no", [P, E])
        minus_half = sb("fminus_half", [P, SUB])

        x_in = sb("fx_in", [P, 2, SUB, C])
        xn = sb("fxn", [P, SUB, C])
        xn_t = sb("fxn_t", [P, 2, TR])
        stats, joined, mean = sb("fstats", [P, SUB, 6]), sb("fjoined", [P, SUB, 6]), sb("fmean", [P, SUB])
        var_eps, rstd = sb("fvar_eps", [P, SUB]), sb("frstd", [P, SUB])
        hid = sb("hid", [P, 2, M, TR])
        logits = sb("logits", [P, SUB, E])
        best = sb("best", [P, SUB, 8])
        best_at = sb("best_at", [P, SUB, 8], U32)
        best_no = sb("best_no", [P, SUB, 2])
        diff = sb("diff", [P, SUB])
        half_tanh = sb("half_tanh", [P, SUB])
        prob = sb("prob", [P, 2, SUB])
        pick = sb("pick", [P, 2, SUB, E])
        gates = sb("gates", [P, SUB, E])
        gates_t = sb("gates_t", [E, SUB, P])
        acc = sb("acc", [P, SUB, C])
        y = sb("fy", [P, 2, SUB, C])

        ps_h = psum("ps_h", [P, M, TR])
        ps_o = psum("ps_o", [P, 2, SUB, C])
        ps_t = psum("ps_t", [P, TR])
        ps_r = psum("ps_r", [P, SUB, C])

        w_in = sem("w_in")
        small_set = sem("small_set")
        ident_set = sem("fident_set")
        gate_set = sem("fgate_set")
        x_loaded = [sem("fx_loaded_even"), sem("fx_loaded_odd")]
        stats_done, eps_done = sem("fstats_done"), sem("feps_done")
        joined_1, joined_2 = sem("fjoined_1"), sem("fjoined_2")
        rstd_done, xn_done = sem("frstd_done"), sem("fxn_done")
        xnt_ps, xnt_done = sem("fxnt_ps"), sem("fxnt_done")
        up_ready = sem("up_ready")
        silu_done = sem("silu_done")
        logits_ps, logits_done = sem("logits_ps"), sem("logits_done")
        best_done, at_done, diff_done = sem("best_done"), sem("at_done"), sem("diff_done")
        tanh_done, prob_done, pick_done = sem("tanh_done"), sem("prob_done"), sem("pick_done")
        weigh_done, gates_done = sem("weigh_done"), sem("gates_done")
        gates_ps, gates_t_done = sem("gates_ps"), sem("gates_t_done")
        down_ready, added = sem("down_ready"), sem("added")
        b2_ready, b2_added = sem("b2_ready"), sem("b2_added")
        y_done = sem("fy_done")
        y_stored = [sem("fy_stored_even"), sem("fy_stored_odd")]

        N_W = 8
        block = ctx.enter_context(nc.Block())

        @block.sync
        def _(sp):
            def load(r, slot):
                sp.dma_start(x_in[:, slot, :, :], x1[bass.ds(r * TR, TR), :].rearrange("(t p) c -> p t c", p=P)
                             ).then_inc(x_loaded[slot], DMA)

            def store(r, slot):
                sp.wait_ge(w_in, N_W * DMA)
                sp.wait_ge(y_done, r + 1)
                sp.dma_start(out[bass.ds(r * TR, TR), :].rearrange("(t p) c -> p t c", p=P), y[:, slot, :, :]
                             ).then_inc(y_stored[slot], DMA)

            load(0, 0)
            load(1, 1)
            sp.dma_start(up_w[:, 0, :], w["rw1"]).then_inc(w_in, DMA)
            sp.dma_start(up_w[:, 1:NE, :], w["w1"].rearrange("e c n -> c e n")).then_inc(w_in, DMA)
            sp.dma_start(up_b[:, :, :], w["up_b"]).then_inc(w_in, DMA)
            sp.dma_start(down_w[:, :, :, :], w["w2"].rearrange("e (m p) c -> p (e m) c", p=P)).then_inc(w_in, DMA)
            sp.dma_start(rw2_sb[:, :, :], w["rw2"].rearrange("(m p) e -> p m e", p=P)).then_inc(w_in, DMA)
            sp.dma_start(rb2_row[:, :], w["rb2"].rearrange("(a n) -> a n", a=1).broadcast_to([P, E])).then_inc(w_in, DMA)
            sp.dma_start(b2_sb[:, :], w["b2"]).then_inc(w_in, DMA)
            sp.dma_start(gate_in[:, :], g_f.rearrange("(a n) -> a n", a=1).broadcast_to([P, 1])).then_inc(w_in, DMA)
            with sp.Fori(0, NT // 2 - 1) as i:
                for slot in range(2):
                    r = 2 * i + slot
                    store(r, slot)
                    load(r + 2, slot)
            for r in (NT - 2, NT - 1):
                store(r, r % 2)
            for even_odd in y_stored:
                sp.wait_ge(even_odd, NT // 2 * DMA)

        @block.tensor
        def _(pe):
            def transpose_x(r, slot):
                pe.wait_ge(xn_done, r + 1)
                if not (isinstance(r, int) and r == 0):
                    pe.wait_ge(gates_t_done, r)
                for t in range(SUB):
                    mm = pe.transpose(ps_t[:, t * P:(t + 1) * P], xn[:, t, :], ident[:, :])
                mm.then_inc(xnt_ps, 1)

            def up(r, slot, e):
                for m in range(M):
                    n = (NE * r + e) * M + m
                    if not (isinstance(n, int) and n < M):
                        pe.wait_ge(silu_done, n - M + 1)
                    pe.matmul(ps_h[:, m, :], up_w[:, e, m * P:(m + 1) * P], xn_t[:, slot, :],
                              start=True, stop=True).then_inc(up_ready, 1)

            def hidden_slot(slot, e):
                return (slot * NE + e) % 2

            def router_down(r, slot):
                pe.wait_ge(silu_done, (NE * r + 1) * M)
                if not (isinstance(r, int) and r == 0):
                    pe.wait_ge(b2_added, r)
                for t in range(SUB):
                    for m in range(M):
                        mm = pe.matmul(ps_r[:, 0, t * E:(t + 1) * E], hid[:, hidden_slot(slot, 0), m, t * P:(t + 1) * P],
                                       rw2_sb[:, m, :], start=(m == 0), stop=(m == M - 1))
                mm.then_inc(logits_ps, 1)

            def down(r, slot, e):
                pe.wait_ge(silu_done, (NE * r + e + 1) * M)
                n = E * r + e - 1
                if not (isinstance(n, int) and n < 2):
                    pe.wait_ge(added, n - 1)
                for t in range(SUB):
                    for m in range(M):
                        mm = pe.matmul(ps_o[:, (e - 1) % 2, t, :], hid[:, hidden_slot(slot, e), m, t * P:(t + 1) * P],
                                       down_w[:, e - 1, m, :], start=(m == 0), stop=(m == M - 1))
                mm.then_inc(down_ready, 1)

            def transpose_gates(r):
                pe.wait_ge(gates_done, r + 1)
                for t in range(SUB):
                    mm = pe.transpose(ps_t[0:E, t * P:(t + 1) * P], gates[:, t, :], ident[:, :])
                mm.then_inc(gates_ps, 1)

            def bias_down(r):
                pe.wait_ge(gates_t_done, r + 1)
                for t in range(SUB):
                    mm = pe.matmul(ps_r[:, t, :], gates_t[:, t, :], b2_sb[:, :], start=True, stop=True)
                mm.then_inc(b2_ready, 1)

            def tile(r, slot, last):
                pe.wait_ge(xnt_done, r + 1)
                for e in range(NE):
                    up(r, slot, e)
                    if e == 1:
                        router_down(r, slot)
                    if e > 1:
                        down(r, slot, e - 1)
                    if e == 3:
                        transpose_gates(r)
                    if e == 4:
                        bias_down(r)
                    if e == 6 and not last:
                        transpose_x(r + 1, 1 - slot)
                down(r, slot, NE - 1)

            pe.wait_ge(w_in, N_W * DMA)
            pe.wait_ge(ident_set, 1)
            transpose_x(0, 0)
            tile(0, 0, False)
            tile(1, 1, False)
            with pe.Fori(1, NT // 2 - 1) as i:
                for slot in range(2):
                    tile(2 * i + slot, slot, False)
            tile(NT - 2, 0, False)
            tile(NT - 1, 1, True)

        @block.scalar
        def _(act):
            def copy_xt(r, slot):
                act.wait_ge(xnt_ps, r + 1)
                if not (isinstance(r, int) and r < 2):
                    act.wait_ge(up_ready, NE * M * (r - 1))
                act.activation(xn_t[:, slot, :], ps_t[:, :], ACT.Copy).then_inc(xnt_done, 1)

            def silu(r, slot, e):
                for m in range(M):
                    n = (NE * r + e) * M + m
                    act.wait_ge(up_ready, n + 1)
                    if m == 0:
                        k = NE * r + e
                        if not (isinstance(k, int) and k < 2):
                            if e == 0:
                                act.wait_ge(down_ready, E * r - 1)
                            elif e == 1:
                                act.wait_ge(down_ready, E * r)
                            elif e == 2:
                                act.wait_ge(logits_ps, r + 1)
                            else:
                                act.wait_ge(down_ready, E * r + e - 2)
                    act.activation(hid[:, (slot * NE + e) % 2, m, :], ps_h[:, m, :], ACT.Silu,
                                   bias=up_b[:, e, m:m + 1]).then_inc(silu_done, 1)

            def tile(r, slot, last):
                for e in range(NE):
                    silu(r, slot, e)
                    if e == 2:
                        act.wait_ge(diff_done, r + 1)
                        act.activation(half_tanh[:, :], diff[:, :], ACT.Tanh, scale=0.5).then_inc(tanh_done, 1)
                    if e == 3:
                        act.wait_ge(gates_ps, r + 1)
                        if not (isinstance(r, int) and r == 0):
                            act.wait_ge(b2_ready, r)
                        act.activation(gates_t[:, :, :], ps_t[0:E, :].rearrange("e (t p) -> e t p", p=P),
                                       ACT.Copy).then_inc(gates_t_done, 1)
                    if e == 6 and not last:
                        copy_xt(r + 1, 1 - slot)

            act.wait_ge(w_in, N_W * DMA)
            act.activation(gate[:, :], gate_in[:, :], ACT.Tanh).then_inc(gate_set, 1)
            copy_xt(0, 0)
            tile(0, 0, False)
            tile(1, 1, False)
            with act.Fori(1, NT // 2 - 1) as i:
                for slot in range(2):
                    tile(2 * i + slot, slot, False)
            tile(NT - 2, 0, False)
            tile(NT - 1, 1, True)

        @block.vector
        def _(dve):
            def norm(pair, slot):
                r = 2 * pair + slot
                dve.wait_ge(x_loaded[slot], (pair + 1) * DMA)
                for t in range(SUB):
                    a = nc.vector.bn_stats(stats[:, t, :], x_in[:, slot, t, :])
                a.then_inc(stats_done, 1)
                dve.wait_ge(stats_done, r + 1)
                join_stats(nc, dve, stats, joined, mean, var_eps, joined_1, joined_2, eps_done, r)
                dve.wait_ge(rstd_done, r + 1)
                for t in range(SUB):
                    a = nc.vector.tensor_scalar(xn[:, t, :], x_in[:, slot, t, :], mean[:, t:t + 1], rstd[:, t:t + 1],
                                                ALU.subtract, ALU.mult)
                a.then_inc(xn_done, 1)

            def add_expert(r, e):
                n = E * r + e - 1
                dve.wait_ge(down_ready, n + 1)
                if e > 1:
                    dve.wait_ge(added, n)
                for t in range(SUB):
                    if e == 1:
                        a = nc.vector.tensor_scalar(acc[:, t, :], ps_o[:, 0, t, :], gates[:, t, 0:1], None, ALU.mult)
                    else:
                        a = nc.vector.scalar_tensor_tensor(acc[:, t, :], ps_o[:, (e - 1) % 2, t, :],
                                                           gates[:, t, e - 1:e], acc[:, t, :], ALU.mult, ALU.add)
                a.then_inc(added, 1)

            def choose(r):
                dve.wait_ge(logits_ps, r + 1)
                nc.vector.tensor_tensor(logits[:, :, :], ps_r[:, 0, 0:SUB * E].rearrange("p (t e) -> p t e", e=E),
                                        rb2_row[:, :].rearrange("p (a e) -> p a e", a=1).broadcast_to([P, SUB, E]),
                                        ALU.add).then_inc(logits_done, 1)
                dve.wait_ge(small_set, 1)
                dve.wait_ge(logits_done, r + 1)
                for t in range(SUB):
                    a = nc.vector.max(best[:, t, :], logits[:, t, :])
                a.then_inc(best_done, 1)
                dve.wait_ge(best_done, r + 1)
                nc.vector.tensor_tensor(diff[:, :], best[:, :, 0], best[:, :, 1], ALU.subtract).then_inc(diff_done, 1)
                for t in range(SUB):
                    a = nc.vector.max_index(best_at[:, t, :], best[:, t, :], logits[:, t, :])
                a.then_inc(at_done, 1)
                dve.wait_ge(at_done, r + 1)
                nc.vector.tensor_copy(best_no[:, :, :], best_at[:, :, 0:2]).then_inc(pick_done, 1)
                dve.wait_ge(tanh_done, r + 1)
                nc.vector.tensor_scalar(prob[:, 0, :], half_tanh[:, :], 0.5, 0.5, ALU.mult, ALU.add)
                nc.vector.tensor_scalar(prob[:, 1, :], half_tanh[:, :], -0.5, 0.5, ALU.mult, ALU.add).then_inc(prob_done, 1)
                dve.wait_ge(pick_done, r + 1)
                dve.wait_ge(prob_done, r + 1)
                for k in range(2):
                    for t in range(SUB):
                        a = nc.vector.tensor_scalar(pick[:, k, t, :], expert_no[:, :], best_no[:, t, k:k + 1],
                                                    prob[:, k, t:t + 1], ALU.is_equal, ALU.mult)
                a.then_inc(weigh_done, 1)
                dve.wait_ge(weigh_done, r + 1)
                if not (isinstance(r, int) and r == 0):
                    dve.wait_ge(gates_ps, r)
                nc.vector.tensor_tensor(gates[:, :, :], pick[:, 0, :, :], pick[:, 1, :, :], ALU.add).then_inc(gates_done, 1)
                dve.wait_ge(gates_done, r + 1)

            def finish(pair, slot):
                r = 2 * pair + slot
                dve.wait_ge(b2_ready, r + 1)
                dve.wait_ge(added, E * (r + 1))
                nc.vector.tensor_tensor(acc[:, :, :], acc[:, :, :], ps_r[:, :, :], ALU.add).then_inc(b2_added, 1)
                dve.wait_ge(b2_added, r + 1)
                if not (isinstance(pair, int) and pair == 0):
                    dve.wait_ge(y_stored[slot], pair * DMA)
                nc.vector.scalar_tensor_tensor(y[:, slot, :, :], acc[:, :, :], gate[:, 0:1], x_in[:, slot, :, :],
                                               ALU.mult, ALU.add).then_inc(y_done, 1)
                dve.wait_ge(y_done, r + 1)

            def tile(pair, slot, last):
                r = 2 * pair + slot
                choose(r)
                for e in range(1, NE):
                    add_expert(r, e)
                    if e == 3 and not last:
                        norm(pair + slot, 1 - slot)
                finish(pair, slot)

            for e in range(E):
                a = nc.vector.memset(expert_no[:, e:e + 1], float(e))
            a.then_inc(small_set, 1)
            dve.wait_ge(small_set, 1)
            norm(0, 0)
            dve.wait_ge(w_in, N_W * DMA)
            dve.wait_ge(gate_set, 1)
            tile(0, 0, False)
            tile(0, 1, False)
            with dve.Fori(1, NT // 2 - 1) as i:
                for slot in range(2):
                    tile(i, slot, False)
            tile(NT // 2 - 1, 0, False)
            tile(NT // 2 - 1, 1, True)

        @block.gpsimd
        def _(pool):
            def rstd_of(r):
                pool.wait_ge(eps_done, r + 1)
                nc.gpsimd.tensor_tensor(rstd[:, :], var_eps[:, :], minus_half[:, :], ALU.pow).then_inc(rstd_done, 1)

            nc.gpsimd.memset(minus_half[:, :], -0.5)
            nc.gpsimd.memset(ident[:, :], 0.0).then_inc(ident_set, 1)
            pool.wait_ge(ident_set, 1)
            nc.gpsimd.affine_select(out=ident[:, :], in_=ident[:, :], compare_op=ALU.not_equal, fill=1.0, base=0,
                                    pattern=[[-1, P]], channel_multiplier=1).then_inc(ident_set, 1)
            with pool.Fori(0, NT) as r:
                rstd_of(r)


def build(nc, a, out):
    B, _, _ = a["x"].shape
    TC = a["ctx_t"].shape[2]
    scratch = {
        "q": nc.dram_tensor("q_rows", [B, 2, H, 2, 2, D, T], F32, kind="Internal").ap(),
        "kself": nc.dram_tensor("kself_rows", [B, H, 2, 2, D, T], F32, kind="Internal").ap(),
        "kx": nc.dram_tensor("kx_rows", [B, H, 2, 2, D, TC], F32, kind="Internal").ap(),
        "y": nc.dram_tensor("y_rows", [B, 2, H, VW, T], F32, kind="Internal").ap(),
    }
    x1 = nc.dram_tensor("x1", [B, T, C], F32, kind="Internal").ap()
    att = {n: a[n] for n in ("Wq", "Wk", "Wv", "Wcq", "Wp", "Wck", "Wcv", "qk_bias", "bcv", "bv", "bp")}
    attention(nc, a["x"], a["ctx_t"], a["g_xattn"], att, x1, scratch)
    ffn = {n: a[n] for n in ("rw1", "rw2", "rb2", "w1", "w2", "b2", "up_b")}
    experts(nc, x1.rearrange("b t c -> (b t) c"), a["g_ffn"], ffn, out.rearrange("b t c -> (b t) c"))


def kernel(**inputs):
    import numpy as np
    import concourse.bacc as bacc
    from concourse import mybir as _mybir
    from concourse.bass_utils import run_bass_kernel_spmd

    i = {n.replace("L0_xattn_", "").replace("L0_ffn_", ""): np.asarray(v) for n, v in inputs.items()}
    ctx = i.pop("ctx_512")
    i["ctx_t"] = np.concatenate([ctx.transpose(0, 2, 1), np.ones((ctx.shape[0], 1, ctx.shape[1]), ctx.dtype)], 1)
    i["Wck"] = np.concatenate([i["Wck"], i.pop("bck")[None, :]], 0)
    i["qk_bias"] = np.stack([i.pop("bq"), i.pop("bk"), i.pop("bcq")], 1)
    up_b = np.concatenate([i.pop("rb1")[None], i.pop("b1")], 0)
    i["up_b"] = up_b.reshape(up_b.shape[0], -1, P).transpose(2, 0, 1)

    nc = bacc.Bacc("TRN2", target_bir_lowering=False, num_devices=1)
    arrays, aps = {}, {}
    for n, v in i.items():
        v = np.ascontiguousarray(v)
        arrays[f"in_{n}"] = v
        aps[n] = nc.dram_tensor(f"in_{n}", v.shape, _mybir.dt.from_np(v.dtype), kind="ExternalInput").ap()
    out = nc.dram_tensor("out", i["x"].shape, _mybir.dt.from_np(i["x"].dtype), kind="ExternalOutput").ap()
    build(nc, aps, out)
    r = run_bass_kernel_spmd(nc, [arrays], core_ids=[0])
    return r.results[0]["out"]
```

```python
from contextlib import ExitStack

import concourse.bass as bass
from concourse import mybir
from concourse.alu_op_type import AluOpType as ALU

F32 = mybir.dt.float32
F32R = mybir.dt.float32r
BF16 = mybir.dt.bfloat16
U32 = mybir.dt.uint32
ACT = mybir.ActivationFunctionType
AX_X = mybir.AxisListType.X

P = 128
T = 256
C = 128
H = 16
D = C // H
HEAD_ROWS = 4 * D
HEADS_IN_TILE = 3
SHIFT = HEADS_IN_TILE * HEAD_ROWS
ROWS = SHIFT + 2
HALF = H // 2
TILES = 3
GROUP = 4
GROUPS = H // GROUP
VW = 2 * D
EPS = 1e-5
NEG = -1.0e37
DMA = 16
LEAD = 5


def join_stats(nc, dve, stats, joined, mean, var_eps, joined_1, joined_2, eps_done, n):
    nc.vector.tensor_tensor(joined[:, :, 0:2], stats[:, :, 1:3], stats[:, :, 4:6], ALU.add)
    nc.vector.tensor_tensor(joined[:, :, 2], stats[:, :, 1], stats[:, :, 4], ALU.subtract).then_inc(joined_1, 1)
    dve.wait_ge(joined_1, n + 1)
    nc.vector.tensor_scalar(mean[:, :], joined[:, :, 0], 0.5, None, ALU.mult)
    nc.vector.tensor_scalar(joined[:, :, 3], joined[:, :, 1], 1.0 / C, EPS, ALU.mult, ALU.add)
    nc.vector.scalar_tensor_tensor(joined[:, :, 4], joined[:, :, 2], 0.25, joined[:, :, 2], ALU.mult,
                                   ALU.mult).then_inc(joined_2, 1)
    dve.wait_ge(joined_2, n + 1)
    nc.vector.tensor_tensor(var_eps[:, :], joined[:, :, 3], joined[:, :, 4], ALU.add).then_inc(eps_done, 1)


def known(eng, count):
    if not isinstance(count, int):
        eng.lower_val(count)
    return count


def attention(nc, x, ctx_t, g_x, w, x1, scratch):
    B = x.shape[0]
    TC = ctx_t.shape[2]
    CK = ctx_t.shape[1]
    NCH = -(-TC // P)
    TAIL = TC - (NCH - 1) * P
    STEPS = NCH + 2
    BSTEPS = STEPS * GROUPS
    NFULL = TC // 512
    REST = TC - NFULL * 512
    REST_W = REST + REST % 2
    SCALE = float(D) ** -0.5
    BANKS = 3
    assert BSTEPS % BANKS == 0 and GROUP * REST_W <= 512

    UNITS = [("cross", qt, i, kc) for qt in range(2) for i in range(GROUP) for kc in range(NFULL)]
    UNITS += [("cross_rest", qt, 0, 0) for qt in range(2)]
    UNITS += [("self", qt, i, 0) for qt in range(2) for i in (0, 2)]
    NU = len(UNITS)
    assert NU % BANKS == 0

    def units_at(pos):
        return range(NU * pos // STEPS, NU * (pos + 1) // STEPS)

    def target(j):
        s, pos = divmod(j + LEAD, STEPS)
        ahead, g = divmod(1 + s, GROUPS)
        return ahead, g, pos

    def in_half(g, i):
        h8 = GROUP * (g % 2) + i
        return g // 2, h8, h8 // HEADS_IN_TILE, h8 % HEADS_IN_TILE

    qs, kself_s, kx_s, ys = scratch["q"], scratch["kself"], scratch["kx"], scratch["y"]
    Wq, Wk, Wv, Wcq, Wp = w["Wq"], w["Wk"], w["Wv"], w["Wcq"], w["Wp"]

    with ExitStack() as ctx:
        def sb(name, shape, dt=F32):
            return ctx.enter_context(nc.sbuf_tensor(name, shape, dt))

        def psum(name, shape):
            return ctx.enter_context(nc.psum_tensor(name, shape, F32))

        def sem(name):
            return ctx.enter_context(nc.semaphore(name))

        wq_sb, wk_sb, wv_sb, wcq_sb, wp_sb = (sb(f"{n}_sb", [P, C]) for n in ("wq", "wk", "wv", "wcq", "wp"))
        wck_sb, wcv_sb = sb("wck_sb", [CK, C]), sb("wcv_sb", [CK - 1, C])
        bias_sb = sb("bias_sb", [P, 3])
        v_bias, bp_row = sb("v_bias", [P, 2, C]), sb("bp_row", [P, C])
        gate_in, gate = sb("gate_in", [P, 1]), sb("gate", [P, 1])
        ident = sb("ident", [P, P])
        ident_b = sb("ident_b", [P, P], BF16)
        mask_q = sb("mask_q", [P, 2, T], BF16)
        mask_k = sb("mask_k", [P, 2, T], BF16)
        minus_half = sb("minus_half", [P, 2])

        kx = [sb(f"kx{i}", [ROWS, TILES, TC], F32R) for i in range(2)]
        kself = [sb(f"kself{i}", [ROWS, TILES, T], F32R) for i in range(2)]
        qx = [sb(f"qx{i}", [ROWS, HALF, T], F32R) for i in range(2)]
        qself = [sb(f"qself{i}", [ROWS, HALF, T], F32R) for i in range(2)]
        v_all = sb("v_all", [P, STEPS, C])
        v_half = [sb(f"v_half{i}", [P, STEPS, HALF, VW]) for i in range(2)]

        x_in, xn, x_res = sb("x_in", [P, 2, C]), sb("xn", [P, 2, C]), sb("x_res", [P, 2, C])
        xn_t = sb("xn_t", [P, T])
        stats, joined, mean = sb("stats", [P, 2, 6]), sb("joined", [P, 2, 6]), sb("mean", [P, 2])
        var_eps, rstd = sb("var_eps", [P, 2]), sb("rstd", [P, 2])
        ctx_in = sb("ctx_in", [CK, TC])
        parts = sb("parts", [P, 3, 2, T], F32R)
        ck_parts = sb("ck_parts", [P, 2, TC], F32R)
        max_x = sb("max_x", [P, GROUP, 2, NFULL + 1])
        max_s = sb("max_s", [P, GROUP, 2])
        neg_max = sb("neg_max", [P, 2, GROUP * 2])
        shift = sb("shift", [P, 2, 2 * GROUP * 2], F32R)
        shift_t = sb("shift_t", [4 * GROUP * 2, P], F32R)
        probs = sb("probs", [P, 3, GROUP * T])
        y_raw = sb("y_raw", [P, 2, 2, T])
        y_in = sb("y_in", [P, 2, 2, T])
        y_rec, y_nrm = sb("y_rec", [P, 2, T]), sb("y_nrm", [P, 2, T])
        y_sum = sb("y_sum", [P, T])
        att = sb("att", [P, 2, C])
        x_new = sb("x_new", [P, 2, C])

        ps_s = psum("ps_s", [P, BANKS, 2, T])
        ps_a = psum("ps_a", [P, BANKS, 512])
        ps_m = psum("ps_m", [P, 512])
        ps_y = psum("ps_y", [P, 2, T])

        consts_in = sem("consts_in")
        zeroed = sem("zeroed")
        ones_set = sem("ones_set")
        masks_zero = sem("masks_zero")
        masks_set = sem("masks_set")
        gate_set = sem("gate_set")
        x_loaded = sem("x_loaded")
        ctx_loaded = sem("ctx_loaded")
        stats_done = sem("stats_done")
        joined_1, joined_2 = sem("joined_1"), sem("joined_2")
        eps_done = sem("eps_done")
        rstd_done = sem("rstd_done")
        xn_done = sem("xn_done")
        xnt_ps = sem("xnt_ps")
        xnt_done = sem("xnt_done")
        qk_ps = sem("qk_ps")
        qk_hi = sem("qk_hi")
        qk_lo = sem("qk_lo")
        cq_ps = sem("cq_ps")
        cq_hi = sem("cq_hi")
        cq_lo = sem("cq_lo")
        ck_ps = sem("ck_ps")
        ck_hi = sem("ck_hi")
        ck_lo = sem("ck_lo")
        cv_ps = sem("cv_ps")
        cv_done = sem("cv_done")
        v_ps = sem("v_ps")
        v_done = sem("v_done")
        qk_stored = sem("qk_stored")
        kx_stored = sem("kx_stored")
        half_in = [sem("half0_in"), sem("half1_in")]
        vhalf_done = [sem("vhalf0_done"), sem("vhalf1_done")]
        unit_ready = sem("unit_ready")
        unit_reduced = sem("unit_reduced")
        neg_done = sem("neg_done")
        shift_hi = sem("shift_hi")
        shift_lo = sem("shift_lo")
        shift_ps = sem("shift_ps")
        shift_t_done = sem("shift_t_done")
        shift_in = sem("shift_in")
        scores_ready = sem("scores_ready")
        exp_done = sem("exp_done")
        pv_done = sem("pv_done")
        y_copied = sem("y_copied")
        y_stored = [sem("y_stored_even"), sem("y_stored_odd")]
        y_loaded = sem("y_loaded")
        rec_done = sem("rec_done")
        nrm_done = sem("nrm_done")
        ysum_done = sem("ysum_done")
        xres_loaded = sem("xres_loaded")
        out_ps = sem("out_ps")
        att_done = sem("att_done")
        x1_done = sem("x1_done")
        x1_stored = sem("x1_stored")

        HALF_DMAS = 3 + 2 + 2 * HEADS_IN_TILE
        NCK = -(-TC // 512)
        NCV = -(-NCH // 4)
        N_CONST = 12

        J_LN, J_XN, J_XT, J_QK, J_CQ, J_REC, J_OUT = 2, 3, 4, 6, 8, 8, 12
        J_CK = [14, 16, 18, 20][:NCK]
        J_CV = [22, 24, 27, 29][:NCV]
        J_V = 31
        J_SHIFT = [STEPS * g + 10 for g in range(GROUPS)]

        block = ctx.enter_context(nc.Block())

        @block.sync
        def _(sp):
            def load_x(c):
                sp.wait_ge(masks_zero, 1)
                if not (isinstance(c, int) and c == 0):
                    sp.wait_ge(xn_done, c)
                sp.dma_start(x_in[:, :, :], x[c, :, :].rearrange("(t p) c -> p t c", p=P)).then_inc(x_loaded, DMA)
                sp.wait_ge(masks_zero, 1)
                if not (isinstance(c, int) and c == 0):
                    sp.wait_ge(cv_ps, c * NCV)
                sp.dma_start(ctx_in[:, :], ctx_t[c, :, :]).then_inc(ctx_loaded, DMA)

            def store_q_parts(c):
                sp.wait_ge(masks_zero, 1)
                sp.wait_ge(qk_lo, c + 1)
                for a in range(2):
                    for b in range(2):
                        sp.dma_start(qs[c, 0, :, a, b, :, :], parts[:, 0, a, :].bitcast(F32)).then_inc(qk_stored, DMA)
                        sp.dma_start(kself_s[c, :, a, b, :, :], parts[:, 1, b, :].bitcast(F32)).then_inc(qk_stored, DMA)
                sp.wait_ge(masks_zero, 1)
                sp.wait_ge(cq_lo, c + 1)
                for a in range(2):
                    for b in range(2):
                        sp.dma_start(qs[c, 1, :, a, b, :, :], parts[:, 2, a, :].bitcast(F32)).then_inc(qk_stored, DMA)

            def store_k_parts(c):
                sp.wait_ge(masks_zero, 1)
                sp.wait_ge(ck_lo, (c + 1) * NCK)
                for a in range(2):
                    for b in range(2):
                        sp.dma_start(kx_s[c, :, a, b, :, :], ck_parts[:, b, :].bitcast(F32)).then_inc(kx_stored, DMA)

            def load_half(c, half):
                q_rows, k_rows = known(sp, (c + 1) * 12 * DMA), known(sp, (c + 1) * 4 * DMA)
                read = known(sp, 2 * (c - 1) * BSTEPS + (half + 1) * BSTEPS)
                sp.wait_ge(masks_zero, 1)
                sp.wait_ge(qk_stored, q_rows)
                sp.wait_ge(kx_stored, k_rows)
                if not (isinstance(c, int) and c == 0):
                    sp.wait_ge(scores_ready, read)
                h0 = half * HALF
                kxr = kx_s[c, h0:h0 + HALF].rearrange("h a b d n -> (h a b d) n")
                ksr = kself_s[c, h0:h0 + HALF].rearrange("h a b d n -> (h a b d) n")
                for g in range(TILES):
                    r0, r1 = g * SHIFT, min((g + 1) * SHIFT, HALF * HEAD_ROWS)
                    sp.dma_start(kx[half][0:r1 - r0, g, :].bitcast(F32), kxr[r0:r1, :]).then_inc(half_in[half], DMA)
                sp.dma_start(kself[half][0:SHIFT, 0:2, :].bitcast(F32),
                             ksr[0:2 * SHIFT, :].rearrange("(g r) n -> r g n", g=2)).then_inc(half_in[half], DMA)
                sp.dma_start(kself[half][0:HALF * HEAD_ROWS - 2 * SHIFT, 2, :].bitcast(F32),
                             ksr[2 * SHIFT:, :]).then_inc(half_in[half], DMA)
                for st, dst in enumerate((qself[half], qx[half])):
                    src = qs[c, st, h0:h0 + HALF].rearrange("h a b d n -> (a b d) h n")
                    for q in range(HEADS_IN_TILE):
                        sp.dma_start(dst[q * HEAD_ROWS:(q + 1) * HEAD_ROWS, q:HALF:HEADS_IN_TILE, :].bitcast(F32),
                                     src[:, q:HALF:HEADS_IN_TILE, :]).then_inc(half_in[half], DMA)

            def store_shift(s, g):
                sp.wait_ge(shift_t_done, s + 1)
                n = GROUP * 2
                for part in range(2):
                    for st, dst in enumerate((qx[g // 2], qself[g // 2])):
                        r = (part * 2 + st) * n
                        h0 = GROUP * (g % 2)
                        sp.dma_start(dst[SHIFT + part:SHIFT + part + 1, h0:h0 + GROUP, :].bitcast(F32),
                                     shift_t[r:r + n, :].bitcast(F32)).then_inc(shift_in, DMA)

            def store_y(b, g):
                copied = known(sp, GROUPS * b + g + 1)
                sp.wait_ge(masks_zero, 1)
                sp.wait_ge(y_copied, copied)
                for i in range(GROUP):
                    sp.dma_start(ys[b, :, GROUP * g + i, :, :].rearrange("s r q -> r s q"),
                                 y_raw[32 * i:32 * i + VW, g % 2, :, :]).then_inc(y_stored[g % 2], DMA)

            def load_y(b):
                stored = known(sp, (b + 1) * (GROUPS // 2) * GROUP * DMA)
                sp.wait_ge(masks_zero, 1)
                for even_odd in y_stored:
                    sp.wait_ge(even_odd, stored)
                for st in range(2):
                    for part in range(2):
                        sp.dma_start(y_in[:, st, part, :],
                                     ys[b, st, :, part * D:(part + 1) * D, :]
                                     ).then_inc(y_loaded, DMA)
                sp.dma_start(x_res[:, :, :], x[b, :, :].rearrange("(t p) c -> p t c", p=P)).then_inc(xres_loaded, DMA)

            def store_x1(b):
                sp.wait_ge(masks_zero, 1)
                sp.wait_ge(x1_done, b + 1)
                sp.dma_start(x1[b, :, :].rearrange("(t p) c -> p t c", p=P), x_new[:, :, :]).then_inc(x1_stored, DMA)

            def element(b, first, last):
                if not last:
                    load_x(b + 1)
                if not first:
                    load_half(b, 1)
                    store_y(b - 1, GROUPS - 1)
                    load_y(b - 1)
                if not last:
                    store_q_parts(b + 1)
                store_shift(GROUPS * b + 1, 1)
                if not first:
                    store_x1(b - 1)
                store_y(b, 0)
                if not last:
                    store_k_parts(b + 1)
                store_shift(GROUPS * b + 2, 2)
                store_y(b, 1)
                if not last:
                    load_half(b + 1, 0)
                store_shift(GROUPS * b + 3, 3)
                store_y(b, 2)
                if not last:
                    store_shift(GROUPS * b + 4, 0)

            load_x(0)
            for dst, src in ((wq_sb, Wq), (wk_sb, Wk), (wcq_sb, Wcq), (wv_sb, Wv), (wp_sb, Wp),
                             (wck_sb, w["Wck"]), (wcv_sb, w["Wcv"])):
                sp.dma_start(dst[:, :], src).then_inc(consts_in, DMA)
            sp.dma_start(bias_sb[:, :], w["qk_bias"]).then_inc(consts_in, DMA)
            for st, n in enumerate(("bcv", "bv")):
                sp.dma_start(v_bias[:, st, :], w[n].rearrange("(a n) -> a n", a=1).broadcast_to([P, C])).then_inc(consts_in, DMA)
            sp.dma_start(bp_row[:, :], w["bp"].rearrange("(a n) -> a n", a=1).broadcast_to([P, C])).then_inc(consts_in, DMA)
            sp.dma_start(gate_in[:, :], g_x.rearrange("(a n) -> a n", a=1).broadcast_to([P, 1])).then_inc(consts_in, DMA)
            store_q_parts(0)
            store_k_parts(0)
            sp.wait_ge(zeroed, 1)
            sp.wait_ge(ones_set, 1)
            load_half(0, 0)
            load_half(0, 1)
            store_shift(0, 0)
            element(0, True, False)
            with sp.Fori(1, B - 1) as b:
                element(b, False, False)
            element(B - 1, False, True)
            store_y(B - 1, GROUPS - 1)
            load_y(B - 1)
            store_x1(B - 1)
            sp.wait_ge(x1_stored, B * DMA)

        @block.tensor
        def _(pe):
            def scores(b, j, pair):
                g, t = divmod(j, STEPS)
                k = 2 * (BSTEPS * b + j) + pair
                if not (isinstance(k, int) and k < BANKS):
                    pe.wait_ge(exp_done, k - BANKS + 1)
                if t == 0 and pair == 0:
                    pe.wait_ge(shift_in, (GROUPS * b + g + 1) * 4 * DMA)
                out = ps_s[:, (2 * j + pair) % BANKS, :, :]
                own = t - NCH
                if own >= 0:
                    qs_ = slice(own * P, (own + 1) * P)
                    pe.matmul(out[:, :, qs_], ident_b[:, :], mask_k[:, own:own + 1, qs_].broadcast_to([P, 2, P]),
                              start=True, stop=False, skip_group_check=True)
                for i in (2 * pair, 2 * pair + 1):
                    half, h8, tile, _ = in_half(g, i)
                    if own < 0:
                        n = P if t < NCH - 1 else TAIL
                        mm = pe.matmul(out[0:n, i % 2, :], kx[half][:, tile, t * P:t * P + n],
                                       qx[half][:, h8, :], start=True, stop=True)
                    else:
                        mm = pe.matmul(out[:, i % 2, :], kself[half][:, tile, own * P:(own + 1) * P],
                                       qself[half][:, h8, :], start=False, stop=(i % 2 == 1), skip_group_check=True)
                mm.then_inc(scores_ready, 1)

            def unit(b, g, u):
                number = NU * (GROUPS * b + g) + u
                if not (isinstance(number, int) and number < BANKS):
                    pe.wait_ge(unit_reduced, number - BANKS + 1)
                kind, qt, i0, kc = UNITS[u]
                out = ps_a[:, u % BANKS, :]
                q = slice(qt * P, (qt + 1) * P)
                if kind == "cross":
                    half, h8, tile, _ = in_half(g, i0)
                    mm = pe.matmul(out, qx[half][0:SHIFT, h8, q], kx[half][0:SHIFT, tile, kc * 512:(kc + 1) * 512],
                                   start=True, stop=True)
                elif kind == "cross_rest":
                    for i in range(GROUP):
                        half, h8, tile, _ = in_half(g, i)
                        mm = pe.matmul(out[:, i * REST_W:(i + 1) * REST_W], qx[half][0:SHIFT, h8, q],
                                       kx[half][0:SHIFT, tile, TC - REST_W:TC], start=True, stop=True)
                else:
                    out = out.rearrange("p (i n) -> p i n", n=T)
                    pe.matmul(out[:, :, q], ident_b[:, :], mask_q[:, qt:qt + 1, q].broadcast_to([P, 2, P]),
                              start=True, stop=False, skip_group_check=True)
                    for i in (i0, i0 + 1):
                        half, h8, tile, _ = in_half(g, i)
                        mm = pe.matmul(out[:, i - i0, :], qself[half][0:SHIFT, h8, q],
                                       kself[half][0:SHIFT, tile, :], start=False, stop=(i == i0 + 1),
                                       skip_group_check=True)
                mm.then_inc(unit_ready, 1)

            def operands_here(b, g):
                if g % 2 == 0:
                    pe.wait_ge(half_in[g // 2], (b + 1) * HALF_DMAS * DMA)

            def pv(b, j):
                g, t = divmod(j, STEPS)
                pe.wait_ge(exp_done, 2 * (BSTEPS * b + j) + 2)
                if t == 0:
                    if not (isinstance(b, int) and GROUPS * b + g == 0):
                        pe.wait_ge(y_copied, GROUPS * b + g)
                    if g % 2 == 0:
                        pe.wait_ge(vhalf_done[g // 2], b + 1)
                for i in range(GROUP):
                    half, h8, _, _ = in_half(g, i)
                    if t < NCH:
                        n = P if t < NCH - 1 else TAIL
                        mm = pe.matmul(ps_y[32 * i:32 * i + VW, 0, :], v_half[half][0:n, t, h8, :],
                                       probs[0:n, j % 3, i * T:(i + 1) * T], start=(t == 0), stop=(t == NCH - 1))
                    elif t == NCH:
                        mm = pe.matmul(ps_y[32 * i:32 * i + VW, 1, :], v_half[half][:, t, h8, :],
                                       probs[:, j % 3, i * T:(i + 1) * T], start=True, stop=False)
                    else:
                        mm = pe.matmul(ps_y[32 * i:32 * i + VW, 1, P:T], v_half[half][:, t, h8, :],
                                       probs[:, j % 3, i * T + P:(i + 1) * T], start=False, stop=True)
                mm.then_inc(pv_done, 1)

            def shift_job(s):
                pe.wait_ge(shift_lo, s + 1)
                pe.transpose(ps_m[0:4 * GROUP * 2, 0:P], shift[:, :, :].rearrange("p a n -> p (a n)").bitcast(F32),
                             ident[:, :]).then_inc(shift_ps, 1)

            def xn_job(c):
                pe.wait_ge(xn_done, c + 1)
                if not (isinstance(c, int) and c == 0):
                    pe.wait_ge(shift_t_done, GROUPS * c - GROUPS + 1)
                for t in range(2):
                    mm = pe.transpose(ps_m[:, t * P:(t + 1) * P], xn[:, t, :], ident[:, :])
                mm.then_inc(xnt_ps, 1)

            def qk_job(c):
                pe.wait_ge(xnt_done, c + 1)
                pe.matmul(ps_m[:, 0:T], wq_sb[:, :], xn_t[:, :], start=True, stop=True)
                pe.matmul(ps_m[:, T:2 * T], wk_sb[:, :], xn_t[:, :], start=True, stop=True).then_inc(qk_ps, 1)

            def cq_job(c):
                pe.wait_ge(qk_lo, c + 1)
                pe.matmul(ps_m[:, 0:T], wcq_sb[:, :], xn_t[:, :], start=True, stop=True).then_inc(cq_ps, 1)

            def ck_job(c, n):
                if n > 0:
                    pe.wait_ge(ck_lo, c * NCK + n)
                else:
                    pe.wait_ge(cq_lo, c + 1)
                    pe.wait_ge(ctx_loaded, (c + 1) * DMA)
                k0, k1 = n * 512, min((n + 1) * 512, TC)
                pe.matmul(ps_m[:, 0:k1 - k0], wck_sb[:, :], ctx_in[:, k0:k1], start=True, stop=True).then_inc(ck_ps, 1)

            def cv_job(c, n):
                if n > 0:
                    pe.wait_ge(cv_done, c * NCV + n)
                else:
                    pe.wait_ge(ck_lo, (c + 1) * NCK)
                for ch in range(4 * n, min(4 * n + 4, NCH)):
                    k = P if ch < NCH - 1 else TAIL
                    mm = pe.matmul(ps_m[0:k, (ch - 4 * n) * C:(ch - 4 * n + 1) * C], ctx_in[0:CK - 1, ch * P:ch * P + k],
                                   wcv_sb[:, :], start=True, stop=True)
                mm.then_inc(cv_ps, 1)

            def v_job(c):
                pe.wait_ge(cv_done, (c + 1) * NCV)
                for t in range(2):
                    mm = pe.matmul(ps_m[:, t * C:(t + 1) * C], xn_t[:, t * P:(t + 1) * P], wv_sb[:, :],
                                   start=True, stop=True)
                mm.then_inc(v_ps, 1)

            def out_job(b):
                pe.wait_ge(ysum_done, b + 1)
                for t in range(2):
                    mm = pe.matmul(ps_m[:, t * C:(t + 1) * C], y_sum[:, t * P:(t + 1) * P], wp_sb[:, :],
                                   start=True, stop=True)
                mm.then_inc(out_ps, 1)

            def element(b, first, last):
                for j in range(BSTEPS):
                    ahead, g, pos = target(j)
                    mine = [] if last and ahead else list(units_at(pos))
                    for pair in range(2):
                        if j + 1 < BSTEPS:
                            scores(b, j + 1, pair)
                        elif not last:
                            scores(b + 1, 0, pair)
                        if mine and pos == 0 and pair == 0:
                            operands_here(b + ahead, g)
                        if mine:
                            unit(b + ahead, g, mine[pair])
                    if not last:
                        if j == J_XT:
                            xn_job(b + 1)
                        if j == J_QK:
                            qk_job(b + 1)
                        if j == J_CQ:
                            cq_job(b + 1)
                        if j in J_CK:
                            if j == J_CK[0] and not first:
                                pe.wait_ge(att_done, b)
                            if j in J_CK[:1]:
                                pe.wait_ge(shift_t_done, GROUPS * b + 2)
                            ck_job(b + 1, J_CK.index(j))
                        if j in J_CV:
                            if j == J_CV[2]:
                                pe.wait_ge(shift_t_done, GROUPS * b + 3)
                            cv_job(b + 1, J_CV.index(j))
                        if j == J_V:
                            v_job(b + 1)
                    if j == J_OUT and not first:
                        pe.wait_ge(shift_t_done, GROUPS * b + 2)
                        out_job(b - 1)
                    if j in J_SHIFT and not (last and j == J_SHIFT[-1]):
                        k = J_SHIFT.index(j)
                        if k == 0 and not last:
                            pe.wait_ge(cq_lo, b + 2)
                        if k == 0 and last:
                            pe.wait_ge(shift_t_done, GROUPS * b + 1)
                        if k == 1 and not last:
                            pe.wait_ge(cv_done, (b + 1) * NCV + 2)
                        if k == 1 and last:
                            pe.wait_ge(att_done, b)
                        if k == 2 and not last:
                            pe.wait_ge(v_done, b + 2)
                        if k == 2 and last or k == 3:
                            pe.wait_ge(shift_t_done, GROUPS * b + k + 1)
                        shift_job(GROUPS * b + 1 + k)
                    pv(b, j)

            pe.wait_ge(consts_in, N_CONST * DMA)
            pe.wait_ge(masks_set, 4)
            xn_job(0)
            qk_job(0)
            cq_job(0)
            for n in range(NCK):
                ck_job(0, n)
            for n in range(NCV):
                cv_job(0, n)
            v_job(0)
            pe.wait_ge(ones_set, 1)
            operands_here(0, 0)
            for u in range(NU):
                unit(0, 0, u)
            pe.wait_ge(v_done, 1)
            shift_job(0)
            for pos in range(LEAD):
                for u in units_at(pos):
                    unit(0, 1, u)
            scores(0, 0, 0)
            scores(0, 0, 1)
            element(0, True, False)
            with pe.Fori(1, B - 1) as b:
                element(b, False, False)
            element(B - 1, False, True)
            pe.wait_ge(shift_t_done, GROUPS * B)
            out_job(B - 1)

        @block.scalar
        def _(act):
            def exp(b, j):
                g, t = divmod(j, STEPS)
                if not (isinstance(b, int) and BSTEPS * b + j < 3):
                    act.wait_ge(pv_done, BSTEPS * b + j - 2)
                n = TAIL if t == NCH - 1 else P
                q0 = P if t == NCH + 1 else 0
                dst = probs[0:n, j % 3, :].rearrange("p (i q) -> p i q", q=T)
                for pair in range(2):
                    act.wait_ge(scores_ready, 2 * (BSTEPS * b + j) + pair + 1)
                    act.activation(dst[:, 2 * pair:2 * pair + 2, q0:T], ps_s[0:n, (2 * j + pair) % BANKS, :, q0:T],
                                   ACT.Exp, scale=SCALE).then_inc(exp_done, 1)

            def copy_y(b, g):
                act.wait_ge(pv_done, BSTEPS * b + (g + 1) * STEPS)
                if not (isinstance(b, int) and GROUPS * b + g < 2):
                    act.wait_ge(y_stored[g % 2], (GROUPS // 2 * b + g // 2) * GROUP * DMA)
                act.activation(y_raw[:, g % 2, :, :], ps_y[:, :, :], ACT.Copy).then_inc(y_copied, 1)

            def xnt(c):
                act.wait_ge(xnt_ps, c + 1)
                if not (isinstance(c, int) and c == 0):
                    act.wait_ge(v_ps, c)
                act.activation(xn_t[:, :], ps_m[:, 0:T], ACT.Copy).then_inc(xnt_done, 1)

            def qk(c):
                act.wait_ge(qk_ps, c + 1)
                if not (isinstance(c, int) and c == 0):
                    act.wait_ge(qk_stored, c * 12 * DMA)
                for i in range(2):
                    a = act.activation(parts[:, i, 0, :], ps_m[:, i * T:(i + 1) * T], ACT.Identity, bias=bias_sb[:, i:i + 1])
                a.then_inc(qk_hi, 1)

            def cq(c):
                act.wait_ge(cq_ps, c + 1)
                act.activation(parts[:, 2, 0, :], ps_m[:, 0:T], ACT.Identity, bias=bias_sb[:, 2:3]).then_inc(cq_hi, 1)

            def ck(c, n):
                act.wait_ge(ck_ps, c * NCK + n + 1)
                if n == 0 and not (isinstance(c, int) and c == 0):
                    act.wait_ge(kx_stored, c * 4 * DMA)
                k0, k1 = n * 512, min((n + 1) * 512, TC)
                act.activation(ck_parts[:, 0, k0:k1], ps_m[:, 0:k1 - k0], ACT.Copy).then_inc(ck_hi, 1)

            def cv(c, n):
                act.wait_ge(cv_ps, c * NCV + n + 1)
                if n == 0 and not (isinstance(c, int) and c == 0):
                    act.wait_ge(vhalf_done[1], c)
                full = min(4 * n + 4, NCH - 1) - 4 * n
                a = None
                if full > 0:
                    a = act.activation(v_all[:, 4 * n:4 * n + full, :],
                                       ps_m[:, 0:full * C].rearrange("p (a c) -> p a c", c=C), ACT.Copy)
                if 4 * n + 4 >= NCH:
                    a = act.activation(v_all[0:TAIL, NCH - 1, :], ps_m[0:TAIL, full * C:(full + 1) * C], ACT.Copy)
                a.then_inc(cv_done, 1)

            def shift_rows(s):
                act.wait_ge(shift_ps, s + 1)
                if not (isinstance(s, int) and s == 0):
                    act.wait_ge(shift_in, s * 4 * DMA)
                act.activation(shift_t[:, :], ps_m[0:4 * GROUP * 2, 0:P], ACT.Copy).then_inc(shift_t_done, 1)

            def element(b, first, last):
                for j in range(BSTEPS):
                    if j + 1 < BSTEPS:
                        exp(b, j + 1)
                    elif not last:
                        exp(b + 1, 0)
                    if j % STEPS == STEPS - 1:
                        copy_y(b, j // STEPS)
                    if not last:
                        if j == J_XT:
                            xnt(b + 1)
                        if j == J_QK:
                            qk(b + 1)
                        if j == J_CQ:
                            cq(b + 1)
                        if j in J_CK:
                            ck(b + 1, J_CK.index(j))
                        if j in J_CV:
                            cv(b + 1, J_CV.index(j))
                    if j in J_SHIFT and not (last and j == J_SHIFT[-1]):
                        shift_rows(GROUPS * b + 1 + J_SHIFT.index(j))

            act.wait_ge(consts_in, N_CONST * DMA)
            act.activation(gate[:, :], gate_in[:, :], ACT.Tanh).then_inc(gate_set, 1)
            xnt(0)
            qk(0)
            cq(0)
            for n in range(NCK):
                ck(0, n)
            act.wait_ge(zeroed, 1)
            for n in range(NCV):
                cv(0, n)
            shift_rows(0)
            exp(0, 0)
            element(0, True, False)
            with act.Fori(1, B - 1) as b:
                element(b, False, False)
            element(B - 1, False, True)

        @block.vector
        def _(dve):
            def reduce_unit(b, g, u):
                dve.wait_ge(unit_ready, NU * (GROUPS * b + g) + u + 1)
                kind, qt, i0, kc = UNITS[u]
                src = ps_a[:, u % BANKS, :]
                if kind == "cross":
                    out = max_x[:, i0, qt, kc:kc + 1]
                elif kind == "cross_rest":
                    out, src = max_x[:, :, qt, NFULL], src[:, 0:GROUP * REST_W].rearrange("p (i n) -> p i n", n=REST_W)
                else:
                    out, src = max_s[:, i0:i0 + 2, qt], src.rearrange("p (i n) -> p i n", n=T)[:, :, 0:(qt + 1) * P]
                nc.vector.tensor_reduce(out, src, AX_X, ALU.max).then_inc(unit_reduced, 1)

            def shift_parts(b, g):
                s = GROUPS * b + g
                dve.wait_ge(unit_reduced, NU * (s + 1))
                if not (isinstance(s, int) and s == 0):
                    dve.wait_ge(shift_ps, s)
                nc.vector.tensor_reduce(neg_max[:, 0, :], max_x[:, :, :, :].rearrange("p i t n -> p (i t) n"),
                                        AX_X, ALU.max, negate=True)
                nc.vector.tensor_scalar(neg_max[:, 1, :], max_s[:, :, :].rearrange("p i t -> p (i t)"), -1.0, None,
                                        ALU.mult).then_inc(neg_done, 1)
                dve.wait_ge(neg_done, s + 1)
                flat = neg_max[:, :, :].rearrange("p a n -> p (a n)")
                nc.vector.tensor_copy(shift[:, 0, :], flat).then_inc(shift_hi, 1)
                dve.wait_ge(shift_hi, s + 1)
                nc.vector.tensor_tensor(shift[:, 1, :], flat, shift[:, 0, :].bitcast(F32), ALU.subtract).then_inc(shift_lo, 1)

            def ln_stats(c):
                dve.wait_ge(x_loaded, (c + 1) * DMA)
                for t in range(2):
                    a = nc.vector.bn_stats(stats[:, t, :], x_in[:, t, :])
                a.then_inc(stats_done, 1)
                dve.wait_ge(stats_done, c + 1)
                join_stats(nc, dve, stats, joined, mean, var_eps, joined_1, joined_2, eps_done, c)

            def ln_apply(c):
                dve.wait_ge(rstd_done, c + 1)
                for t in range(2):
                    a = nc.vector.tensor_scalar(xn[:, t, :], x_in[:, t, :], mean[:, t:t + 1], rstd[:, t:t + 1],
                                                ALU.subtract, ALU.mult)
                a.then_inc(xn_done, 1)

            def lo_part(out_lo, hi, src, bias):
                return nc.vector.scalar_tensor_tensor(out_lo, src, bias, hi.bitcast(F32), ALU.add, ALU.subtract)

            def qk(c):
                dve.wait_ge(qk_hi, c + 1)
                for i in range(2):
                    a = lo_part(parts[:, i, 1, :], parts[:, i, 0, :], ps_m[:, i * T:(i + 1) * T], bias_sb[:, i:i + 1])
                a.then_inc(qk_lo, 1)

            def cq(c):
                dve.wait_ge(cq_hi, c + 1)
                lo_part(parts[:, 2, 1, :], parts[:, 2, 0, :], ps_m[:, 0:T], bias_sb[:, 2:3]).then_inc(cq_lo, 1)

            def ck(c, n):
                dve.wait_ge(ck_hi, c * NCK + n + 1)
                k0, k1 = n * 512, min((n + 1) * 512, TC)
                nc.vector.tensor_tensor(ck_parts[:, 1, k0:k1], ps_m[:, 0:k1 - k0], ck_parts[:, 0, k0:k1].bitcast(F32),
                                        ALU.subtract).then_inc(ck_lo, 1)

            def v(c):
                dve.wait_ge(v_ps, c + 1)
                if not (isinstance(c, int) and c == 0):
                    dve.wait_ge(vhalf_done[1], c)
                nc.vector.tensor_copy(v_all[:, NCH:NCH + 2, :],
                                      ps_m[:, 0:2 * C].rearrange("p (a c) -> p a c", c=C)).then_inc(v_done, 1)

            def reciprocals(b):
                dve.wait_ge(y_loaded, (b + 1) * 4 * DMA)
                if not (isinstance(b, int) and b == 0):
                    dve.wait_ge(nrm_done, b)
                nc.vector.reciprocal(y_rec[:, :, :], y_in[:, :, 1, :]).then_inc(rec_done, 1)

            def residual(b):
                dve.wait_ge(out_ps, b + 1)
                dve.wait_ge(xres_loaded, (b + 1) * DMA)
                nc.vector.tensor_tensor(att[:, :, :], ps_m[:, 0:2 * C].rearrange("p (a c) -> p a c", c=C),
                                        bp_row[:, :].rearrange("p (a c) -> p a c", a=1).broadcast_to([P, 2, C]),
                                        ALU.add).then_inc(att_done, 1)
                dve.wait_ge(att_done, b + 1)
                if not (isinstance(b, int) and b == 0):
                    dve.wait_ge(x1_stored, b * DMA)
                nc.vector.scalar_tensor_tensor(x_new[:, :, :], att[:, :, :], gate[:, 0:1], x_res[:, :, :],
                                               ALU.mult, ALU.add).then_inc(x1_done, 1)

            def element(b, first, last):
                for j in range(BSTEPS):
                    ahead, g, pos = target(j)
                    if not (last and ahead):
                        for u in units_at(pos):
                            reduce_unit(b + ahead, g, u)
                        if pos == STEPS - 1:
                            shift_parts(b + ahead, g)
                    if not last:
                        if j == J_LN:
                            ln_stats(b + 1)
                        if j == J_XN:
                            ln_apply(b + 1)
                        if j == J_QK + 1:
                            qk(b + 1)
                        if j == J_CQ + 1:
                            cq(b + 1)
                        if j - 1 in J_CK:
                            ck(b + 1, J_CK.index(j - 1))
                        if j == J_V + 1:
                            v(b + 1)
                    if not first:
                        if j == J_REC:
                            reciprocals(b - 1)
                        if j == J_OUT + 1:
                            residual(b - 1)

            ln_stats(0)
            ln_apply(0)
            nc.vector.memset(ps_y[:, :, :], 0.0)
            nc.vector.memset(v_all[64:P, NCH - 1, :], 0.0)
            for i in range(2):
                nc.vector.memset(kx[i][64:ROWS, TILES - 1, :].bitcast(F32), 0.0)
                nc.vector.memset(kself[i][64:ROWS, TILES - 1, :].bitcast(F32), 0.0)
                nc.vector.memset(qx[i][:, :, :].bitcast(F32), 0.0)
                a = nc.vector.memset(qself[i][:, :, :].bitcast(F32), 0.0)
            a.then_inc(zeroed, 1)
            dve.wait_ge(zeroed, 1)
            for i in range(2):
                nc.vector.memset(kx[i][SHIFT:ROWS, :, :].bitcast(F32), 1.0)
                a = nc.vector.memset(kself[i][SHIFT:ROWS, :, :].bitcast(F32), 1.0)
            a.then_inc(ones_set, 1)
            dve.wait_ge(consts_in, N_CONST * DMA)
            qk(0)
            cq(0)
            for n in range(NCK):
                ck(0, n)
            v(0)
            for u in range(NU):
                reduce_unit(0, 0, u)
            shift_parts(0, 0)
            for pos in range(LEAD):
                for u in units_at(pos):
                    reduce_unit(0, 1, u)
            dve.wait_ge(gate_set, 1)
            element(0, True, False)
            with dve.Fori(1, B - 1) as b:
                element(b, False, False)
            element(B - 1, False, True)
            reciprocals(B - 1)
            residual(B - 1)

        @block.gpsimd
        def _(pool):
            def fill_v_half(b, half):
                pool.wait_ge(cv_done, (b + 1) * NCV)
                pool.wait_ge(v_done, b + 1)
                if not (isinstance(b, int) and b == 0):
                    pool.wait_ge(pv_done, (b - 1) * BSTEPS + (half + 1) * (BSTEPS // 2))
                for st, (n0, n1) in enumerate(((0, NCH), (NCH, NCH + 2))):
                    src = v_all[:, n0:n1, half * HALF * D:(half + 1) * HALF * D].rearrange("p n (h d) -> p n h d", d=D)
                    bias = v_bias[:, st:st + 1, half * HALF * D:(half + 1) * HALF * D].rearrange("p n (h d) -> p n h d", d=D)
                    a = nc.gpsimd.tensor_tensor(v_half[half][:, n0:n1, :, 0:D], src,
                                                bias.broadcast_to([P, n1 - n0, HALF, D]), ALU.add)
                a.then_inc(vhalf_done[half], 1)

            def rstd_of(c):
                pool.wait_ge(eps_done, c + 1)
                nc.gpsimd.tensor_tensor(rstd[:, :], var_eps[:, :], minus_half[:, :], ALU.pow).then_inc(rstd_done, 1)

            def normalise(b):
                pool.wait_ge(rec_done, b + 1)
                nc.gpsimd.tensor_tensor(y_nrm[:, :, :], y_in[:, :, 0, :], y_rec[:, :, :], ALU.mult).then_inc(nrm_done, 1)
                pool.wait_ge(nrm_done, b + 1)
                if not (isinstance(b, int) and b == 0):
                    pool.wait_ge(out_ps, b)
                nc.gpsimd.tensor_tensor(y_sum[:, :], y_nrm[:, 0, :], y_nrm[:, 1, :], ALU.add).then_inc(ysum_done, 1)

            def element(b, first, last):
                if not first:
                    fill_v_half(b, 1)
                if not last:
                    rstd_of(b + 1)
                if not first:
                    normalise(b - 1)
                if not last:
                    fill_v_half(b + 1, 0)

            nc.gpsimd.memset(minus_half[:, :], -0.5).then_inc(masks_zero, 1)
            pool.wait_ge(masks_zero, 1)
            rstd_of(0)
            for m in (ident, ident_b):
                nc.gpsimd.memset(m[:, :], 0.0).then_inc(masks_zero, 1)
            for m in (mask_q, mask_k):
                nc.gpsimd.memset(m[:, :, :], 0.0).then_inc(masks_zero, 1)
            pool.wait_ge(masks_zero, 5)
            for m in (ident, ident_b):
                nc.gpsimd.affine_select(out=m[:, :], in_=m[:, :], compare_op=ALU.not_equal, fill=1.0, base=0,
                                        pattern=[[-1, P]], channel_multiplier=1).then_inc(masks_set, 1)
            nc.gpsimd.affine_select(out=mask_q[:, :, :], in_=mask_q[:, :, :], compare_op=ALU.is_ge, fill=NEG, base=0,
                                    pattern=[[P, 2], [-1, T]], channel_multiplier=1).then_inc(masks_set, 1)
            nc.gpsimd.affine_select(out=mask_k[:, :, :], in_=mask_k[:, :, :], compare_op=ALU.is_ge, fill=NEG, base=0,
                                    pattern=[[-P, 2], [1, T]], channel_multiplier=-1).then_inc(masks_set, 1)
            for i in range(2):
                nc.gpsimd.memset(v_half[i][:, :, :, D:VW], 1.0)
            pool.wait_ge(zeroed, 1)
            pool.wait_ge(consts_in, N_CONST * DMA)
            fill_v_half(0, 0)
            fill_v_half(0, 1)
            element(0, True, False)
            with pool.Fori(1, B - 1) as b:
                element(b, False, False)
            element(B - 1, False, True)
            normalise(B - 1)


def experts(nc, x1, g_f, w, out):
    R = x1.shape[0]
    E, _, HID = w["w1"].shape
    TR = 512
    NT = R // TR
    SUB = TR // P
    M = HID // P
    NE = E + 1
    RING_H = 3
    RING_O = 3
    assert NE * M % RING_H == 0

    with ExitStack() as ctx:
        def sb(name, shape, dt=F32):
            return ctx.enter_context(nc.sbuf_tensor(name, shape, dt))

        def psum(name, shape):
            return ctx.enter_context(nc.psum_tensor(name, shape, F32))

        def sem(name):
            return ctx.enter_context(nc.semaphore(name))

        up_w, down_w = sb("up_w", [P, NE, HID]), sb("down_w", [P, E, M, C])
        up_hi, up_lo = sb("up_hi", [P, NE, HID], F32R), sb("up_lo", [P, NE, HID], F32R)
        down_hi, down_lo = sb("down_hi", [P, E, M, C], F32R), sb("down_lo", [P, E, M, C], F32R)
        up_b = sb("up_b", [P, NE, M])
        rw2_sb = sb("rw2_sb", [P, M, E])
        rb2_row = sb("rb2_row", [P, E])
        b2_sb = sb("b2_sb", [2 * E, C])
        gate_in, gate = sb("fgate_in", [P, 1]), sb("fgate", [P, 1])
        ident = sb("fident", [P, P])
        select = sb("select", [2 * E, E, P], F32R)
        expert_no = sb("expert_no", [P, E])
        minus_half = sb("fminus_half", [P, SUB])

        x_in = sb("fx_in", [P, 2, SUB, C])
        xn = sb("fxn", [P, SUB, C])
        x_hi, x_lo = sb("x_hi", [P, 2, TR], F32R), sb("x_lo", [P, 2, TR], F32R)
        stats, joined, mean = sb("fstats", [P, SUB, 6]), sb("fjoined", [P, SUB, 6]), sb("fmean", [P, SUB])
        var_eps, rstd = sb("fvar_eps", [P, SUB]), sb("frstd", [P, SUB])
        hid = sb("hid", [P, 2, M, TR])
        hid_hi, hid_lo = sb("hid_hi", [P, 2, M, TR], F32R), sb("hid_lo", [P, 2, M, TR], F32R)
        logits = sb("logits", [P, SUB, E])
        best = sb("best", [P, SUB, 8])
        best_at = sb("best_at", [P, SUB, 8], U32)
        best_no = sb("best_no", [P, SUB, 2])
        diff = sb("diff", [P, SUB])
        half_tanh = sb("half_tanh", [P, SUB])
        prob = sb("prob", [P, 2, SUB])
        pick = sb("pick", [P, 2, SUB, E])
        gates = sb("gates", [P, SUB, E])
        gate_parts = sb("gate_parts", [P, SUB, 2, E], F32R)
        gates_t = sb("gates_t", [2 * E, TR], F32R)
        spread = sb("spread", [P, 2, TR])
        weighed = sb("weighed", [P, 2, TR])
        acc = sb("acc", [P, TR])
        y = sb("fy", [P, 2, SUB, C])

        ps_h = psum("ps_h", [P, RING_H, TR])
        ps_o = psum("ps_o", [P, RING_O, TR])
        ps_t = psum("ps_t", [P, TR])
        ps_g = psum("ps_g", [P, TR])

        w_in = sem("w_in")
        w_loaded = [sem(f"w_loaded{e}") for e in range(NE)]
        w_hi_act, w_hi_pool = sem("w_hi_by_scalar"), sem("w_hi_by_gpsimd")
        w_split = sem("w_split")
        small_set = sem("small_set")
        select_set = sem("select_set")
        ident_set = sem("fident_set")
        gate_set = sem("fgate_set")
        x_loaded = [sem("fx_loaded_even"), sem("fx_loaded_odd")]
        stats_done, eps_done = sem("fstats_done"), sem("feps_done")
        joined_1, joined_2 = sem("fjoined_1"), sem("fjoined_2")
        rstd_done, xn_done = sem("frstd_done"), sem("fxn_done")
        xnt_ps, x_hi_done, x_lo_done = sem("fxnt_ps"), sem("x_hi_done"), sem("x_lo_done")
        up_ready = sem("up_ready")
        silu_done, hid_hi_done, hid_lo_done = sem("silu_done"), sem("hid_hi_done"), sem("hid_lo_done")
        logits_ps, logits_done = sem("logits_ps"), sem("logits_done")
        best_done, at_done, diff_done = sem("best_done"), sem("at_done"), sem("diff_done")
        tanh_done, prob_done, pick_done = sem("tanh_done"), sem("prob_done"), sem("pick_done")
        picked, gates_done, gates_hi, gates_lo = sem("picked"), sem("gates_done"), sem("gates_hi"), sem("gates_lo")
        gates_ps, gates_t_done = sem("gates_ps"), sem("gates_t_done")
        spread_ps, spread_done = sem("spread_ps"), sem("spread_done")
        down_ready, weighed_done, added = sem("down_ready"), sem("weighed_done"), sem("added")
        out_ps, y_done = sem("fout_ps"), sem("fy_done")
        y_stored = [sem("fy_stored_even"), sem("fy_stored_odd")]

        N_W = 6
        block = ctx.enter_context(nc.Block())

        def first_tile(r):
            return isinstance(r, int) and r == 0

        def hidden_slot(slot, e):
            return (slot * NE + e) % 2

        @block.sync
        def _(sp):
            def load(r, slot):
                sp.dma_start(x_in[:, slot, :, :], x1[bass.ds(r * TR, TR), :].rearrange("(t p) c -> p t c", p=P)
                             ).then_inc(x_loaded[slot], DMA)

            def store(r, slot):
                sp.wait_ge(w_in, N_W * DMA)
                sp.wait_ge(y_done, r + 1)
                sp.dma_start(out[bass.ds(r * TR, TR), :].rearrange("(t p) c -> p t c", p=P), y[:, slot, :, :]
                             ).then_inc(y_stored[slot], DMA)

            load(0, 0)
            sp.dma_start(up_w[:, 0, :], w["rw1"]).then_inc(w_loaded[0], DMA)
            sp.dma_start(up_b[:, :, :], w["up_b"]).then_inc(w_in, DMA)
            for e in range(1, NE):
                sp.dma_start(up_w[:, e, :], w["w1"][e - 1]).then_inc(w_loaded[e], DMA)
                sp.dma_start(down_w[:, e - 1, :, :], w["w2"][e - 1].rearrange("(m p) c -> p m c", p=P)
                             ).then_inc(w_loaded[e], DMA)
                if e == 1:
                    sp.dma_start(rw2_sb[:, :, :], w["rw2"].rearrange("(m p) e -> p m e", p=P)).then_inc(w_in, DMA)
                    sp.dma_start(rb2_row[:, :], w["rb2"].rearrange("(a n) -> a n", a=1).broadcast_to([P, E])).then_inc(w_in, DMA)
                    for part in range(2):
                        sp.dma_start(b2_sb[part * E:(part + 1) * E, :], w["b2"]).then_inc(w_in, DMA)
                    sp.dma_start(gate_in[:, :], g_f.rearrange("(a n) -> a n", a=1).broadcast_to([P, 1])).then_inc(w_in, DMA)
            load(1, 1)
            with sp.Fori(0, NT // 2 - 1) as i:
                for slot in range(2):
                    r = 2 * i + slot
                    store(r, slot)
                    load(r + 2, slot)
            for r in (NT - 2, NT - 1):
                store(r, r % 2)
            for even_odd in y_stored:
                sp.wait_ge(even_odd, NT // 2 * DMA)

        @block.tensor
        def _(pe):
            def transpose_x(r):
                pe.wait_ge(xn_done, r + 1)
                if not first_tile(r):
                    pe.wait_ge(gates_t_done, r)
                for t in range(SUB):
                    mm = pe.transpose(ps_t[:, t * P:(t + 1) * P], xn[:, t, :], ident[:, :])
                mm.then_inc(xnt_ps, 1)

            def up(r, slot, e, m):
                n = (NE * r + e) * M + m
                if not (isinstance(n, int) and n < RING_H):
                    pe.wait_ge(silu_done, n - RING_H + 1)
                if first_tile(r) and m == 0:
                    pe.wait_ge(w_split, e + 1)
                cols = slice(m * P, (m + 1) * P)
                bank = ps_h[:, (e * M + m) % RING_H, :]
                pe.matmul(bank, up_hi[:, e, cols], x_lo[:, slot, :], start=True, stop=False)
                pe.matmul(bank, up_lo[:, e, cols], x_hi[:, slot, :], start=False, stop=False)
                pe.matmul(bank, up_hi[:, e, cols], x_hi[:, slot, :], start=False, stop=True).then_inc(up_ready, 1)

            def router_down(r, slot):
                pe.wait_ge(silu_done, (NE * r + 1) * M)
                for t in range(SUB):
                    for m in range(M):
                        mm = pe.matmul(ps_t[:, t * E:(t + 1) * E],
                                       hid[:, hidden_slot(slot, 0), m, t * P:(t + 1) * P],
                                       rw2_sb[:, m, :], start=(m == 0), stop=(m == M - 1))
                mm.then_inc(logits_ps, 1)

            def down(r, slot, e, m):
                pe.wait_ge(hid_lo_done, (E * r + e - 1) * M + m + 1)
                if m == 0:
                    if e > RING_O:
                        pe.wait_ge(weighed_done, E * r + e - RING_O)
                    elif not first_tile(r):
                        pe.wait_ge(weighed_done, E * r - (1 if e == 1 else 0))
                bank, hs = ps_o[:, (e - 1) % RING_O, :], hidden_slot(slot, e)
                pe.matmul(bank, down_hi[:, e - 1, m, :], hid_hi[:, hs, m, :], start=(m == 0), stop=False)
                pe.matmul(bank, down_lo[:, e - 1, m, :], hid_hi[:, hs, m, :], start=False, stop=False)
                mm = pe.matmul(bank, down_hi[:, e - 1, m, :], hid_lo[:, hs, m, :], start=False, stop=(m == M - 1))
                if m == M - 1:
                    mm.then_inc(down_ready, 1)

            def transpose_gates(r):
                pe.wait_ge(gates_lo, r + 1)
                for t in range(SUB):
                    mm = pe.transpose(ps_t[0:2 * E, t * P:(t + 1) * P],
                                      gate_parts[:, t, :, :].rearrange("p a e -> p (a e)").bitcast(F32), ident[:, :])
                mm.then_inc(gates_ps, 1)

            def spread_gates(r, e):
                if e == 1:
                    pe.wait_ge(gates_t_done, r + 1)
                    if not first_tile(r):
                        pe.wait_ge(y_done, r)
                else:
                    pe.wait_ge(spread_done, E * r + e - 1)
                pe.matmul(ps_g[:, :], select[:, e - 1, :], gates_t[:, :], start=True, stop=True).then_inc(spread_ps, 1)

            def turn_output(r):
                pe.wait_ge(added, (E - 1) * (r + 1))
                for t in range(SUB):
                    rows = slice(t * P, (t + 1) * P)
                    pe.matmul(ps_g[:, rows], acc[:, rows], ident[:, :], start=True, stop=False)
                    mm = pe.matmul(ps_g[:, rows], gates_t[:, rows].bitcast(F32), b2_sb[:, :], start=False, stop=True)
                mm.then_inc(out_ps, 1)

            def tile(r, slot, last):
                pe.wait_ge(x_lo_done, r + 1)
                for s in range(NE):
                    for m in range(M):
                        up(r, slot, s, m)
                        if s == 0 and not first_tile(r):
                            down(r - 1, 1 - slot, E, m)
                            if m == 2:
                                spread_gates(r - 1, E)
                        if s >= 2:
                            down(r, slot, s - 1, m)
                        if s == 1 and m == 2 and not first_tile(r):
                            turn_output(r - 1)
                        if s == 3 and m == 1:
                            transpose_gates(r)
                        if s == 3 and m == 3:
                            spread_gates(r, 1)
                        if s == 4 and m in (1, 3):
                            spread_gates(r, 2 if m == 1 else 3)
                        if s >= 5 and m == 2:
                            spread_gates(r, s - 1)
                        if s == 7 and m == 1 and not last:
                            transpose_x(r + 1)
                    if s == 1:
                        router_down(r, slot)

            pe.wait_ge(ident_set, 2)
            transpose_x(0)
            pe.wait_ge(w_in, N_W * DMA)
            pe.wait_ge(select_set, 1)
            tile(0, 0, False)
            tile(1, 1, False)
            with pe.Fori(1, NT // 2 - 1) as i:
                for slot in range(2):
                    tile(2 * i + slot, slot, False)
            tile(NT - 2, 0, False)
            tile(NT - 1, 1, True)
            for m in range(M):
                down(NT - 1, 1, E, m)
                if m == 2:
                    spread_gates(NT - 1, E)
            turn_output(NT - 1)

        @block.scalar
        def _(act):
            def weights_hi(e):
                act.wait_ge(w_loaded[e], (1 if e == 0 else 2) * DMA)
                a = act.activation(up_hi[:, e, :], up_w[:, e, :], ACT.Copy)
                if e > 0:
                    a = act.activation(down_hi[:, e - 1, :, :], down_w[:, e - 1, :, :], ACT.Copy)
                a.then_inc(w_hi_act, 1)

            def x_parts_hi(r, slot):
                act.wait_ge(xnt_ps, r + 1)
                if not (isinstance(r, int) and r < 2):
                    act.wait_ge(up_ready, NE * M * (r - 1))
                act.activation(x_hi[:, slot, :], ps_t[:, :], ACT.Copy).then_inc(x_hi_done, 1)

            def silu(r, slot, e, m):
                act.wait_ge(up_ready, (NE * r + e) * M + m + 1)
                if m == 0:
                    if e == 2:
                        act.wait_ge(logits_ps, r + 1)
                    elif e > 2 or not first_tile(r):
                        act.wait_ge(down_ready, E * r + (e - 1 if e < 2 else e - 2))
                act.activation(hid[:, hidden_slot(slot, e), m, :], ps_h[:, (e * M + m) % RING_H, :],
                               ACT.Silu, bias=up_b[:, e, m:m + 1]).then_inc(silu_done, 1)

            def hidden_hi(r, slot, e, m):
                act.wait_ge(silu_done, (NE * r + e) * M + m + 1)
                hs = hidden_slot(slot, e)
                act.activation(hid_hi[:, hs, m, :], hid[:, hs, m, :], ACT.Copy).then_inc(hid_hi_done, 1)

            def copy_gates_t(r):
                act.wait_ge(gates_ps, r + 1)
                if not first_tile(r):
                    act.wait_ge(out_ps, r)
                act.activation(gates_t[:, :], ps_t[0:2 * E, :], ACT.Copy).then_inc(gates_t_done, 1)

            def copy_spread(r, e):
                n = E * r + e
                act.wait_ge(spread_ps, n)
                if not (isinstance(n, int) and n < 3):
                    act.wait_ge(weighed_done, n - 2)
                act.activation(spread[:, e % 2, :], ps_g[:, :], ACT.Copy).then_inc(spread_done, 1)

            def tile(r, slot, last):
                for s in range(NE):
                    for m in range(M):
                        silu(r, slot, s, m)
                        if s == 0 and m == 0 and not first_tile(r):
                            hidden_hi(r - 1, 1 - slot, E, M - 1)
                        if s >= 2 and m == 0:
                            hidden_hi(r, slot, s - 1, M - 1)
                        if s >= 1 and m > 0:
                            hidden_hi(r, slot, s, m - 1)
                        if s == 0 and m == 3 and not first_tile(r):
                            copy_spread(r - 1, E)
                        if s == 2 and m == 1:
                            act.wait_ge(diff_done, r + 1)
                            act.activation(half_tanh[:, :], diff[:, :], ACT.Tanh, scale=0.5).then_inc(tanh_done, 1)
                        if s == 3 and m == 2:
                            copy_gates_t(r)
                        if s == 4 and m in (0, 2):
                            copy_spread(r, 1 if m == 0 else 2)
                        if s == 5 and m == 0:
                            copy_spread(r, 3)
                        if s >= 5 and m == 3:
                            copy_spread(r, s - 1)
                        if s == 7 and m == 2 and not last:
                            x_parts_hi(r + 1, 1 - slot)

            weights_hi(0)
            weights_hi(1)
            x_parts_hi(0, 0)
            act.wait_ge(w_in, N_W * DMA)
            act.activation(gate[:, :], gate_in[:, :], ACT.Tanh).then_inc(gate_set, 1)
            tile(0, 0, False)
            tile(1, 1, False)
            with act.Fori(1, NT // 2 - 1) as i:
                for slot in range(2):
                    tile(2 * i + slot, slot, False)
            tile(NT - 2, 0, False)
            tile(NT - 1, 1, True)
            hidden_hi(NT - 1, 1, E, M - 1)
            copy_spread(NT - 1, E)

        @block.vector
        def _(dve):
            def weights_lo(e):
                if e < 2:
                    dve.wait_ge(w_hi_act, e + 1)
                else:
                    dve.wait_ge(w_hi_pool, e - 1)
                a = nc.vector.tensor_tensor(up_lo[:, e, :], up_w[:, e, :], up_hi[:, e, :].bitcast(F32), ALU.subtract)
                if e > 0:
                    a = nc.vector.tensor_tensor(down_lo[:, e - 1, :, :], down_w[:, e - 1, :, :],
                                                down_hi[:, e - 1, :, :].bitcast(F32), ALU.subtract)
                a.then_inc(w_split, 1)

            def row_stats(pair, slot):
                r = 2 * pair + slot
                dve.wait_ge(x_loaded[slot], (pair + 1) * DMA)
                for t in range(SUB):
                    a = nc.vector.bn_stats(stats[:, t, :], x_in[:, slot, t, :])
                a.then_inc(stats_done, 1)

            def join(r):
                dve.wait_ge(stats_done, r + 1)
                join_stats(nc, dve, stats, joined, mean, var_eps, joined_1, joined_2, eps_done, r)

            def normalise(r, slot):
                dve.wait_ge(rstd_done, r + 1)
                if not first_tile(r):
                    dve.wait_ge(xnt_ps, r)
                for t in range(SUB):
                    a = nc.vector.tensor_scalar(xn[:, t, :], x_in[:, slot, t, :], mean[:, t:t + 1], rstd[:, t:t + 1],
                                                ALU.subtract, ALU.mult)
                a.then_inc(xn_done, 1)

            def x_parts_lo(r, slot):
                dve.wait_ge(x_hi_done, r + 1)
                nc.vector.tensor_tensor(x_lo[:, slot, :], ps_t[:, :], x_hi[:, slot, :].bitcast(F32), ALU.subtract
                                        ).then_inc(x_lo_done, 1)

            def hidden_lo(r, slot, e, m):
                dve.wait_ge(hid_hi_done, (E * r + e - 1) * M + m + 1)
                hs = hidden_slot(slot, e)
                nc.vector.tensor_tensor(hid_lo[:, hs, m, :], hid[:, hs, m, :], hid_hi[:, hs, m, :].bitcast(F32),
                                        ALU.subtract).then_inc(hid_lo_done, 1)

            def add_expert(r, e):
                n = E * r + e
                dve.wait_ge(down_ready, n)
                dve.wait_ge(spread_done, n)
                if e == 1:
                    nc.vector.tensor_tensor(acc[:, :], ps_o[:, 0, :], spread[:, e % 2, :], ALU.mult
                                            ).then_inc(weighed_done, 1)
                else:
                    nc.vector.tensor_tensor(weighed[:, e % 2, :], ps_o[:, (e - 1) % RING_O, :], spread[:, e % 2, :],
                                            ALU.mult).then_inc(weighed_done, 1)
                    dve.wait_ge(weighed_done, n)
                    if e > 2:
                        dve.wait_ge(added, (E - 1) * r + e - 2)
                    nc.vector.tensor_tensor(acc[:, :], acc[:, :], weighed[:, e % 2, :], ALU.add).then_inc(added, 1)

            def best_two(r):
                dve.wait_ge(logits_ps, r + 1)
                nc.vector.tensor_tensor(logits[:, :, :], ps_t[:, 0:SUB * E].rearrange("p (t e) -> p t e", e=E),
                                        rb2_row[:, :].rearrange("p (a e) -> p a e", a=1).broadcast_to([P, SUB, E]),
                                        ALU.add).then_inc(logits_done, 1)
                dve.wait_ge(small_set, 1)
                dve.wait_ge(logits_done, r + 1)
                for t in range(SUB):
                    a = nc.vector.max(best[:, t, :], logits[:, t, :])
                a.then_inc(best_done, 1)
                dve.wait_ge(best_done, r + 1)
                nc.vector.tensor_tensor(diff[:, :], best[:, :, 0], best[:, :, 1], ALU.subtract).then_inc(diff_done, 1)
                for t in range(SUB):
                    a = nc.vector.max_index(best_at[:, t, :], best[:, t, :], logits[:, t, :])
                a.then_inc(at_done, 1)

            def weigh_two(r):
                dve.wait_ge(at_done, r + 1)
                nc.vector.tensor_copy(best_no[:, :, :], best_at[:, :, 0:2]).then_inc(pick_done, 1)
                dve.wait_ge(tanh_done, r + 1)
                nc.vector.tensor_scalar(prob[:, 0, :], half_tanh[:, :], 0.5, 0.5, ALU.mult, ALU.add)
                nc.vector.tensor_scalar(prob[:, 1, :], half_tanh[:, :], -0.5, 0.5, ALU.mult, ALU.add).then_inc(prob_done, 1)
                dve.wait_ge(pick_done, r + 1)
                dve.wait_ge(prob_done, r + 1)
                for k in range(2):
                    for t in range(SUB):
                        a = nc.vector.tensor_scalar(pick[:, k, t, :], expert_no[:, :], best_no[:, t, k:k + 1],
                                                    prob[:, k, t:t + 1], ALU.is_equal, ALU.mult)
                a.then_inc(picked, 1)
                dve.wait_ge(picked, r + 1)
                nc.vector.tensor_tensor(gates[:, :, :], pick[:, 0, :, :], pick[:, 1, :, :], ALU.add).then_inc(gates_done, 1)
                dve.wait_ge(gates_done, r + 1)
                if not first_tile(r):
                    dve.wait_ge(gates_ps, r)
                nc.vector.tensor_copy(gate_parts[:, :, 0, :], gates[:, :, :]).then_inc(gates_hi, 1)
                dve.wait_ge(gates_hi, r + 1)
                nc.vector.tensor_tensor(gate_parts[:, :, 1, :], gates[:, :, :], gate_parts[:, :, 0, :].bitcast(F32),
                                        ALU.subtract).then_inc(gates_lo, 1)

            def finish(pair, slot):
                dve.wait_ge(out_ps, 2 * pair + slot + 1)
                if not (isinstance(pair, int) and pair == 0):
                    dve.wait_ge(y_stored[slot], pair * DMA)
                nc.vector.scalar_tensor_tensor(y[:, slot, :, :], ps_g[:, :].rearrange("p (t c) -> p t c", c=C),
                                               gate[:, 0:1], x_in[:, slot, :, :], ALU.mult, ALU.add).then_inc(y_done, 1)

            def tile(pair, slot, last):
                r = 2 * pair + slot
                first = first_tile(r)
                for s in range(NE):
                    if s < 2 and not first:
                        add_expert(r - 1, E - 1 + s)
                    if s == 2:
                        if not first:
                            finish(pair + slot - 1, 1 - slot)
                        best_two(r)
                    if s == 4:
                        add_expert(r, 1)
                    if s >= 5:
                        add_expert(r, s - 2)
                    for m in range(M):
                        if s == 0 and m == 0 and not first:
                            hidden_lo(r - 1, 1 - slot, E, M - 1)
                        if s >= 2 and m == 0:
                            hidden_lo(r, slot, s - 1, M - 1)
                        if s >= 1 and m > 0:
                            hidden_lo(r, slot, s, m - 1)
                        if s == 2 and m == 1:
                            weigh_two(r)
                        if s == 4 and m == 2:
                            add_expert(r, 2)
                        if not last:
                            if s == 5 and m == 1:
                                row_stats(pair + slot, 1 - slot)
                            if s == 5 and m == 3:
                                join(r + 1)
                            if s == 6 and m == 1:
                                normalise(r + 1, 1 - slot)
                            if s == 8 and m == 0:
                                x_parts_lo(r + 1, 1 - slot)
                        if first and m == 1 and s + 2 < NE:
                            weights_lo(s + 2)

            for e in range(E):
                a = nc.vector.memset(expert_no[:, e:e + 1], float(e))
            a.then_inc(small_set, 1)
            row_stats(0, 0)
            join(0)
            normalise(0, 0)
            dve.wait_ge(ident_set, 2)
            nc.vector.tensor_tensor(select[:, :, :],
                                    ident[0:2 * E, 0:E].rearrange("k (e a) -> k e a", a=1).broadcast_to([2 * E, E, P]),
                                    ident[0:2 * E, E:2 * E].rearrange("k (e a) -> k e a", a=1).broadcast_to([2 * E, E, P]),
                                    ALU.add).then_inc(select_set, 1)
            weights_lo(0)
            x_parts_lo(0, 0)
            weights_lo(1)
            dve.wait_ge(w_in, N_W * DMA)
            dve.wait_ge(gate_set, 1)
            tile(0, 0, False)
            tile(0, 1, False)
            with dve.Fori(1, NT // 2 - 1) as i:
                for slot in range(2):
                    tile(i, slot, False)
            tile(NT // 2 - 1, 0, False)
            tile(NT // 2 - 1, 1, True)
            add_expert(NT - 1, E - 1)
            hidden_lo(NT - 1, 1, E, M - 1)
            add_expert(NT - 1, E)
            finish(NT // 2 - 1, 1)

        @block.gpsimd
        def _(pool):
            nc.gpsimd.memset(minus_half[:, :], -0.5)
            nc.gpsimd.memset(ident[:, :], 0.0).then_inc(ident_set, 1)
            pool.wait_ge(ident_set, 1)
            nc.gpsimd.affine_select(out=ident[:, :], in_=ident[:, :], compare_op=ALU.not_equal, fill=1.0, base=0,
                                    pattern=[[-1, P]], channel_multiplier=1).then_inc(ident_set, 1)

            def rstd_of(r):
                pool.wait_ge(eps_done, r + 1)
                nc.gpsimd.tensor_tensor(rstd[:, :], var_eps[:, :], minus_half[:, :], ALU.pow).then_inc(rstd_done, 1)

            rstd_of(0)
            for e in range(2, NE):
                pool.wait_ge(w_loaded[e], 2 * DMA)
                nc.gpsimd.tensor_copy(up_hi[:, e, :], up_w[:, e, :])
                nc.gpsimd.tensor_copy(down_hi[:, e - 1, :, :], down_w[:, e - 1, :, :]).then_inc(w_hi_pool, 1)
            with pool.Fori(1, NT) as r:
                rstd_of(r)


def build(nc, a, out):
    B, _, _ = a["x"].shape
    TC = a["ctx_t"].shape[2]
    scratch = {
        "q": nc.dram_tensor("q_rows", [B, 2, H, 2, 2, D, T], F32, kind="Internal").ap(),
        "kself": nc.dram_tensor("kself_rows", [B, H, 2, 2, D, T], F32, kind="Internal").ap(),
        "kx": nc.dram_tensor("kx_rows", [B, H, 2, 2, D, TC], F32, kind="Internal").ap(),
        "y": nc.dram_tensor("y_rows", [B, 2, H, VW, T], F32, kind="Internal").ap(),
    }
    x1 = nc.dram_tensor("x1", [B, T, C], F32, kind="Internal").ap()
    att = {n: a[n] for n in ("Wq", "Wk", "Wv", "Wcq", "Wp", "Wck", "Wcv", "qk_bias", "bcv", "bv", "bp")}
    attention(nc, a["x"], a["ctx_t"], a["g_xattn"], att, x1, scratch)
    ffn = {n: a[n] for n in ("rw1", "rw2", "rb2", "w1", "w2", "b2", "up_b")}
    experts(nc, x1.rearrange("b t c -> (b t) c"), a["g_ffn"], ffn, out.rearrange("b t c -> (b t) c"))


def kernel(**inputs):
    import numpy as np
    import concourse.bacc as bacc
    from concourse import mybir as _mybir
    from concourse.bass_utils import run_bass_kernel_spmd

    i = {n.replace("L0_xattn_", "").replace("L0_ffn_", ""): np.asarray(v) for n, v in inputs.items()}
    ctx = i.pop("ctx_512")
    i["ctx_t"] = np.concatenate([ctx.transpose(0, 2, 1), np.ones((ctx.shape[0], 1, ctx.shape[1]), ctx.dtype)], 1)
    i["Wck"] = np.concatenate([i["Wck"], i.pop("bck")[None, :]], 0)
    i["qk_bias"] = np.stack([i.pop("bq"), i.pop("bk"), i.pop("bcq")], 1)
    up_b = np.concatenate([i.pop("rb1")[None], i.pop("b1")], 0)
    i["up_b"] = up_b.reshape(up_b.shape[0], -1, P).transpose(2, 0, 1)

    nc = bacc.Bacc("TRN2", target_bir_lowering=False, num_devices=1)
    arrays, aps = {}, {}
    for n, v in i.items():
        v = np.ascontiguousarray(v)
        arrays[f"in_{n}"] = v
        aps[n] = nc.dram_tensor(f"in_{n}", v.shape, _mybir.dt.from_np(v.dtype), kind="ExternalInput").ap()
    out = nc.dram_tensor("out", i["x"].shape, _mybir.dt.from_np(i["x"].dtype), kind="ExternalOutput").ap()
    build(nc, aps, out)
    r = run_bass_kernel_spmd(nc, [arrays], core_ids=[0])
    return r.results[0]["out"]
```

```python
from contextlib import ExitStack

import concourse.bass as bass
from concourse import mybir
from concourse.alu_op_type import AluOpType as ALU

F32 = mybir.dt.float32
F32R = mybir.dt.float32r
BF16 = mybir.dt.bfloat16
U32 = mybir.dt.uint32
ACT = mybir.ActivationFunctionType
AX_X = mybir.AxisListType.X

P = 128
T = 256
C = 128
H = 16
D = C // H
HEAD_ROWS = 4 * D
HEADS_IN_TILE = 3
SHIFT = HEADS_IN_TILE * HEAD_ROWS
ROWS = SHIFT + 2
HALF = H // 2
TILES = 3
GROUP = 4
GROUPS = H // GROUP
VW = 2 * D
TILE_ROWS = 512
EPS = 1e-5
NEG = -1.0e37
DMA = 16
LEAD = 5


def join_stats(nc, dve, stats, joined, mean, var_eps, joined_1, joined_2, eps_done, n):
    nc.vector.tensor_tensor(joined[:, :, 0:2], stats[:, :, 1:3], stats[:, :, 4:6], ALU.add)
    nc.vector.tensor_tensor(joined[:, :, 2], stats[:, :, 1], stats[:, :, 4], ALU.subtract).then_inc(joined_1, 1)
    dve.wait_ge(joined_1, n + 1)
    nc.vector.tensor_scalar(mean[:, :], joined[:, :, 0], 0.5, None, ALU.mult)
    nc.vector.tensor_scalar(joined[:, :, 3], joined[:, :, 1], 1.0 / C, EPS, ALU.mult, ALU.add)
    nc.vector.scalar_tensor_tensor(joined[:, :, 4], joined[:, :, 2], 0.25, joined[:, :, 2], ALU.mult,
                                   ALU.mult).then_inc(joined_2, 1)
    dve.wait_ge(joined_2, n + 1)
    nc.vector.tensor_tensor(var_eps[:, :], joined[:, :, 3], joined[:, :, 4], ALU.add).then_inc(eps_done, 1)


def known(eng, count):
    if not isinstance(count, int):
        eng.lower_val(count)
    return count


class Shared:

    def __init__(self, nc, ctx, hidden, tile_rows):
        def sb(name, shape, dt=F32):
            return ctx.enter_context(nc.sbuf_tensor(name, shape, dt))

        def sem(name):
            return ctx.enter_context(nc.semaphore(name))

        sub = tile_rows // P
        self.started = sem("started")
        self.ident = sb("ident", [P, P])
        self.ps_m = ctx.enter_context(nc.psum_tensor("ps_m", [P, 512], F32))

        self.wp_sb, self.bp_row, self.gate = sb("wp_sb", [P, C]), sb("bp_row", [P, C]), sb("gate", [P, 1])
        self.y_raw = sb("y_raw", [P, 2, 2, T])
        self.y_in = sb("y_in", [P, 2, 2, T])
        self.y_rec, self.y_nrm = sb("y_rec", [P, 2, T]), sb("y_nrm", [P, 2, T])
        self.y_sum = sb("y_sum", [P, T])
        self.x_res, self.att, self.x_new = sb("x_res", [P, 2, C]), sb("att", [P, 2, C]), sb("x_new", [P, 2, C])
        self.y_stored = [sem("y_stored_even"), sem("y_stored_odd")]
        self.y_loaded = sem("y_loaded")
        self.xres_loaded = sem("xres_loaded")
        self.rec_done = sem("rec_done")
        self.nrm_done = sem("nrm_done")
        self.ysum_done = sem("ysum_done")
        self.out_ps = sem("out_ps")
        self.att_done = sem("att_done")
        self.x1_done = sem("x1_done")
        self.x1_stored = sem("x1_stored")

        self.router_w = sb("router_w", [P, hidden])
        self.rows_in, self.rows_n = sb("rows_in", [P, 2, sub, C]), sb("rows_n", [P, sub, C])
        self.stats, self.joined = sb("rows_stats", [P, sub, 6]), sb("rows_joined", [P, sub, 6])
        self.mean, self.var_eps, self.rstd = sb("rows_mean", [P, sub]), sb("rows_var_eps", [P, sub]), sb("rows_rstd", [P, sub])
        self.minus_half = sb("rows_minus_half", [P, sub])
        self.router_loaded = sem("router_loaded")
        self.rows_loaded = [sem("rows_loaded_even"), sem("rows_loaded_odd")]
        self.stats_done, self.eps_done = sem("rows_stats_done"), sem("rows_eps_done")
        self.joined_1, self.joined_2 = sem("rows_joined_1"), sem("rows_joined_2")
        self.rstd_done, self.rows_n_done = sem("rows_rstd_done"), sem("rows_n_done")
        self.turned = sem("rows_turned")


def load_y(sp, o, ys, x, b):
    stored = known(sp, (b + 1) * (GROUPS // 2) * GROUP * DMA)
    sp.wait_ge(o.started, 1)
    for even_odd in o.y_stored:
        sp.wait_ge(even_odd, stored)
    for st in range(2):
        for part in range(2):
            sp.dma_start(o.y_in[:, st, part, :],
                         ys[b, st, :, part * D:(part + 1) * D, :]
                         ).then_inc(o.y_loaded, DMA)
    sp.dma_start(o.x_res[:, :, :], x[b, :, :].rearrange("(t p) c -> p t c", p=P)).then_inc(o.xres_loaded, DMA)


def store_x1(sp, o, x1, b):
    sp.wait_ge(o.started, 1)
    sp.wait_ge(o.x1_done, b + 1)
    sp.dma_start(x1[b, :, :].rearrange("(t p) c -> p t c", p=P), o.x_new[:, :, :]).then_inc(o.x1_stored, DMA)


def reciprocals(nc, dve, o, b):
    dve.wait_ge(o.y_loaded, (b + 1) * 4 * DMA)
    if not (isinstance(b, int) and b == 0):
        dve.wait_ge(o.nrm_done, b)
    nc.vector.reciprocal(o.y_rec[:, :, :], o.y_in[:, :, 1, :]).then_inc(o.rec_done, 1)


def normalise(nc, pool, o, b):
    pool.wait_ge(o.rec_done, b + 1)
    nc.gpsimd.tensor_tensor(o.y_nrm[:, :, :], o.y_in[:, :, 0, :], o.y_rec[:, :, :], ALU.mult).then_inc(o.nrm_done, 1)
    pool.wait_ge(o.nrm_done, b + 1)
    if not (isinstance(b, int) and b == 0):
        pool.wait_ge(o.out_ps, b)
    nc.gpsimd.tensor_tensor(o.y_sum[:, :], o.y_nrm[:, 0, :], o.y_nrm[:, 1, :], ALU.add).then_inc(o.ysum_done, 1)


def out_job(pe, o, b):
    pe.wait_ge(o.ysum_done, b + 1)
    for t in range(2):
        mm = pe.matmul(o.ps_m[:, t * C:(t + 1) * C], o.y_sum[:, t * P:(t + 1) * P], o.wp_sb[:, :],
                       start=True, stop=True)
    mm.then_inc(o.out_ps, 1)


def residual(nc, dve, o, b):
    dve.wait_ge(o.out_ps, b + 1)
    dve.wait_ge(o.xres_loaded, (b + 1) * DMA)
    nc.vector.tensor_tensor(o.att[:, :, :], o.ps_m[:, 0:2 * C].rearrange("p (a c) -> p a c", c=C),
                            o.bp_row[:, :].rearrange("p (a c) -> p a c", a=1).broadcast_to([P, 2, C]),
                            ALU.add).then_inc(o.att_done, 1)
    dve.wait_ge(o.att_done, b + 1)
    if not (isinstance(b, int) and b == 0):
        dve.wait_ge(o.x1_stored, b * DMA)
    nc.vector.scalar_tensor_tensor(o.x_new[:, :, :], o.att[:, :, :], o.gate[:, 0:1], o.x_res[:, :, :],
                                   ALU.mult, ALU.add).then_inc(o.x1_done, 1)


def load_rows(sp, o, x1_rows, r, slot):
    TR = TILE_ROWS
    sp.dma_start(o.rows_in[:, slot, :, :], x1_rows[bass.ds(r * TR, TR), :].rearrange("(t p) c -> p t c", p=P)
                 ).then_inc(o.rows_loaded[slot], DMA)


def row_stats(nc, dve, o, pair, slot):
    dve.wait_ge(o.rows_loaded[slot], (pair + 1) * DMA)
    for t in range(o.rows_in.shape[2]):
        a = nc.vector.bn_stats(o.stats[:, t, :], o.rows_in[:, slot, t, :])
    a.then_inc(o.stats_done, 1)


def join_rows(nc, dve, o, r):
    dve.wait_ge(o.stats_done, r + 1)
    join_stats(nc, dve, o.stats, o.joined, o.mean, o.var_eps, o.joined_1, o.joined_2, o.eps_done, r)


def rstd_of_rows(nc, pool, o, r):
    pool.wait_ge(o.eps_done, r + 1)
    nc.gpsimd.tensor_tensor(o.rstd[:, :], o.var_eps[:, :], o.minus_half[:, :], ALU.pow).then_inc(o.rstd_done, 1)


def normalise_rows(nc, dve, o, r, slot):
    dve.wait_ge(o.rstd_done, r + 1)
    if not (isinstance(r, int) and r == 0):
        dve.wait_ge(o.turned, r)
    for t in range(o.rows_in.shape[2]):
        a = nc.vector.tensor_scalar(o.rows_n[:, t, :], o.rows_in[:, slot, t, :], o.mean[:, t:t + 1], o.rstd[:, t:t + 1],
                                    ALU.subtract, ALU.mult)
    a.then_inc(o.rows_n_done, 1)


def attention(nc, x, ctx_t, g_x, w, x1, scratch, o):
    B = x.shape[0]
    TC = ctx_t.shape[2]
    CK = ctx_t.shape[1]
    NCH = -(-TC // P)
    TAIL = TC - (NCH - 1) * P
    STEPS = NCH + 2
    BSTEPS = STEPS * GROUPS
    NFULL = TC // 512
    REST = TC - NFULL * 512
    REST_W = REST + REST % 2
    SCALE = float(D) ** -0.5
    BANKS = 3
    assert BSTEPS % BANKS == 0 and GROUP * REST_W <= 512

    UNITS = [("cross", qt, i, kc) for qt in range(2) for i in range(GROUP) for kc in range(NFULL)]
    UNITS += [("cross_rest", qt, 0, 0) for qt in range(2)]
    UNITS += [("self", qt, i, 0) for qt in range(2) for i in (0, 2)]
    NU = len(UNITS)
    assert NU % BANKS == 0

    def units_at(pos):
        return range(NU * pos // STEPS, NU * (pos + 1) // STEPS)

    def target(j):
        s, pos = divmod(j + LEAD, STEPS)
        ahead, g = divmod(1 + s, GROUPS)
        return ahead, g, pos

    def in_half(g, i):
        h8 = GROUP * (g % 2) + i
        return g // 2, h8, h8 // HEADS_IN_TILE, h8 % HEADS_IN_TILE

    x1_rows = x1.rearrange("b t c -> (b t) c")
    qs, kself_s, kx_s, ys = scratch["q"], scratch["kself"], scratch["kx"], scratch["y"]
    Wq, Wk, Wv, Wcq, Wp = w["Wq"], w["Wk"], w["Wv"], w["Wcq"], w["Wp"]

    with ExitStack() as ctx:
        def sb(name, shape, dt=F32):
            return ctx.enter_context(nc.sbuf_tensor(name, shape, dt))

        def psum(name, shape):
            return ctx.enter_context(nc.psum_tensor(name, shape, F32))

        def sem(name):
            return ctx.enter_context(nc.semaphore(name))

        wq_sb, wk_sb, wv_sb, wcq_sb = (sb(f"{n}_sb", [P, C]) for n in ("wq", "wk", "wv", "wcq"))
        wck_sb, wcv_sb = sb("wck_sb", [CK, C]), sb("wcv_sb", [CK - 1, C])
        bias_sb = sb("bias_sb", [P, 3])
        v_bias = sb("v_bias", [P, 2, C])
        gate_in = sb("gate_in", [P, 1])
        ident_b = sb("ident_b", [P, P], BF16)
        mask_q = sb("mask_q", [P, 2, T], BF16)
        mask_k = sb("mask_k", [P, 2, T], BF16)
        minus_half = sb("minus_half", [P, 2])

        kx = [sb(f"kx{i}", [ROWS, TILES, TC], F32R) for i in range(2)]
        kself = [sb(f"kself{i}", [ROWS, TILES, T], F32R) for i in range(2)]
        qx = [sb(f"qx{i}", [ROWS, HALF, T], F32R) for i in range(2)]
        qself = [sb(f"qself{i}", [ROWS, HALF, T], F32R) for i in range(2)]
        v_all = sb("v_all", [P, STEPS, C])
        v_half = [sb(f"v_half{i}", [P, STEPS, HALF, VW]) for i in range(2)]

        x_in, xn = sb("x_in", [P, 2, C]), sb("xn", [P, 2, C])
        xn_t = sb("xn_t", [P, T])
        stats, joined, mean = sb("stats", [P, 2, 6]), sb("joined", [P, 2, 6]), sb("mean", [P, 2])
        var_eps, rstd = sb("var_eps", [P, 2]), sb("rstd", [P, 2])
        ctx_in = sb("ctx_in", [CK, TC])
        parts = sb("parts", [P, 3, 2, T], F32R)
        ck_parts = sb("ck_parts", [P, 2, TC], F32R)
        max_x = sb("max_x", [P, GROUP, 2, NFULL + 1])
        max_s = sb("max_s", [P, GROUP, 2])
        neg_max = sb("neg_max", [P, 2, GROUP * 2])
        shift = sb("shift", [P, 2, 2 * GROUP * 2], F32R)
        shift_t = sb("shift_t", [4 * GROUP * 2, P], F32R)
        probs = sb("probs", [P, 3, GROUP * T])

        ps_s = psum("ps_s", [P, BANKS, 2, T])
        ps_a = psum("ps_a", [P, BANKS, 512])
        ps_y = psum("ps_y", [P, 2, T])

        wck_in = sem("wck_in")
        consts_in = sem("consts_in")
        zeroed = sem("zeroed")
        ones_set = sem("ones_set")
        half1_zeroed, half1_set = sem("half1_zeroed"), sem("half1_set")
        masks_zero = sem("masks_zero")
        masks_set = sem("masks_set")
        gate_set = sem("gate_set")
        x_loaded = sem("x_loaded")
        ctx_loaded = sem("ctx_loaded")
        stats_done = sem("stats_done")
        joined_1, joined_2 = sem("joined_1"), sem("joined_2")
        eps_done = sem("eps_done")
        rstd_done = sem("rstd_done")
        xn_done = sem("xn_done")
        xnt_ps = sem("xnt_ps")
        xnt_done = sem("xnt_done")
        qk_ps = sem("qk_ps")
        qk_hi = sem("qk_hi")
        qk_lo = sem("qk_lo")
        cq_ps = sem("cq_ps")
        cq_hi = sem("cq_hi")
        cq_lo = sem("cq_lo")
        ck_ps = sem("ck_ps")
        ck_hi = sem("ck_hi")
        ck_lo = sem("ck_lo")
        cv_ps = sem("cv_ps")
        cv_done = sem("cv_done")
        v_ps = sem("v_ps")
        v_done = sem("v_done")
        qk_stored = sem("qk_stored")
        kx_stored = sem("kx_stored")
        half_in = [sem("half0_in"), sem("half1_in")]
        vhalf_done = [sem("vhalf0_done"), sem("vhalf1_done")]
        unit_ready = sem("unit_ready")
        unit_reduced = sem("unit_reduced")
        neg_done = sem("neg_done")
        shift_hi = sem("shift_hi")
        shift_lo = sem("shift_lo")
        shift_ps = sem("shift_ps")
        shift_t_done = sem("shift_t_done")
        shift_in = sem("shift_in")
        scores_ready = sem("scores_ready")
        exp_done = sem("exp_done")
        pv_done = sem("pv_done")
        y_copied = sem("y_copied")

        HALF_DMAS = 3 + 2 + 2 * HEADS_IN_TILE
        NCK = -(-TC // 512)
        NCV = -(-NCH // 4)
        N_CONST = 11

        J_LN, J_XN, J_XT, J_QK, J_CQ, J_REC, J_OUT = 2, 3, 4, 6, 8, 8, 12
        J_CK = [14, 16, 18, 20][:NCK]
        J_CV = [22, 24, 27, 29][:NCV]
        J_V = 31
        J_SHIFT = [STEPS * g + 10 for g in range(GROUPS)]

        def ck_bank(c, n):
            if not (isinstance(c, int) and c == 0):
                return o.ps_m
            return ps_s[:, n, :, :].rearrange("p a n -> p (a n)") if n < BANKS else ps_a[:, n - BANKS, :]

        block = ctx.enter_context(nc.Block())

        @block.sync
        def _(sp):
            def load_x(c):
                sp.wait_ge(masks_zero, 1)
                if not (isinstance(c, int) and c == 0):
                    sp.wait_ge(xn_done, c)
                sp.dma_start(x_in[:, :, :], x[c, :, :].rearrange("(t p) c -> p t c", p=P)).then_inc(x_loaded, DMA)
                sp.wait_ge(masks_zero, 1)
                if not (isinstance(c, int) and c == 0):
                    sp.wait_ge(cv_ps, c * NCV)
                sp.dma_start(ctx_in[:, :], ctx_t[c, :, :]).then_inc(ctx_loaded, DMA)

            def store_q_parts(c):
                sp.wait_ge(masks_zero, 1)
                sp.wait_ge(qk_lo, c + 1)
                for a in range(2):
                    for b in range(2):
                        sp.dma_start(qs[c, 0, :, a, b, :, :], parts[:, 0, a, :].bitcast(F32)).then_inc(qk_stored, DMA)
                        sp.dma_start(kself_s[c, :, a, b, :, :], parts[:, 1, b, :].bitcast(F32)).then_inc(qk_stored, DMA)
                sp.wait_ge(masks_zero, 1)
                sp.wait_ge(cq_lo, c + 1)
                for a in range(2):
                    for b in range(2):
                        sp.dma_start(qs[c, 1, :, a, b, :, :], parts[:, 2, a, :].bitcast(F32)).then_inc(qk_stored, DMA)

            def store_k_parts(c):
                sp.wait_ge(masks_zero, 1)
                sp.wait_ge(ck_lo, (c + 1) * NCK)
                for a in range(2):
                    for b in range(2):
                        sp.dma_start(kx_s[c, :, a, b, :, :], ck_parts[:, b, :].bitcast(F32)).then_inc(kx_stored, DMA)

            def load_half(c, half):
                q_rows, k_rows = known(sp, (c + 1) * 12 * DMA), known(sp, (c + 1) * 4 * DMA)
                read = known(sp, 2 * (c - 1) * BSTEPS + (half + 1) * BSTEPS)
                sp.wait_ge(masks_zero, 1)
                sp.wait_ge(qk_stored, q_rows)
                sp.wait_ge(kx_stored, k_rows)
                if not (isinstance(c, int) and c == 0):
                    sp.wait_ge(scores_ready, read)
                h0 = half * HALF
                kxr = kx_s[c, h0:h0 + HALF].rearrange("h a b d n -> (h a b d) n")
                ksr = kself_s[c, h0:h0 + HALF].rearrange("h a b d n -> (h a b d) n")
                for g in range(TILES):
                    r0, r1 = g * SHIFT, min((g + 1) * SHIFT, HALF * HEAD_ROWS)
                    sp.dma_start(kx[half][0:r1 - r0, g, :].bitcast(F32), kxr[r0:r1, :]).then_inc(half_in[half], DMA)
                sp.dma_start(kself[half][0:SHIFT, 0:2, :].bitcast(F32),
                             ksr[0:2 * SHIFT, :].rearrange("(g r) n -> r g n", g=2)).then_inc(half_in[half], DMA)
                sp.dma_start(kself[half][0:HALF * HEAD_ROWS - 2 * SHIFT, 2, :].bitcast(F32),
                             ksr[2 * SHIFT:, :]).then_inc(half_in[half], DMA)
                for st, dst in enumerate((qself[half], qx[half])):
                    src = qs[c, st, h0:h0 + HALF].rearrange("h a b d n -> (a b d) h n")
                    for q in range(HEADS_IN_TILE):
                        sp.dma_start(dst[q * HEAD_ROWS:(q + 1) * HEAD_ROWS, q:HALF:HEADS_IN_TILE, :].bitcast(F32),
                                     src[:, q:HALF:HEADS_IN_TILE, :]).then_inc(half_in[half], DMA)

            def store_shift(s, g):
                sp.wait_ge(shift_t_done, s + 1)
                n = GROUP * 2
                for part in range(2):
                    for st, dst in enumerate((qx[g // 2], qself[g // 2])):
                        r = (part * 2 + st) * n
                        h0 = GROUP * (g % 2)
                        sp.dma_start(dst[SHIFT + part:SHIFT + part + 1, h0:h0 + GROUP, :].bitcast(F32),
                                     shift_t[r:r + n, :].bitcast(F32)).then_inc(shift_in, DMA)

            def store_y(b, g):
                copied = known(sp, GROUPS * b + g + 1)
                sp.wait_ge(masks_zero, 1)
                sp.wait_ge(y_copied, copied)
                for i in range(GROUP):
                    sp.dma_start(ys[b, :, GROUP * g + i, :, :].rearrange("s r q -> r s q"),
                                 o.y_raw[32 * i:32 * i + VW, g % 2, :, :]).then_inc(o.y_stored[g % 2], DMA)

            def element(b, first, last):
                if not last:
                    load_x(b + 1)
                if not first:
                    load_half(b, 1)
                    store_y(b - 1, GROUPS - 1)
                    load_y(sp, o, ys, x, b - 1)
                if not last:
                    store_q_parts(b + 1)
                store_shift(GROUPS * b + 1, 1)
                if not first:
                    store_x1(sp, o, x1, b - 1)
                store_y(b, 0)
                if not last:
                    store_k_parts(b + 1)
                store_shift(GROUPS * b + 2, 2)
                store_y(b, 1)
                if not last:
                    load_half(b + 1, 0)
                store_shift(GROUPS * b + 3, 3)
                store_y(b, 2)
                if not last:
                    store_shift(GROUPS * b + 4, 0)

            sp.dma_start(wck_sb[:, :], w["Wck"]).then_inc(wck_in, DMA)
            load_x(0)
            for dst, src in ((wq_sb, Wq), (wk_sb, Wk), (bias_sb, w["qk_bias"]), (wcq_sb, Wcq), (wv_sb, Wv),
                             (wcv_sb, w["Wcv"]), (o.wp_sb, Wp)):
                sp.dma_start(dst[:, :], src).then_inc(consts_in, DMA)
            for st, n in enumerate(("bcv", "bv")):
                sp.dma_start(v_bias[:, st, :], w[n].rearrange("(a n) -> a n", a=1).broadcast_to([P, C])).then_inc(consts_in, DMA)
            sp.dma_start(o.bp_row[:, :], w["bp"].rearrange("(a n) -> a n", a=1).broadcast_to([P, C])).then_inc(consts_in, DMA)
            sp.dma_start(gate_in[:, :], g_x.rearrange("(a n) -> a n", a=1).broadcast_to([P, 1])).then_inc(consts_in, DMA)
            store_k_parts(0)
            store_q_parts(0)
            sp.wait_ge(zeroed, 2)
            sp.wait_ge(ones_set, 1)
            load_half(0, 0)
            sp.wait_ge(half1_set, 2)
            load_half(0, 1)
            store_shift(0, 0)
            element(0, True, False)
            with sp.Fori(1, B - 1) as b:
                element(b, False, False)
            element(B - 1, False, True)
            sp.wait_ge(o.x1_stored, (B - 1) * DMA)
            load_rows(sp, o, x1_rows, 0, 0)
            load_rows(sp, o, x1_rows, 1, 1)
            sp.dma_start(o.router_w[:, :], w["rw1"]).then_inc(o.router_loaded, DMA)
            store_y(B - 1, GROUPS - 1)

        @block.tensor
        def _(pe):
            def scores(b, j, pair):
                g, t = divmod(j, STEPS)
                k = 2 * (BSTEPS * b + j) + pair
                if not (isinstance(k, int) and k < BANKS):
                    pe.wait_ge(exp_done, k - BANKS + 1)
                if t == 0 and pair == 0:
                    pe.wait_ge(shift_in, (GROUPS * b + g + 1) * 4 * DMA)
                out = ps_s[:, (2 * j + pair) % BANKS, :, :]
                own = t - NCH
                if own >= 0:
                    qs_ = slice(own * P, (own + 1) * P)
                    pe.matmul(out[:, :, qs_], ident_b[:, :], mask_k[:, own:own + 1, qs_].broadcast_to([P, 2, P]),
                              start=True, stop=False, skip_group_check=True)
                for i in (2 * pair, 2 * pair + 1):
                    half, h8, tile, _ = in_half(g, i)
                    if own < 0:
                        n = P if t < NCH - 1 else TAIL
                        mm = pe.matmul(out[0:n, i % 2, :], kx[half][:, tile, t * P:t * P + n],
                                       qx[half][:, h8, :], start=True, stop=True)
                    else:
                        mm = pe.matmul(out[:, i % 2, :], kself[half][:, tile, own * P:(own + 1) * P],
                                       qself[half][:, h8, :], start=False, stop=(i % 2 == 1), skip_group_check=True)
                mm.then_inc(scores_ready, 1)

            def unit(b, g, u):
                number = NU * (GROUPS * b + g) + u
                if not (isinstance(number, int) and number < BANKS):
                    pe.wait_ge(unit_reduced, number - BANKS + 1)
                kind, qt, i0, kc = UNITS[u]
                out = ps_a[:, u % BANKS, :]
                q = slice(qt * P, (qt + 1) * P)
                if kind == "cross":
                    half, h8, tile, _ = in_half(g, i0)
                    mm = pe.matmul(out, qx[half][0:SHIFT, h8, q], kx[half][0:SHIFT, tile, kc * 512:(kc + 1) * 512],
                                   start=True, stop=True)
                elif kind == "cross_rest":
                    for i in range(GROUP):
                        half, h8, tile, _ = in_half(g, i)
                        mm = pe.matmul(out[:, i * REST_W:(i + 1) * REST_W], qx[half][0:SHIFT, h8, q],
                                       kx[half][0:SHIFT, tile, TC - REST_W:TC], start=True, stop=True)
                else:
                    out = out.rearrange("p (i n) -> p i n", n=T)
                    pe.matmul(out[:, :, q], ident_b[:, :], mask_q[:, qt:qt + 1, q].broadcast_to([P, 2, P]),
                              start=True, stop=False, skip_group_check=True)
                    for i in (i0, i0 + 1):
                        half, h8, tile, _ = in_half(g, i)
                        mm = pe.matmul(out[:, i - i0, :], qself[half][0:SHIFT, h8, q],
                                       kself[half][0:SHIFT, tile, :], start=False, stop=(i == i0 + 1),
                                       skip_group_check=True)
                mm.then_inc(unit_ready, 1)

            def operands_here(b, g):
                if g % 2 == 0:
                    pe.wait_ge(half_in[g // 2], (b + 1) * HALF_DMAS * DMA)

            def pv(b, j):
                g, t = divmod(j, STEPS)
                pe.wait_ge(exp_done, 2 * (BSTEPS * b + j) + 2)
                if t == 0:
                    if not (isinstance(b, int) and GROUPS * b + g == 0):
                        pe.wait_ge(y_copied, GROUPS * b + g)
                    if g % 2 == 0:
                        pe.wait_ge(vhalf_done[g // 2], b + 1)
                for i in range(GROUP):
                    half, h8, _, _ = in_half(g, i)
                    if t < NCH:
                        n = P if t < NCH - 1 else TAIL
                        mm = pe.matmul(ps_y[32 * i:32 * i + VW, 0, :], v_half[half][0:n, t, h8, :],
                                       probs[0:n, j % 3, i * T:(i + 1) * T], start=(t == 0), stop=(t == NCH - 1))
                    elif t == NCH:
                        mm = pe.matmul(ps_y[32 * i:32 * i + VW, 1, :], v_half[half][:, t, h8, :],
                                       probs[:, j % 3, i * T:(i + 1) * T], start=True, stop=False)
                    else:
                        mm = pe.matmul(ps_y[32 * i:32 * i + VW, 1, P:T], v_half[half][:, t, h8, :],
                                       probs[:, j % 3, i * T + P:(i + 1) * T], start=False, stop=True)
                mm.then_inc(pv_done, 1)

            def shift_job(s):
                pe.wait_ge(shift_lo, s + 1)
                pe.transpose(o.ps_m[0:4 * GROUP * 2, 0:P], shift[:, :, :].rearrange("p a n -> p (a n)").bitcast(F32),
                             o.ident[:, :]).then_inc(shift_ps, 1)

            def xn_job(c):
                pe.wait_ge(xn_done, c + 1)
                if not (isinstance(c, int) and c == 0):
                    pe.wait_ge(shift_t_done, GROUPS * c - GROUPS + 1)
                for t in range(2):
                    mm = pe.transpose(o.ps_m[:, t * P:(t + 1) * P], xn[:, t, :], o.ident[:, :])
                mm.then_inc(xnt_ps, 1)

            def qk_job(c):
                pe.wait_ge(xnt_done, c + 1)
                pe.matmul(o.ps_m[:, 0:T], wq_sb[:, :], xn_t[:, :], start=True, stop=True)
                pe.matmul(o.ps_m[:, T:2 * T], wk_sb[:, :], xn_t[:, :], start=True, stop=True).then_inc(qk_ps, 1)

            def cq_job(c):
                pe.wait_ge(qk_lo, c + 1)
                pe.matmul(o.ps_m[:, 0:T], wcq_sb[:, :], xn_t[:, :], start=True, stop=True).then_inc(cq_ps, 1)

            def ck_job(c, n):
                if isinstance(c, int) and c == 0:
                    pe.wait_ge(ctx_loaded, DMA)
                elif n > 0:
                    pe.wait_ge(ck_lo, c * NCK + n)
                else:
                    pe.wait_ge(cq_lo, c + 1)
                    pe.wait_ge(ctx_loaded, (c + 1) * DMA)
                k0, k1 = n * 512, min((n + 1) * 512, TC)
                pe.matmul(ck_bank(c, n)[:, 0:k1 - k0], wck_sb[:, :], ctx_in[:, k0:k1], start=True, stop=True).then_inc(ck_ps, 1)

            def cv_job(c, n):
                if n > 0:
                    pe.wait_ge(cv_done, c * NCV + n)
                else:
                    pe.wait_ge(ck_lo, (c + 1) * NCK)
                    pe.wait_ge(cq_lo, c + 1)
                for ch in range(4 * n, min(4 * n + 4, NCH)):
                    k = P if ch < NCH - 1 else TAIL
                    mm = pe.matmul(o.ps_m[0:k, (ch - 4 * n) * C:(ch - 4 * n + 1) * C], ctx_in[0:CK - 1, ch * P:ch * P + k],
                                   wcv_sb[:, :], start=True, stop=True)
                mm.then_inc(cv_ps, 1)

            def v_job(c):
                pe.wait_ge(cv_done, (c + 1) * NCV)
                for t in range(2):
                    mm = pe.matmul(o.ps_m[:, t * C:(t + 1) * C], xn_t[:, t * P:(t + 1) * P], wv_sb[:, :],
                                   start=True, stop=True)
                mm.then_inc(v_ps, 1)

            def element(b, first, last):
                for j in range(BSTEPS):
                    ahead, g, pos = target(j)
                    mine = [] if last and ahead else list(units_at(pos))
                    for pair in range(2):
                        if j + 1 < BSTEPS:
                            scores(b, j + 1, pair)
                        elif not last:
                            scores(b + 1, 0, pair)
                        if mine and pos == 0 and pair == 0:
                            operands_here(b + ahead, g)
                        if mine:
                            unit(b + ahead, g, mine[pair])
                    if not last:
                        if j == J_XT:
                            xn_job(b + 1)
                        if j == J_QK:
                            qk_job(b + 1)
                        if j == J_CQ:
                            cq_job(b + 1)
                        if j in J_CK:
                            if j == J_CK[0] and not first:
                                pe.wait_ge(o.att_done, b)
                            if j in J_CK[:1]:
                                pe.wait_ge(shift_t_done, GROUPS * b + 2)
                            ck_job(b + 1, J_CK.index(j))
                        if j in J_CV:
                            if j == J_CV[2]:
                                pe.wait_ge(shift_t_done, GROUPS * b + 3)
                            cv_job(b + 1, J_CV.index(j))
                        if j == J_V:
                            v_job(b + 1)
                    if j == J_OUT and not first:
                        pe.wait_ge(shift_t_done, GROUPS * b + 2)
                        out_job(pe, o, b - 1)
                    if j in J_SHIFT and not (last and j == J_SHIFT[-1]):
                        k = J_SHIFT.index(j)
                        if k == 0 and not last:
                            pe.wait_ge(cq_lo, b + 2)
                        if k == 0 and last:
                            pe.wait_ge(shift_t_done, GROUPS * b + 1)
                        if k == 1 and not last:
                            pe.wait_ge(cv_done, (b + 1) * NCV + 2)
                        if k == 1 and last:
                            pe.wait_ge(o.att_done, b)
                        if k == 2 and not last:
                            pe.wait_ge(v_done, b + 2)
                        if k == 2 and last or k == 3:
                            pe.wait_ge(shift_t_done, GROUPS * b + k + 1)
                        shift_job(GROUPS * b + 1 + k)
                    pv(b, j)

            pe.wait_ge(wck_in, DMA)
            for n in range(NCK):
                ck_job(0, n)
            pe.wait_ge(consts_in, N_CONST * DMA)
            pe.wait_ge(masks_set, 4)
            xn_job(0)
            qk_job(0)
            cq_job(0)
            for n in range(NCV):
                cv_job(0, n)
            v_job(0)
            pe.wait_ge(ones_set, 1)
            pe.wait_ge(half1_set, 2)
            operands_here(0, 0)
            for u in range(NU):
                unit(0, 0, u)
            pe.wait_ge(v_done, 1)
            shift_job(0)
            for pos in range(LEAD):
                for u in units_at(pos):
                    unit(0, 1, u)
            scores(0, 0, 0)
            scores(0, 0, 1)
            element(0, True, False)
            with pe.Fori(1, B - 1) as b:
                element(b, False, False)
            element(B - 1, False, True)

        @block.scalar
        def _(act):
            def exp(b, j):
                g, t = divmod(j, STEPS)
                if not (isinstance(b, int) and BSTEPS * b + j < 3):
                    act.wait_ge(pv_done, BSTEPS * b + j - 2)
                n = TAIL if t == NCH - 1 else P
                q0 = P if t == NCH + 1 else 0
                dst = probs[0:n, j % 3, :].rearrange("p (i q) -> p i q", q=T)
                for pair in range(2):
                    act.wait_ge(scores_ready, 2 * (BSTEPS * b + j) + pair + 1)
                    act.activation(dst[:, 2 * pair:2 * pair + 2, q0:T], ps_s[0:n, (2 * j + pair) % BANKS, :, q0:T],
                                   ACT.Exp, scale=SCALE).then_inc(exp_done, 1)

            def copy_y(b, g):
                act.wait_ge(pv_done, BSTEPS * b + (g + 1) * STEPS)
                if not (isinstance(b, int) and GROUPS * b + g < 2):
                    act.wait_ge(o.y_stored[g % 2], (GROUPS // 2 * b + g // 2) * GROUP * DMA)
                act.activation(o.y_raw[:, g % 2, :, :], ps_y[:, :, :], ACT.Copy).then_inc(y_copied, 1)

            def xnt(c):
                act.wait_ge(xnt_ps, c + 1)
                if not (isinstance(c, int) and c == 0):
                    act.wait_ge(v_ps, c)
                act.activation(xn_t[:, :], o.ps_m[:, 0:T], ACT.Copy).then_inc(xnt_done, 1)

            def qk(c):
                act.wait_ge(qk_ps, c + 1)
                if not (isinstance(c, int) and c == 0):
                    act.wait_ge(qk_stored, c * 12 * DMA)
                for i in range(2):
                    a = act.activation(parts[:, i, 0, :], o.ps_m[:, i * T:(i + 1) * T], ACT.Identity, bias=bias_sb[:, i:i + 1])
                a.then_inc(qk_hi, 1)

            def cq(c):
                act.wait_ge(cq_ps, c + 1)
                act.activation(parts[:, 2, 0, :], o.ps_m[:, 0:T], ACT.Identity, bias=bias_sb[:, 2:3]).then_inc(cq_hi, 1)

            def ck(c, n):
                act.wait_ge(ck_ps, c * NCK + n + 1)
                if n == 0 and not (isinstance(c, int) and c == 0):
                    act.wait_ge(kx_stored, c * 4 * DMA)
                k0, k1 = n * 512, min((n + 1) * 512, TC)
                act.activation(ck_parts[:, 0, k0:k1], ck_bank(c, n)[:, 0:k1 - k0], ACT.Copy).then_inc(ck_hi, 1)

            def cv(c, n):
                act.wait_ge(cv_ps, c * NCV + n + 1)
                if n == 0 and not (isinstance(c, int) and c == 0):
                    act.wait_ge(vhalf_done[1], c)
                full = min(4 * n + 4, NCH - 1) - 4 * n
                a = None
                if full > 0:
                    a = act.activation(v_all[:, 4 * n:4 * n + full, :],
                                       o.ps_m[:, 0:full * C].rearrange("p (a c) -> p a c", c=C), ACT.Copy)
                if 4 * n + 4 >= NCH:
                    a = act.activation(v_all[0:TAIL, NCH - 1, :], o.ps_m[0:TAIL, full * C:(full + 1) * C], ACT.Copy)
                a.then_inc(cv_done, 1)

            def shift_rows(s):
                act.wait_ge(shift_ps, s + 1)
                if not (isinstance(s, int) and s == 0):
                    act.wait_ge(shift_in, s * 4 * DMA)
                act.activation(shift_t[:, :], o.ps_m[0:4 * GROUP * 2, 0:P], ACT.Copy).then_inc(shift_t_done, 1)

            def element(b, first, last):
                for j in range(BSTEPS):
                    if j + 1 < BSTEPS:
                        exp(b, j + 1)
                    elif not last:
                        exp(b + 1, 0)
                    if j % STEPS == STEPS - 1:
                        copy_y(b, j // STEPS)
                    if not last:
                        if j == J_XT:
                            xnt(b + 1)
                        if j == J_QK:
                            qk(b + 1)
                        if j == J_CQ:
                            cq(b + 1)
                        if j in J_CK:
                            ck(b + 1, J_CK.index(j))
                        if j in J_CV:
                            cv(b + 1, J_CV.index(j))
                    if j in J_SHIFT and not (last and j == J_SHIFT[-1]):
                        shift_rows(GROUPS * b + 1 + J_SHIFT.index(j))

            for n in range(NCK):
                ck(0, n)
            act.wait_ge(consts_in, N_CONST * DMA)
            xnt(0)
            qk(0)
            cq(0)
            act.activation(o.gate[:, :], gate_in[:, :], ACT.Tanh).then_inc(gate_set, 1)
            act.wait_ge(zeroed, 1)
            for n in range(NCV):
                cv(0, n)
            shift_rows(0)
            exp(0, 0)
            element(0, True, False)
            with act.Fori(1, B - 1) as b:
                element(b, False, False)
            element(B - 1, False, True)

        @block.vector
        def _(dve):
            def reduce_unit(b, g, u):
                dve.wait_ge(unit_ready, NU * (GROUPS * b + g) + u + 1)
                kind, qt, i0, kc = UNITS[u]
                src = ps_a[:, u % BANKS, :]
                if kind == "cross":
                    out = max_x[:, i0, qt, kc:kc + 1]
                elif kind == "cross_rest":
                    out, src = max_x[:, :, qt, NFULL], src[:, 0:GROUP * REST_W].rearrange("p (i n) -> p i n", n=REST_W)
                else:
                    out, src = max_s[:, i0:i0 + 2, qt], src.rearrange("p (i n) -> p i n", n=T)[:, :, 0:(qt + 1) * P]
                nc.vector.tensor_reduce(out, src, AX_X, ALU.max).then_inc(unit_reduced, 1)

            def shift_parts(b, g):
                s = GROUPS * b + g
                dve.wait_ge(unit_reduced, NU * (s + 1))
                if not (isinstance(s, int) and s == 0):
                    dve.wait_ge(shift_ps, s)
                nc.vector.tensor_reduce(neg_max[:, 0, :], max_x[:, :, :, :].rearrange("p i t n -> p (i t) n"),
                                        AX_X, ALU.max, negate=True)
                nc.vector.tensor_scalar(neg_max[:, 1, :], max_s[:, :, :].rearrange("p i t -> p (i t)"), -1.0, None,
                                        ALU.mult).then_inc(neg_done, 1)
                dve.wait_ge(neg_done, s + 1)
                flat = neg_max[:, :, :].rearrange("p a n -> p (a n)")
                nc.vector.tensor_copy(shift[:, 0, :], flat).then_inc(shift_hi, 1)
                dve.wait_ge(shift_hi, s + 1)
                nc.vector.tensor_tensor(shift[:, 1, :], flat, shift[:, 0, :].bitcast(F32), ALU.subtract).then_inc(shift_lo, 1)

            def ln_stats(c):
                dve.wait_ge(x_loaded, (c + 1) * DMA)
                for t in range(2):
                    a = nc.vector.bn_stats(stats[:, t, :], x_in[:, t, :])
                a.then_inc(stats_done, 1)
                dve.wait_ge(stats_done, c + 1)
                join_stats(nc, dve, stats, joined, mean, var_eps, joined_1, joined_2, eps_done, c)

            def ln_apply(c):
                dve.wait_ge(rstd_done, c + 1)
                for t in range(2):
                    a = nc.vector.tensor_scalar(xn[:, t, :], x_in[:, t, :], mean[:, t:t + 1], rstd[:, t:t + 1],
                                                ALU.subtract, ALU.mult)
                a.then_inc(xn_done, 1)

            def lo_part(out_lo, hi, src, bias):
                return nc.vector.scalar_tensor_tensor(out_lo, src, bias, hi.bitcast(F32), ALU.add, ALU.subtract)

            def qk(c):
                dve.wait_ge(qk_hi, c + 1)
                for i in range(2):
                    a = lo_part(parts[:, i, 1, :], parts[:, i, 0, :], o.ps_m[:, i * T:(i + 1) * T], bias_sb[:, i:i + 1])
                a.then_inc(qk_lo, 1)

            def cq(c):
                dve.wait_ge(cq_hi, c + 1)
                lo_part(parts[:, 2, 1, :], parts[:, 2, 0, :], o.ps_m[:, 0:T], bias_sb[:, 2:3]).then_inc(cq_lo, 1)

            def ck(c, n):
                dve.wait_ge(ck_hi, c * NCK + n + 1)
                k0, k1 = n * 512, min((n + 1) * 512, TC)
                nc.vector.tensor_tensor(ck_parts[:, 1, k0:k1], ck_bank(c, n)[:, 0:k1 - k0], ck_parts[:, 0, k0:k1].bitcast(F32),
                                        ALU.subtract).then_inc(ck_lo, 1)

            def v(c):
                dve.wait_ge(v_ps, c + 1)
                if not (isinstance(c, int) and c == 0):
                    dve.wait_ge(vhalf_done[1], c)
                nc.vector.tensor_copy(v_all[:, NCH:NCH + 2, :],
                                      o.ps_m[:, 0:2 * C].rearrange("p (a c) -> p a c", c=C)).then_inc(v_done, 1)

            def element(b, first, last):
                for j in range(BSTEPS):
                    ahead, g, pos = target(j)
                    if not (last and ahead):
                        for u in units_at(pos):
                            reduce_unit(b + ahead, g, u)
                        if pos == STEPS - 1:
                            shift_parts(b + ahead, g)
                    if not last:
                        if j == J_LN:
                            ln_stats(b + 1)
                        if j == J_XN:
                            ln_apply(b + 1)
                        if j == J_QK + 1:
                            qk(b + 1)
                        if j == J_CQ + 1:
                            cq(b + 1)
                        if j - 1 in J_CK:
                            ck(b + 1, J_CK.index(j - 1))
                        if j == J_V + 1:
                            v(b + 1)
                    if not first:
                        if j == J_REC:
                            reciprocals(nc, dve, o, b - 1)
                        if j == J_OUT + 1:
                            residual(nc, dve, o, b - 1)

            ln_stats(0)
            ln_apply(0)
            for n in range(NCK):
                ck(0, n)
            nc.vector.memset(v_all[64:P, NCH - 1, :], 0.0)
            nc.vector.memset(qx[0][:, :, :].bitcast(F32), 0.0)
            nc.vector.memset(kself[0][64:ROWS, TILES - 1, :].bitcast(F32), 0.0)
            nc.vector.memset(kx[0][64:ROWS, TILES - 1, :].bitcast(F32), 0.0).then_inc(zeroed, 1)
            dve.wait_ge(consts_in, N_CONST * DMA)
            qk(0)
            nc.vector.memset(qself[0][:, :, :].bitcast(F32), 0.0).then_inc(zeroed, 1)
            cq(0)
            dve.wait_ge(zeroed, 2)
            nc.vector.memset(kself[0][SHIFT:ROWS, :, :].bitcast(F32), 1.0)
            nc.vector.memset(kx[0][SHIFT:ROWS, :, :].bitcast(F32), 1.0).then_inc(ones_set, 1)
            nc.vector.memset(ps_y[:, :, :], 0.0)
            v(0)
            for u in range(NU):
                reduce_unit(0, 0, u)
            shift_parts(0, 0)
            for pos in range(LEAD):
                for u in units_at(pos):
                    reduce_unit(0, 1, u)
            dve.wait_ge(gate_set, 1)
            element(0, True, False)
            with dve.Fori(1, B - 1) as b:
                element(b, False, False)
            element(B - 1, False, True)
            row_stats(nc, dve, o, 0, 0)
            join_rows(nc, dve, o, 0)
            normalise_rows(nc, dve, o, 0, 0)

        @block.gpsimd
        def _(pool):
            def fill_v_half(b, half):
                pool.wait_ge(cv_done, (b + 1) * NCV)
                pool.wait_ge(v_done, b + 1)
                if not (isinstance(b, int) and b == 0):
                    pool.wait_ge(pv_done, (b - 1) * BSTEPS + (half + 1) * (BSTEPS // 2))
                for st, (n0, n1) in enumerate(((0, NCH), (NCH, NCH + 2))):
                    src = v_all[:, n0:n1, half * HALF * D:(half + 1) * HALF * D].rearrange("p n (h d) -> p n h d", d=D)
                    bias = v_bias[:, st:st + 1, half * HALF * D:(half + 1) * HALF * D].rearrange("p n (h d) -> p n h d", d=D)
                    a = nc.gpsimd.tensor_tensor(v_half[half][:, n0:n1, :, 0:D], src,
                                                bias.broadcast_to([P, n1 - n0, HALF, D]), ALU.add)
                a.then_inc(vhalf_done[half], 1)

            def rstd_of(c):
                pool.wait_ge(eps_done, c + 1)
                nc.gpsimd.tensor_tensor(rstd[:, :], var_eps[:, :], minus_half[:, :], ALU.pow).then_inc(rstd_done, 1)

            def element(b, first, last):
                if not first:
                    fill_v_half(b, 1)
                if not last:
                    rstd_of(b + 1)
                if not first:
                    normalise(nc, pool, o, b - 1)
                if not last:
                    fill_v_half(b + 1, 0)

            nc.gpsimd.memset(o.minus_half[:, :], -0.5).then_inc(o.started, 1)
            nc.gpsimd.memset(minus_half[:, :], -0.5).then_inc(masks_zero, 1)
            pool.wait_ge(masks_zero, 1)
            rstd_of(0)
            for m in (o.ident, ident_b):
                nc.gpsimd.memset(m[:, :], 0.0).then_inc(masks_zero, 1)
            for m in (mask_q, mask_k):
                nc.gpsimd.memset(m[:, :, :], 0.0).then_inc(masks_zero, 1)
            pool.wait_ge(masks_zero, 5)
            for m in (o.ident, ident_b):
                nc.gpsimd.affine_select(out=m[:, :], in_=m[:, :], compare_op=ALU.not_equal, fill=1.0, base=0,
                                        pattern=[[-1, P]], channel_multiplier=1).then_inc(masks_set, 1)
            nc.gpsimd.affine_select(out=mask_q[:, :, :], in_=mask_q[:, :, :], compare_op=ALU.is_ge, fill=NEG, base=0,
                                    pattern=[[P, 2], [-1, T]], channel_multiplier=1).then_inc(masks_set, 1)
            nc.gpsimd.affine_select(out=mask_k[:, :, :], in_=mask_k[:, :, :], compare_op=ALU.is_ge, fill=NEG, base=0,
                                    pattern=[[-P, 2], [1, T]], channel_multiplier=-1).then_inc(masks_set, 1)
            nc.gpsimd.memset(qx[1][:, :, :].bitcast(F32), 0.0)
            nc.gpsimd.memset(qself[1][:, :, :].bitcast(F32), 0.0).then_inc(half1_zeroed, 1)
            pool.wait_ge(half1_zeroed, 1)
            nc.gpsimd.memset(kself[1][64:ROWS, TILES - 1, :].bitcast(F32), 0.0)
            nc.gpsimd.memset(kx[1][64:ROWS, TILES - 1, :].bitcast(F32), 0.0).then_inc(half1_zeroed, 1)
            pool.wait_ge(half1_zeroed, 2)
            nc.gpsimd.memset(kself[1][SHIFT:ROWS, :, :].bitcast(F32), 1.0).then_inc(half1_set, 1)
            nc.gpsimd.memset(kx[1][SHIFT:ROWS, :, :].bitcast(F32), 1.0).then_inc(half1_set, 1)
            pool.wait_ge(half1_set, 2)
            for i in range(2):
                nc.gpsimd.memset(v_half[i][:, :, :, D:VW], 1.0)
            pool.wait_ge(zeroed, 1)
            pool.wait_ge(consts_in, N_CONST * DMA)
            fill_v_half(0, 0)
            fill_v_half(0, 1)
            element(0, True, False)
            with pool.Fori(1, B - 1) as b:
                element(b, False, False)
            element(B - 1, False, True)
            rstd_of_rows(nc, pool, o, 0)


def experts(nc, x, x1, y_rows, g_f, w, out, o):
    LAST_B = x.shape[0] - 1
    x1_rows = x1.rearrange("b t c -> (b t) c")
    R = x1_rows.shape[0]
    E, _, HID = w["w1"].shape
    TR = TILE_ROWS
    NT = R // TR
    SUB = TR // P
    M = HID // P
    NE = E + 1
    RING_H = 3
    STAGED = 4
    RING_O = 3
    assert NE * M % RING_H == 0

    with ExitStack() as ctx:
        def sb(name, shape, dt=F32):
            return ctx.enter_context(nc.sbuf_tensor(name, shape, dt))

        def psum(name, shape):
            return ctx.enter_context(nc.psum_tensor(name, shape, F32))

        def sem(name):
            return ctx.enter_context(nc.semaphore(name))

        up_w, down_w = sb("up_w", [P, STAGED, HID]), sb("down_w", [P, STAGED, M, C])
        up_hi, up_lo = sb("up_hi", [P, NE, HID], F32R), sb("up_lo", [P, NE, HID], F32R)
        down_hi, down_lo = sb("down_hi", [P, E, M, C], F32R), sb("down_lo", [P, E, M, C], F32R)
        up_b = sb("up_b", [P, NE, M])
        rw2_sb = sb("rw2_sb", [P, M, E])
        rb2_row = sb("rb2_row", [P, E])
        b2_sb = sb("b2_sb", [2 * E, C])
        gate_in, gate = sb("fgate_in", [P, 1]), sb("fgate", [P, 1])
        select = sb("select", [2 * E, E, P], F32R)
        expert_no = sb("expert_no", [P, E])

        x_hi, x_lo = sb("x_hi", [P, 2, TR], F32R), sb("x_lo", [P, 2, TR], F32R)
        hid = sb("hid", [P, 2, M, TR])
        hid_hi, hid_lo = sb("hid_hi", [P, 2, M, TR], F32R), sb("hid_lo", [P, 2, M, TR], F32R)
        logits = sb("logits", [P, SUB, E])
        best = sb("best", [P, SUB, 8])
        best_at = sb("best_at", [P, SUB, 8], U32)
        best_no = sb("best_no", [P, SUB, 2])
        diff = sb("diff", [P, SUB])
        half_tanh = sb("half_tanh", [P, SUB])
        prob = sb("prob", [P, 2, SUB])
        pick = sb("pick", [P, 2, SUB, E])
        gates = sb("gates", [P, SUB, E])
        gate_parts = sb("gate_parts", [P, SUB, 2, E], F32R)
        gates_t = sb("gates_t", [2 * E, TR], F32R)
        spread = sb("spread", [P, 2, TR])
        weighed = sb("weighed", [P, 2, TR])
        acc = sb("acc", [P, TR])
        y = sb("fy", [P, 2, SUB, C])

        ps_h = psum("ps_h", [P, RING_H, TR])
        ps_o = psum("ps_o", [P, RING_O, TR])
        ps_t = psum("ps_t", [P, TR])
        ps_g = o.ps_m

        w_in = sem("w_in")
        w_loaded = [sem(f"w_loaded{e}") for e in range(NE)]
        w_hi_act, w_hi_pool = sem("w_hi_by_scalar"), sem("w_hi_by_gpsimd")
        w_split = sem("w_split")
        small_set = sem("small_set")
        select_set = sem("select_set")
        gate_set = sem("fgate_set")
        x_hi_done, x_lo_done = sem("x_hi_done"), sem("x_lo_done")
        up_ready = sem("up_ready")
        silu_done, hid_hi_done, hid_lo_done = sem("silu_done"), sem("hid_hi_done"), sem("hid_lo_done")
        logits_ps, logits_done = sem("logits_ps"), sem("logits_done")
        best_done, at_done, diff_done = sem("best_done"), sem("at_done"), sem("diff_done")
        tanh_done, prob_done, pick_done = sem("tanh_done"), sem("prob_done"), sem("pick_done")
        picked, gates_done, gates_hi, gates_lo = sem("picked"), sem("gates_done"), sem("gates_hi"), sem("gates_lo")
        gates_ps, gates_t_done = sem("gates_ps"), sem("gates_t_done")
        spread_ps, spread_done = sem("spread_ps"), sem("spread_done")
        down_ready, weighed_done, added = sem("down_ready"), sem("weighed_done"), sem("added")
        out_ps, y_done = sem("fout_ps"), sem("fy_done")
        y_stored = [sem("fy_stored_even"), sem("fy_stored_odd")]

        N_W = 6
        block = ctx.enter_context(nc.Block())

        def first_tile(r):
            return isinstance(r, int) and r == 0

        def hidden_slot(slot, e):
            return (slot * NE + e) % 2

        @block.sync
        def _(sp):
            def store(r, slot):
                sp.wait_ge(w_in, N_W * DMA)
                sp.wait_ge(y_done, r + 1)
                sp.dma_start(out[bass.ds(r * TR, TR), :].rearrange("(t p) c -> p t c", p=P), y[:, slot, :, :]
                             ).then_inc(y_stored[slot], DMA)

            def load_weights(e):
                if e > STAGED:
                    sp.wait_ge(w_split, e - STAGED + 1)
                k = (e - 1) % STAGED
                sp.dma_start(up_w[:, k, :], w["w1"][e - 1]).then_inc(w_loaded[e], DMA)
                sp.dma_start(down_w[:, k, :, :], w["w2"][e - 1].rearrange("(m p) c -> p m c", p=P)
                             ).then_inc(w_loaded[e], DMA)

            sp.dma_start(up_b[:, :, :], w["up_b"]).then_inc(w_in, DMA)
            sp.dma_start(rw2_sb[:, :, :], w["rw2"].rearrange("(m p) e -> p m e", p=P)).then_inc(w_in, DMA)
            sp.dma_start(rb2_row[:, :], w["rb2"].rearrange("(a n) -> a n", a=1).broadcast_to([P, E])).then_inc(w_in, DMA)
            for part in range(2):
                sp.dma_start(b2_sb[part * E:(part + 1) * E, :], w["b2"]).then_inc(w_in, DMA)
            sp.dma_start(gate_in[:, :], g_f.rearrange("(a n) -> a n", a=1).broadcast_to([P, 1])).then_inc(w_in, DMA)
            load_weights(1)
            load_y(sp, o, y_rows, x, LAST_B)
            for e in range(2, NE):
                load_weights(e)
            store_x1(sp, o, x1, LAST_B)
            sp.wait_ge(o.x1_stored, (LAST_B + 1) * DMA)
            with sp.Fori(0, NT // 2 - 1) as i:
                for slot in range(2):
                    r = 2 * i + slot
                    store(r, slot)
                    load_rows(sp, o, x1_rows, r + 2, slot)
            for r in (NT - 2, NT - 1):
                store(r, r % 2)
            for even_odd in y_stored:
                sp.wait_ge(even_odd, NT // 2 * DMA)

        @block.tensor
        def _(pe):
            def transpose_x(r):
                pe.wait_ge(o.rows_n_done, r + 1)
                if not first_tile(r):
                    pe.wait_ge(gates_t_done, r)
                for t in range(SUB):
                    mm = pe.transpose(ps_t[:, t * P:(t + 1) * P], o.rows_n[:, t, :], o.ident[:, :])
                mm.then_inc(o.turned, 1)

            def up(r, slot, e, m):
                n = (NE * r + e) * M + m
                if not (isinstance(n, int) and n < RING_H):
                    pe.wait_ge(silu_done, n - RING_H + 1)
                if first_tile(r) and m == 0:
                    pe.wait_ge(w_split, e + 1)
                cols = slice(m * P, (m + 1) * P)
                bank = ps_h[:, (e * M + m) % RING_H, :]
                pe.matmul(bank, up_hi[:, e, cols], x_lo[:, slot, :], start=True, stop=False)
                pe.matmul(bank, up_lo[:, e, cols], x_hi[:, slot, :], start=False, stop=False)
                pe.matmul(bank, up_hi[:, e, cols], x_hi[:, slot, :], start=False, stop=True).then_inc(up_ready, 1)

            def router_down(r, slot):
                if first_tile(r):
                    pe.wait_ge(w_in, N_W * DMA)
                    pe.wait_ge(select_set, 1)
                pe.wait_ge(silu_done, (NE * r + 1) * M)
                for t in range(SUB):
                    for m in range(M):
                        mm = pe.matmul(ps_t[:, t * E:(t + 1) * E],
                                       hid[:, hidden_slot(slot, 0), m, t * P:(t + 1) * P],
                                       rw2_sb[:, m, :], start=(m == 0), stop=(m == M - 1))
                mm.then_inc(logits_ps, 1)

            def down(r, slot, e, m):
                pe.wait_ge(hid_lo_done, (E * r + e - 1) * M + m + 1)
                if m == 0:
                    if e > RING_O:
                        pe.wait_ge(weighed_done, E * r + e - RING_O)
                    elif not first_tile(r):
                        pe.wait_ge(weighed_done, E * r - (1 if e == 1 else 0))
                bank, hs = ps_o[:, (e - 1) % RING_O, :], hidden_slot(slot, e)
                pe.matmul(bank, down_hi[:, e - 1, m, :], hid_hi[:, hs, m, :], start=(m == 0), stop=False)
                pe.matmul(bank, down_lo[:, e - 1, m, :], hid_hi[:, hs, m, :], start=False, stop=False)
                mm = pe.matmul(bank, down_hi[:, e - 1, m, :], hid_lo[:, hs, m, :], start=False, stop=(m == M - 1))
                if m == M - 1:
                    mm.then_inc(down_ready, 1)

            def transpose_gates(r):
                pe.wait_ge(gates_lo, r + 1)
                for t in range(SUB):
                    mm = pe.transpose(ps_t[0:2 * E, t * P:(t + 1) * P],
                                      gate_parts[:, t, :, :].rearrange("p a e -> p (a e)").bitcast(F32), o.ident[:, :])
                mm.then_inc(gates_ps, 1)

            def spread_gates(r, e):
                if e == 1:
                    pe.wait_ge(gates_t_done, r + 1)
                    if first_tile(r):
                        pe.wait_ge(o.att_done, LAST_B + 1)
                    else:
                        pe.wait_ge(y_done, r)
                else:
                    pe.wait_ge(spread_done, E * r + e - 1)
                pe.matmul(ps_g[:, :], select[:, e - 1, :], gates_t[:, :], start=True, stop=True).then_inc(spread_ps, 1)

            def turn_output(r):
                pe.wait_ge(added, (E - 1) * (r + 1))
                for t in range(SUB):
                    rows = slice(t * P, (t + 1) * P)
                    pe.matmul(ps_g[:, rows], acc[:, rows], o.ident[:, :], start=True, stop=False)
                    mm = pe.matmul(ps_g[:, rows], gates_t[:, rows].bitcast(F32), b2_sb[:, :], start=False, stop=True)
                mm.then_inc(out_ps, 1)

            def tile(r, slot, last):
                pe.wait_ge(x_lo_done, r + 1)
                for s in range(NE):
                    for m in range(M):
                        up(r, slot, s, m)
                        if s == 0 and not first_tile(r):
                            down(r - 1, 1 - slot, E, m)
                            if m == 2:
                                spread_gates(r - 1, E)
                        if s >= 2:
                            down(r, slot, s - 1, m)
                        if s == 1 and m == 2 and not first_tile(r):
                            turn_output(r - 1)
                        if s == 3 and m == 0 and first_tile(r):
                            out_job(pe, o, LAST_B)
                        if s == 3 and m == 1:
                            transpose_gates(r)
                        if s == 3 and m == 3:
                            spread_gates(r, 1)
                        if s == 4 and m in (1, 3):
                            spread_gates(r, 2 if m == 1 else 3)
                        if s >= 5 and m == 2:
                            spread_gates(r, s - 1)
                        if s == 7 and m == 1 and not last:
                            transpose_x(r + 1)
                    if s == 1:
                        router_down(r, slot)

            transpose_x(0)
            tile(0, 0, False)
            tile(1, 1, False)
            with pe.Fori(1, NT // 2 - 1) as i:
                for slot in range(2):
                    tile(2 * i + slot, slot, False)
            tile(NT - 2, 0, False)
            tile(NT - 1, 1, True)
            for m in range(M):
                down(NT - 1, 1, E, m)
                if m == 2:
                    spread_gates(NT - 1, E)
            turn_output(NT - 1)

        @block.scalar
        def _(act):
            def weights_hi(e):
                if e == 0:
                    act.wait_ge(o.router_loaded, DMA)
                    a = act.activation(up_hi[:, 0, :], o.router_w[:, :], ACT.Copy)
                else:
                    act.wait_ge(w_loaded[e], 2 * DMA)
                    k = (e - 1) % STAGED
                    act.activation(up_hi[:, e, :], up_w[:, k, :], ACT.Copy)
                    a = act.activation(down_hi[:, e - 1, :, :], down_w[:, k, :, :], ACT.Copy)
                a.then_inc(w_hi_act, 1)

            def x_parts_hi(r, slot):
                act.wait_ge(o.turned, r + 1)
                if not (isinstance(r, int) and r < 2):
                    act.wait_ge(up_ready, NE * M * (r - 1))
                act.activation(x_hi[:, slot, :], ps_t[:, :], ACT.Copy).then_inc(x_hi_done, 1)

            def silu(r, slot, e, m):
                act.wait_ge(up_ready, (NE * r + e) * M + m + 1)
                if m == 0:
                    if e == 2:
                        act.wait_ge(logits_ps, r + 1)
                    elif e > 2 or not first_tile(r):
                        act.wait_ge(down_ready, E * r + (e - 1 if e < 2 else e - 2))
                act.activation(hid[:, hidden_slot(slot, e), m, :], ps_h[:, (e * M + m) % RING_H, :],
                               ACT.Silu, bias=up_b[:, e, m:m + 1]).then_inc(silu_done, 1)

            def hidden_hi(r, slot, e, m):
                act.wait_ge(silu_done, (NE * r + e) * M + m + 1)
                hs = hidden_slot(slot, e)
                act.activation(hid_hi[:, hs, m, :], hid[:, hs, m, :], ACT.Copy).then_inc(hid_hi_done, 1)

            def copy_gates_t(r):
                act.wait_ge(gates_ps, r + 1)
                if not first_tile(r):
                    act.wait_ge(out_ps, r)
                act.activation(gates_t[:, :], ps_t[0:2 * E, :], ACT.Copy).then_inc(gates_t_done, 1)

            def copy_spread(r, e):
                n = E * r + e
                act.wait_ge(spread_ps, n)
                if not (isinstance(n, int) and n < 3):
                    act.wait_ge(weighed_done, n - 2)
                act.activation(spread[:, e % 2, :], ps_g[:, :], ACT.Copy).then_inc(spread_done, 1)

            def tile(r, slot, last):
                for s in range(NE):
                    for m in range(M):
                        silu(r, slot, s, m)
                        if s == 0 and m == 0 and not first_tile(r):
                            hidden_hi(r - 1, 1 - slot, E, M - 1)
                        if s >= 2 and m == 0:
                            hidden_hi(r, slot, s - 1, M - 1)
                        if s >= 1 and m > 0:
                            hidden_hi(r, slot, s, m - 1)
                        if s == 0 and m == 3 and not first_tile(r):
                            copy_spread(r - 1, E)
                        if s == 0 and m == 3 and first_tile(r):
                            weights_hi(2)
                        if s == 2 and m == 1:
                            act.wait_ge(diff_done, r + 1)
                            act.activation(half_tanh[:, :], diff[:, :], ACT.Tanh, scale=0.5).then_inc(tanh_done, 1)
                        if s == 3 and m == 2:
                            copy_gates_t(r)
                        if s == 4 and m in (0, 2):
                            copy_spread(r, 1 if m == 0 else 2)
                        if s == 5 and m == 0:
                            copy_spread(r, 3)
                        if s >= 5 and m == 3:
                            copy_spread(r, s - 1)
                        if s == 7 and m == 2 and not last:
                            x_parts_hi(r + 1, 1 - slot)

            weights_hi(0)
            x_parts_hi(0, 0)
            weights_hi(1)
            act.wait_ge(w_in, N_W * DMA)
            act.activation(gate[:, :], gate_in[:, :], ACT.Tanh).then_inc(gate_set, 1)
            tile(0, 0, False)
            tile(1, 1, False)
            with act.Fori(1, NT // 2 - 1) as i:
                for slot in range(2):
                    tile(2 * i + slot, slot, False)
            tile(NT - 2, 0, False)
            tile(NT - 1, 1, True)
            hidden_hi(NT - 1, 1, E, M - 1)
            copy_spread(NT - 1, E)

        @block.vector
        def _(dve):
            def weights_lo(e):
                if e < 3:
                    dve.wait_ge(w_hi_act, e + 1)
                else:
                    dve.wait_ge(w_hi_pool, e - 2)
                k = (e - 1) % STAGED
                raw = up_w[:, k, :] if e > 0 else o.router_w[:, :]
                a = nc.vector.tensor_tensor(up_lo[:, e, :], raw, up_hi[:, e, :].bitcast(F32), ALU.subtract)
                if e > 0:
                    a = nc.vector.tensor_tensor(down_lo[:, e - 1, :, :], down_w[:, k, :, :],
                                                down_hi[:, e - 1, :, :].bitcast(F32), ALU.subtract)
                a.then_inc(w_split, 1)

            def x_parts_lo(r, slot):
                dve.wait_ge(x_hi_done, r + 1)
                nc.vector.tensor_tensor(x_lo[:, slot, :], ps_t[:, :], x_hi[:, slot, :].bitcast(F32), ALU.subtract
                                        ).then_inc(x_lo_done, 1)

            def hidden_lo(r, slot, e, m):
                dve.wait_ge(hid_hi_done, (E * r + e - 1) * M + m + 1)
                hs = hidden_slot(slot, e)
                nc.vector.tensor_tensor(hid_lo[:, hs, m, :], hid[:, hs, m, :], hid_hi[:, hs, m, :].bitcast(F32),
                                        ALU.subtract).then_inc(hid_lo_done, 1)

            def add_expert(r, e):
                n = E * r + e
                dve.wait_ge(down_ready, n)
                dve.wait_ge(spread_done, n)
                if e == 1:
                    nc.vector.tensor_tensor(acc[:, :], ps_o[:, 0, :], spread[:, e % 2, :], ALU.mult
                                            ).then_inc(weighed_done, 1)
                else:
                    nc.vector.tensor_tensor(weighed[:, e % 2, :], ps_o[:, (e - 1) % RING_O, :], spread[:, e % 2, :],
                                            ALU.mult).then_inc(weighed_done, 1)
                    dve.wait_ge(weighed_done, n)
                    if e > 2:
                        dve.wait_ge(added, (E - 1) * r + e - 2)
                    nc.vector.tensor_tensor(acc[:, :], acc[:, :], weighed[:, e % 2, :], ALU.add).then_inc(added, 1)

            def best_two(r):
                dve.wait_ge(logits_ps, r + 1)
                nc.vector.tensor_tensor(logits[:, :, :], ps_t[:, 0:SUB * E].rearrange("p (t e) -> p t e", e=E),
                                        rb2_row[:, :].rearrange("p (a e) -> p a e", a=1).broadcast_to([P, SUB, E]),
                                        ALU.add).then_inc(logits_done, 1)
                dve.wait_ge(small_set, 1)
                dve.wait_ge(logits_done, r + 1)
                for t in range(SUB):
                    a = nc.vector.max(best[:, t, :], logits[:, t, :])
                a.then_inc(best_done, 1)
                dve.wait_ge(best_done, r + 1)
                nc.vector.tensor_tensor(diff[:, :], best[:, :, 0], best[:, :, 1], ALU.subtract).then_inc(diff_done, 1)
                for t in range(SUB):
                    a = nc.vector.max_index(best_at[:, t, :], best[:, t, :], logits[:, t, :])
                a.then_inc(at_done, 1)

            def weigh_two(r):
                dve.wait_ge(at_done, r + 1)
                nc.vector.tensor_copy(best_no[:, :, :], best_at[:, :, 0:2]).then_inc(pick_done, 1)
                dve.wait_ge(tanh_done, r + 1)
                nc.vector.tensor_scalar(prob[:, 0, :], half_tanh[:, :], 0.5, 0.5, ALU.mult, ALU.add)
                nc.vector.tensor_scalar(prob[:, 1, :], half_tanh[:, :], -0.5, 0.5, ALU.mult, ALU.add).then_inc(prob_done, 1)
                dve.wait_ge(pick_done, r + 1)
                dve.wait_ge(prob_done, r + 1)
                for k in range(2):
                    for t in range(SUB):
                        a = nc.vector.tensor_scalar(pick[:, k, t, :], expert_no[:, :], best_no[:, t, k:k + 1],
                                                    prob[:, k, t:t + 1], ALU.is_equal, ALU.mult)
                a.then_inc(picked, 1)
                dve.wait_ge(picked, r + 1)
                nc.vector.tensor_tensor(gates[:, :, :], pick[:, 0, :, :], pick[:, 1, :, :], ALU.add).then_inc(gates_done, 1)
                dve.wait_ge(gates_done, r + 1)
                if not first_tile(r):
                    dve.wait_ge(gates_ps, r)
                nc.vector.tensor_copy(gate_parts[:, :, 0, :], gates[:, :, :]).then_inc(gates_hi, 1)
                dve.wait_ge(gates_hi, r + 1)
                nc.vector.tensor_tensor(gate_parts[:, :, 1, :], gates[:, :, :], gate_parts[:, :, 0, :].bitcast(F32),
                                        ALU.subtract).then_inc(gates_lo, 1)

            def finish(pair, slot):
                dve.wait_ge(out_ps, 2 * pair + slot + 1)
                if not (isinstance(pair, int) and pair == 0):
                    dve.wait_ge(y_stored[slot], pair * DMA)
                nc.vector.scalar_tensor_tensor(y[:, slot, :, :], ps_g[:, :].rearrange("p (t c) -> p t c", c=C),
                                               gate[:, 0:1], o.rows_in[:, slot, :, :], ALU.mult, ALU.add).then_inc(y_done, 1)

            def tile(pair, slot, last):
                r = 2 * pair + slot
                first = first_tile(r)
                for s in range(NE):
                    if s < 2 and not first:
                        add_expert(r - 1, E - 1 + s)
                    if s == 2:
                        if not first:
                            finish(pair + slot - 1, 1 - slot)
                        best_two(r)
                    if s == 4:
                        add_expert(r, 1)
                    if s >= 5:
                        add_expert(r, s - 2)
                    for m in range(M):
                        if s == 0 and m == 0 and not first:
                            hidden_lo(r - 1, 1 - slot, E, M - 1)
                        if s >= 2 and m == 0:
                            hidden_lo(r, slot, s - 1, M - 1)
                        if s >= 1 and m > 0:
                            hidden_lo(r, slot, s, m - 1)
                        if s == 2 and m == 1:
                            weigh_two(r)
                        if s == 4 and m == 2:
                            add_expert(r, 2)
                        if not last:
                            if s == 5 and m == 1:
                                row_stats(nc, dve, o, pair + slot, 1 - slot)
                            if s == 5 and m == 3:
                                join_rows(nc, dve, o, r + 1)
                            if s == 6 and m == 1:
                                normalise_rows(nc, dve, o, r + 1, 1 - slot)
                            if s == 8 and m == 0:
                                x_parts_lo(r + 1, 1 - slot)
                        if first and s == 1 and m == 2:
                            reciprocals(nc, dve, o, LAST_B)
                        if first and s == 3 and m == 1:
                            residual(nc, dve, o, LAST_B)
                        if first and m == 1 and s + 2 < NE:
                            weights_lo(s + 2)

            for e in range(E):
                a = nc.vector.memset(expert_no[:, e:e + 1], float(e))
            a.then_inc(small_set, 1)
            weights_lo(0)
            x_parts_lo(0, 0)
            nc.vector.tensor_tensor(select[:, :, :],
                                    o.ident[0:2 * E, 0:E].rearrange("k (e a) -> k e a", a=1).broadcast_to([2 * E, E, P]),
                                    o.ident[0:2 * E, E:2 * E].rearrange("k (e a) -> k e a", a=1).broadcast_to([2 * E, E, P]),
                                    ALU.add).then_inc(select_set, 1)
            weights_lo(1)
            dve.wait_ge(w_in, N_W * DMA)
            dve.wait_ge(gate_set, 1)
            tile(0, 0, False)
            tile(0, 1, False)
            with dve.Fori(1, NT // 2 - 1) as i:
                for slot in range(2):
                    tile(i, slot, False)
            tile(NT // 2 - 1, 0, False)
            tile(NT // 2 - 1, 1, True)
            add_expert(NT - 1, E - 1)
            hidden_lo(NT - 1, 1, E, M - 1)
            add_expert(NT - 1, E)
            finish(NT // 2 - 1, 1)

        @block.gpsimd
        def _(pool):
            def weights_hi(e):
                pool.wait_ge(w_loaded[e], 2 * DMA)
                k = (e - 1) % STAGED
                nc.gpsimd.tensor_copy(up_hi[:, e, :], up_w[:, k, :])
                nc.gpsimd.tensor_copy(down_hi[:, e - 1, :, :], down_w[:, k, :, :]).then_inc(w_hi_pool, 1)

            weights_hi(3)
            normalise(nc, pool, o, LAST_B)
            for e in range(4, NE):
                weights_hi(e)
            with pool.Fori(1, NT) as r:
                rstd_of_rows(nc, pool, o, r)


def build(nc, a, out):
    B, _, _ = a["x"].shape
    TC = a["ctx_t"].shape[2]
    scratch = {
        "q": nc.dram_tensor("q_rows", [B, 2, H, 2, 2, D, T], F32, kind="Internal").ap(),
        "kself": nc.dram_tensor("kself_rows", [B, H, 2, 2, D, T], F32, kind="Internal").ap(),
        "kx": nc.dram_tensor("kx_rows", [B, H, 2, 2, D, TC], F32, kind="Internal").ap(),
        "y": nc.dram_tensor("y_rows", [B, 2, H, VW, T], F32, kind="Internal").ap(),
    }
    x1 = nc.dram_tensor("x1", [B, T, C], F32, kind="Internal").ap()
    att = {n: a[n] for n in ("Wq", "Wk", "Wv", "Wcq", "Wp", "Wck", "Wcv", "qk_bias", "bcv", "bv", "bp", "rw1")}
    ffn = {n: a[n] for n in ("rw2", "rb2", "w1", "w2", "b2", "up_b")}
    with ExitStack() as ctx:
        o = Shared(nc, ctx, a["rw1"].shape[1], TILE_ROWS)
        attention(nc, a["x"], a["ctx_t"], a["g_xattn"], att, x1, scratch, o)
        experts(nc, a["x"], x1, scratch["y"], a["g_ffn"], ffn, out.rearrange("b t c -> (b t) c"), o)


def kernel(**inputs):
    import numpy as np
    import concourse.bacc as bacc
    from concourse import mybir as _mybir
    from concourse.bass_utils import run_bass_kernel_spmd

    i = {n.replace("L0_xattn_", "").replace("L0_ffn_", ""): np.asarray(v) for n, v in inputs.items()}
    ctx = i.pop("ctx_512")
    i["ctx_t"] = np.concatenate([ctx.transpose(0, 2, 1), np.ones((ctx.shape[0], 1, ctx.shape[1]), ctx.dtype)], 1)
    i["Wck"] = np.concatenate([i["Wck"], i.pop("bck")[None, :]], 0)
    i["qk_bias"] = np.stack([i.pop("bq"), i.pop("bk"), i.pop("bcq")], 1)
    up_b = np.concatenate([i.pop("rb1")[None], i.pop("b1")], 0)
    i["up_b"] = up_b.reshape(up_b.shape[0], -1, P).transpose(2, 0, 1)

    nc = bacc.Bacc("TRN2", target_bir_lowering=False, num_devices=1)
    arrays, aps = {}, {}
    for n, v in i.items():
        v = np.ascontiguousarray(v)
        arrays[f"in_{n}"] = v
        aps[n] = nc.dram_tensor(f"in_{n}", v.shape, _mybir.dt.from_np(v.dtype), kind="ExternalInput").ap()
    out = nc.dram_tensor("out", i["x"].shape, _mybir.dt.from_np(i["x"].dtype), kind="ExternalOutput").ap()
    build(nc, aps, out)
    r = run_bass_kernel_spmd(nc, [arrays], core_ids=[0])
    return r.results[0]["out"]
```
